# Optimizing a Trainium2 kernel written in Bass

```python
import numpy as np
import jax
import jax.numpy as jnp

def _softmax(x, axis=-1):
    return jax.nn.softmax(x, axis=axis)

def _gelu(x):
    return jax.nn.gelu(x, approximate=True)

def _silu(x):
    return jax.nn.silu(x)

def _sigmoid(x):
    return jax.nn.sigmoid(x)

def _layernorm(x, axis=-1, eps=1e-05):
    m = jnp.mean(x, axis=axis, keepdims=True)
    v = jnp.var(x, axis=axis, keepdims=True)
    return (x - m) / jnp.sqrt(v + eps)

def _scatter_add(tgt, idx, src, axis=0):
    return tgt.at[idx].add(src)

def _segment_sum(src, seg, n):
    return jax.ops.segment_sum(src, seg, n)
kernel_name = 'mk_xattn_ffn_d2_seqx_r4_12bc38'

def setup_inputs(seed: int=0):
    np.random.seed(seed)
    _w = jnp.asarray

    def _rec_inputs():
        import jax
        import jax.numpy as jnp
        _rk = jax.random.key(seed)
        x = -0.0003929 + 0.9999 * jax.random.normal(jax.random.fold_in(_rk, 1), (8, 112, 256), jnp.float32)
        _lenS = 112 - jax.random.randint(jax.random.fold_in(_rk, 7), (8,), 0, max(1, 112 // 4) + 1, jnp.int32)
        _lenS2 = 375 - jax.random.randint(jax.random.fold_in(_rk, 8), (8,), 0, max(1, 375 // 4) + 1, jnp.int32)
        _ctx_1024P = jax.random.normal(jax.random.fold_in(_rk, 11), (8, 16, 256), jnp.float32)
        _ctx_1024c = jax.random.dirichlet(jax.random.fold_in(_rk, 511), 0.3 * jnp.ones((16,), jnp.float32), (8, 375))
        _ctx_1024t = jnp.einsum('bsk,bkd->bsd', _ctx_1024c, _ctx_1024P)
        _ctx_1024t = _ctx_1024t * jax.lax.rsqrt(jnp.mean(jnp.square(_ctx_1024t)) + 1e-12) * 0.953939
        ctx_1024 = 2.81802e-05 + 1.00001 * (_ctx_1024t + 0.3 * jax.random.normal(jax.random.fold_in(_rk, 611), (8, 375, 256), jnp.float32))
        return (x, ctx_1024, _lenS2)
    x, ctx_1024, _lenS2 = _rec_inputs()

    def _L0_xattn_setup():
        import jax, jax.numpy as jnp
        import numpy as np
        NEG = -10000000000000.0
        key = jax.random.key(seed)
        ks = jax.random.split(key, 7)
        B, L, D, E = (8, 512, 256, 256)
        Q = jax.random.normal(ks[0], (B, L, D), dtype=jnp.float32)
        K = jax.random.normal(ks[1], (B, L, D), dtype=jnp.float32)
        V = jax.random.normal(ks[2], (B, L, D), dtype=jnp.float32)
        query_pad_idxs = jax.random.randint(ks[3], (B,), 0, L)
        key_pad_idxs = jax.random.randint(ks[4], (B,), 0, L)
        W = jax.random.normal(ks[5], (E, D), dtype=jnp.float32) / np.sqrt(D)
        b = jax.random.normal(ks[6], (E,), dtype=jnp.float32) * 0.01
        return {'Q': Q, 'K': K, 'V': V, 'query_pad_idxs': query_pad_idxs, 'key_pad_idxs': key_pad_idxs, 'W': W, 'b': b}
    _L0_xattn_all = _L0_xattn_setup()
    _L0_xattn_in = {k: v for k, v in _L0_xattn_all.items() if k in ('W', 'b')}
    del _L0_xattn_all

    def _L0_ffn_setup():
        import jax, jax.numpy as jnp
        import numpy as np
        B, S, D = (4, 512, 256)
        E, F = (8, 1024)
        key = jax.random.key(seed)
        ks = jax.random.split(key, 5)
        x = jax.random.normal(ks[0], (B, S, D), dtype=jnp.float32)
        switch_w = jax.random.normal(ks[1], (D, E), dtype=jnp.float32) * D ** (-0.5)
        switch_b = jnp.zeros((E,), dtype=jnp.float32)
        w1 = jax.random.normal(ks[2], (E, D, F), dtype=jnp.float32) * D ** (-0.5)
        b1 = jnp.zeros((E, F), dtype=jnp.float32)
        w2 = jax.random.normal(ks[3], (E, F, D), dtype=jnp.float32) * F ** (-0.5)
        b2 = jnp.zeros((E, D), dtype=jnp.float32)
        return {'x': x, 'switch_w': switch_w, 'switch_b': switch_b, 'w1': w1, 'b1': b1, 'w2': w2, 'b2': b2}
    _L0_ffn_all = _L0_ffn_setup()
    _L0_ffn_in = {k: v for k, v in _L0_ffn_all.items() if k in ('switch_w', 'switch_b', 'w1', 'b1', 'w2', 'b2')}
    del _L0_ffn_all

    def _L1_xattn_setup():
        import jax, jax.numpy as jnp
        import numpy as np
        D_MODEL = 256
        NUM_HEADS = 16
        DEPTH = D_MODEL // NUM_HEADS
        key = jax.random.key(seed)
        ks = jax.random.split(key, 10)
        B, T, C = (2, 512, 768)
        s = 1.0 / np.sqrt(D_MODEL)
        inp = {'x': jax.random.normal(ks[0], (B, T, D_MODEL), dtype=jnp.float32), 'context': jax.random.normal(ks[1], (B, C, D_MODEL), dtype=jnp.float32), 'Wq': jax.random.normal(ks[2], (D_MODEL, D_MODEL), dtype=jnp.float32) * s, 'bq': jnp.zeros((D_MODEL,), dtype=jnp.float32), 'Wk': jax.random.normal(ks[3], (D_MODEL, D_MODEL), dtype=jnp.float32) * s, 'bk': jnp.zeros((D_MODEL,), dtype=jnp.float32), 'Wv': jax.random.normal(ks[4], (D_MODEL, D_MODEL), dtype=jnp.float32) * s, 'bv': jnp.zeros((D_MODEL,), dtype=jnp.float32), 'Wo': jax.random.normal(ks[5], (D_MODEL, D_MODEL), dtype=jnp.float32) * s, 'bo': jnp.zeros((D_MODEL,), dtype=jnp.float32)}
        return inp
    _L1_xattn_all = _L1_xattn_setup()
    _L1_xattn_in = {k: v for k, v in _L1_xattn_all.items() if k in ('Wq', 'bq', 'Wk', 'bk', 'Wv', 'bv', 'Wo', 'bo')}
    del _L1_xattn_all

    def _L1_ffn_setup():
        import jax, jax.numpy as jnp
        import numpy as np
        D_MODEL = 256
        FF = 1024
        E = 8
        TOP_K = 2
        CAP_FACTOR = 1.25
        B, T = (4, 512)

        def _moe_forward(x, gate_w, gate_b, w1, b1, w2, b2):
            Bb, Tt, d = x.shape
            S = Bb * Tt
            C = int(CAP_FACTOR * S / E)
            xf = x.reshape(S, d)
            logits = xf @ gate_w + gate_b
            probs = jax.nn.softmax(logits, axis=1)
            topk_p, topk_i = jax.lax.top_k(probs, TOP_K)
            topk_pn = topk_p / jnp.sum(topk_p, axis=1, keepdims=True)
            rows = jnp.arange(S)
            w_te = jnp.zeros((S, E), xf.dtype).at[rows[:, None], topk_i].set(topk_pn)
            mask = jnp.zeros((S, E), bool).at[rows[:, None], topk_i].set(True)
            rank = jnp.cumsum(mask.astype(jnp.int32), axis=0)
            slot = jnp.where(mask & (rank <= C), rank - 1, C)
            e_grid = jnp.broadcast_to(jnp.arange(E), (S, E))
            t_grid = jnp.broadcast_to(rows[:, None], (S, E))
            buf = jnp.full((E, C + 1), S, jnp.int32).at[e_grid, slot].set(t_grid)
            idx = buf[:, :C]
            valid = idx < S
            x_pad = jnp.concatenate([xf, jnp.zeros((1, d), xf.dtype)], axis=0)
            xin = x_pad[idx]
            h = jax.nn.relu(jnp.einsum('ecd,edh->ech', xin, w1) + b1[:, None, :])
            out = jnp.einsum('ech,ehd->ecd', h, w2) + b2[:, None, :]
            w_pad = jnp.concatenate([w_te, jnp.zeros((1, E), xf.dtype)], axis=0)
            tok_w = w_pad[idx, jnp.arange(E)[:, None]]
            out = out * jnp.where(valid, tok_w, 0.0)[:, :, None]
            final = jnp.zeros((S + 1, d), xf.dtype).at[idx.reshape(-1)].add(out.reshape(-1, d))[:S]
            return final.reshape(Bb, Tt, d)
        key = jax.random.key(seed)
        ks = jax.random.split(key, 7)
        s = 0.02
        return {'x': jax.random.normal(ks[0], (B, T, D_MODEL), jnp.float32), 'gate_w': jax.random.normal(ks[1], (D_MODEL, E), jnp.float32) * s, 'gate_b': jnp.zeros((E,), jnp.float32), 'w1': jax.random.normal(ks[2], (E, D_MODEL, FF), jnp.float32) * s, 'b1': jnp.zeros((E, FF), jnp.float32), 'w2': jax.random.normal(ks[3], (E, FF, D_MODEL), jnp.float32) * s, 'b2': jnp.zeros((E, D_MODEL), jnp.float32)}
    _L1_ffn_all = _L1_ffn_setup()
    _L1_ffn_in = {k: v for k, v in _L1_ffn_all.items() if k in ('gate_w', 'gate_b', 'w1', 'b1', 'w2', 'b2')}
    del _L1_ffn_all
    return {'x': x, 'ctx_1024': ctx_1024, '_lenS2': _lenS2, 'L0_xattn_W': _L0_xattn_in['W'], 'L0_xattn_b': _L0_xattn_in['b'], 'L0_ffn_switch_w': _L0_ffn_in['switch_w'], 'L0_ffn_switch_b': _L0_ffn_in['switch_b'], 'L0_ffn_w1': _L0_ffn_in['w1'], 'L0_ffn_b1': _L0_ffn_in['b1'], 'L0_ffn_w2': _L0_ffn_in['w2'], 'L0_ffn_b2': _L0_ffn_in['b2'], 'L1_xattn_Wq': _L1_xattn_in['Wq'], 'L1_xattn_bq': _L1_xattn_in['bq'], 'L1_xattn_Wk': _L1_xattn_in['Wk'], 'L1_xattn_bk': _L1_xattn_in['bk'], 'L1_xattn_Wv': _L1_xattn_in['Wv'], 'L1_xattn_bv': _L1_xattn_in['bv'], 'L1_xattn_Wo': _L1_xattn_in['Wo'], 'L1_xattn_bo': _L1_xattn_in['bo'], 'L1_ffn_gate_w': _L1_ffn_in['gate_w'], 'L1_ffn_gate_b': _L1_ffn_in['gate_b'], 'L1_ffn_w1': _L1_ffn_in['w1'], 'L1_ffn_b1': _L1_ffn_in['b1'], 'L1_ffn_w2': _L1_ffn_in['w2'], 'L1_ffn_b2': _L1_ffn_in['b2']}

def reference(x, ctx_1024, _lenS2, L0_xattn_W, L0_xattn_b, L0_ffn_switch_w, L0_ffn_switch_b, L0_ffn_w1, L0_ffn_b1, L0_ffn_w2, L0_ffn_b2, L1_xattn_Wq, L1_xattn_bq, L1_xattn_Wk, L1_xattn_bk, L1_xattn_Wv, L1_xattn_bv, L1_xattn_Wo, L1_xattn_bo, L1_ffn_gate_w, L1_ffn_gate_b, L1_ffn_w1, L1_ffn_b1, L1_ffn_w2, L1_ffn_b2):
    import jax
    import jax.numpy as jnp

    def _L0_xattn_ref(Q, K, V, query_pad_idxs, key_pad_idxs, W, b):
        import jax, jax.numpy as jnp
        import numpy as np
        NEG = -10000000000000.0
        B, Lq, D = Q.shape
        Lk = K.shape[1]
        scale = 1.0 / jnp.sqrt(jnp.asarray(D, dtype=Q.dtype))
        scores = jnp.einsum('bqd,bkd->bqk', Q, K) * scale
        qpos = jnp.arange(Lq)[None, :, None]
        kpos = jnp.arange(Lk)[None, None, :]
        mask = (qpos >= query_pad_idxs[:, None, None]) & (kpos >= key_pad_idxs[:, None, None])
        scores = jnp.where(mask, jnp.asarray(NEG, scores.dtype), scores)
        attn = jax.nn.softmax(scores, axis=2)
        out = jnp.einsum('bqk,bkd->bqd', attn, V)
        return out @ W.T + b

    def _L0_ffn_ref(x, switch_w, switch_b, w1, b1, w2, b2):
        import jax, jax.numpy as jnp
        import numpy as np
        B, S, D = (4, 512, 256)
        E, F = (8, 1024)
        b, s, d = x.shape
        t = x.reshape(-1, d)
        logits = t @ switch_w + switch_b
        route_prob = jax.nn.softmax(logits, axis=-1)
        route_prob_max = jnp.max(route_prob, axis=-1)
        routes = jnp.argmax(route_prob, axis=-1)
        out = jnp.zeros_like(t)
        n_experts = w1.shape[0]
        for e in range(n_experts):
            h = jax.nn.gelu(t @ w1[e] + b1[e])
            y = h @ w2[e] + b2[e]
            mask = (routes == e)[:, None]
            out = jnp.where(mask, y, out)
        out = out * route_prob_max[:, None]
        return out.reshape(b, s, d)

    def _L1_xattn_ref(x, context, Wq, bq, Wk, bk, Wv, bv, Wo, bo):
        import jax, jax.numpy as jnp
        import numpy as np
        D_MODEL = 256
        NUM_HEADS = 16
        DEPTH = D_MODEL // NUM_HEADS
        B, T, D = x.shape
        C = context.shape[1]
        H, d = (NUM_HEADS, DEPTH)
        q = x @ Wq.T + bq
        k = context @ Wk.T + bk
        v = context @ Wv.T + bv
        q = q.reshape(B, T, H, d).transpose(0, 2, 1, 3)
        k = k.reshape(B, C, H, d).transpose(0, 2, 1, 3)
        v = v.reshape(B, C, H, d).transpose(0, 2, 1, 3)
        scores = jnp.einsum('bhtd,bhcd->bhtc', q, k) / jnp.sqrt(jnp.asarray(d, x.dtype))
        attn = jax.nn.softmax(scores, axis=-1)
        out = jnp.einsum('bhtc,bhcd->bhtd', attn, v)
        out = out.transpose(0, 2, 1, 3).reshape(B, T, D)
        return out @ Wo.T + bo

    def _L1_ffn_ref(x, gate_w, gate_b, w1, b1, w2, b2):
        import jax, jax.numpy as jnp
        import numpy as np
        D_MODEL = 256
        FF = 1024
        E = 8
        TOP_K = 2
        CAP_FACTOR = 1.25
        B, T = (4, 512)

        def _moe_forward(x, gate_w, gate_b, w1, b1, w2, b2):
            Bb, Tt, d = x.shape
            S = Bb * Tt
            C = int(CAP_FACTOR * S / E)
            xf = x.reshape(S, d)
            logits = xf @ gate_w + gate_b
            probs = jax.nn.softmax(logits, axis=1)
            topk_p, topk_i = jax.lax.top_k(probs, TOP_K)
            topk_pn = topk_p / jnp.sum(topk_p, axis=1, keepdims=True)
            rows = jnp.arange(S)
            w_te = jnp.zeros((S, E), xf.dtype).at[rows[:, None], topk_i].set(topk_pn)
            mask = jnp.zeros((S, E), bool).at[rows[:, None], topk_i].set(True)
            rank = jnp.cumsum(mask.astype(jnp.int32), axis=0)
            slot = jnp.where(mask & (rank <= C), rank - 1, C)
            e_grid = jnp.broadcast_to(jnp.arange(E), (S, E))
            t_grid = jnp.broadcast_to(rows[:, None], (S, E))
            buf = jnp.full((E, C + 1), S, jnp.int32).at[e_grid, slot].set(t_grid)
            idx = buf[:, :C]
            valid = idx < S
            x_pad = jnp.concatenate([xf, jnp.zeros((1, d), xf.dtype)], axis=0)
            xin = x_pad[idx]
            h = jax.nn.relu(jnp.einsum('ecd,edh->ech', xin, w1) + b1[:, None, :])
            out = jnp.einsum('ech,ehd->ecd', h, w2) + b2[:, None, :]
            w_pad = jnp.concatenate([w_te, jnp.zeros((1, E), xf.dtype)], axis=0)
            tok_w = w_pad[idx, jnp.arange(E)[:, None]]
            out = out * jnp.where(valid, tok_w, 0.0)[:, :, None]
            final = jnp.zeros((S + 1, d), xf.dtype).at[idx.reshape(-1)].add(out.reshape(-1, d))[:S]
            return final.reshape(Bb, Tt, d)
        return _moe_forward(x, gate_w, gate_b, w1, b1, w2, b2)
    x = x + _L0_xattn_ref(_layernorm(x, axis=-1), ctx_1024, ctx_1024, _lenS2, _lenS2, L0_xattn_W, L0_xattn_b)
    x = x + _L0_ffn_ref(_layernorm(x, axis=-1), L0_ffn_switch_w, L0_ffn_switch_b, L0_ffn_w1, L0_ffn_b1, L0_ffn_w2, L0_ffn_b2)
    x = x + _L1_xattn_ref(_layernorm(x, axis=-1), ctx_1024, L1_xattn_Wq, L1_xattn_bq, L1_xattn_Wk, L1_xattn_bk, L1_xattn_Wv, L1_xattn_bv, L1_xattn_Wo, L1_xattn_bo)
    x = x + _L1_ffn_ref(_layernorm(x, axis=-1), L1_ffn_gate_w, L1_ffn_gate_b, L1_ffn_w1, L1_ffn_b1, L1_ffn_w2, L1_ffn_b2)
    return x

_drawn_inputs = setup_inputs


def setup_inputs(seed=0):
    import zlib

    import numpy as np

    out = dict(_drawn_inputs(seed))
    spreads = {'L0_ffn_switch_b': (0.0, 0.1),
     'L0_ffn_b1': (0.0, 0.32),
     'L0_ffn_b2': (0.0, 0.1),
     'L1_xattn_bq': (0.0, 0.367),
     'L1_xattn_bk': (0.0, 0.8),
     'L1_xattn_bv': (0.0, 0.1),
     'L1_xattn_bo': (0.0, 0.1),
     'L1_ffn_gate_b': (0.0, 0.1),
     'L1_ffn_b1': (0.0, 0.433),
     'L1_ffn_b2': (0.0, 0.1)}
    factors = {'L0_xattn_b': 2.959}
    for name, (base, spread) in spreads.items():
        noise = np.random.default_rng([zlib.crc32(name.encode()), seed]).standard_normal(out[name].shape)
        drawn = base * np.exp(spread * noise) if base else spread * noise
        out[name] = jnp.asarray(drawn.astype(out[name].dtype))
    for name, factor in factors.items():
        out[name] = (out[name] * factor).astype(out[name].dtype)
    return out
```

```python
import concourse.bass as bass
from concourse import mybir
from contextlib import ExitStack


def build_program(nc, A, out):
    f32 = mybir.dt.float32
    bf16 = mybir.dt.bfloat16
    i32 = mybir.dt.int32
    u32 = mybir.dt.uint32
    ALU = mybir.AluOpType
    ACT = mybir.ActivationFunctionType
    AX = mybir.AxisListType

    B, T, D = A["x"].shape
    KL = A["ctx_1024"].shape[1]
    NE = A["L0_ffn_w1"].shape[0]
    FF = A["L0_ffn_w1"].shape[2]
    P = 128
    DC = D // P
    FC = FF // P
    KT = 3
    KP = KL // KT
    NH, HD = 16, D // 16
    HPC = P // HD
    HW = 32
    CAP = int(1.25 * B * T / NE)
    HC = CAP // 2
    N_OVER = 6
    NSLOT0 = NE + N_OVER
    ROWS0 = NSLOT0 * CAP
    ROWS1 = NE * CAP
    BIG = -16.0e13
    EPS = 1e-5
    LATE = (4, 6, 8)

    x_rows = A["x"].rearrange("b t d -> t b d")
    out_rows = out.rearrange("b t d -> t b d")
    ctx_rows = A["ctx_1024"].rearrange("b (j p) d -> p b j d", p=KP)

    tok_rows = [nc.dram_tensor("slot_tokens_0", (ROWS0, D), f32).ap(),
                nc.dram_tensor("slot_tokens_1", (ROWS1 + 2 * B * T, D), f32).ap()]
    res_rows = [nc.dram_tensor("slot_results_0", (ROWS0, D), f32).ap(),
                nc.dram_tensor("slot_results_1", (ROWS1, D), f32).ap()]

    stack = ExitStack()
    with stack:
        def sb(name, shape, dt=f32):
            return stack.enter_context(nc.sbuf_tensor(name, list(shape), dt))

        def sem(name):
            return stack.enter_context(nc.semaphore(name))

        bank = [stack.enter_context(nc.psum_tensor(f"bank{i}", [P, 512], f32)) for i in range(8)]

        ident = sb("ident", [P, P])
        tri = sb("tri", [T, T], bf16)
        ones = sb("ones", [T, T], bf16)
        kpos = sb("kpos", [T, KL])
        kpos_i = sb("kpos_i", [T, KL], i32)
        qpos = sb("qpos", [T, 1])
        qpos_i = sb("qpos_i", [T, 1], i32)
        eidx = sb("eidx", [T, NE])
        eidx_i = sb("eidx_i", [T, NE], i32)
        headmask = sb("headmask", [P, HPC])
        tokid = sb("tokid", [T, B])
        tokid_i = sb("tokid_i", [T, B], i32)
        neg_half = sb("neg_half", [T, B])
        zeros = sb("zeros", [P, 2 * D])
        shared = sb("raw_weights_then_results", [P, 2 * B * D])
        raw = shared[:, 0:5 * DC * D].rearrange("p (n c d) -> p n c d", n=5, c=DC)
        wT = sb("weights_T", [P, 5, DC, D])
        bias_rows = sb("bias_rows", [P, P])
        bias_rows2 = sb("bias_rows2", [4 * NE + 4, P])
        biasT = sb("biasT", [P, P + 4 * NE + 4])
        b_attn = sb("b_attn", [T, 2, D])
        bv = sb("bv", [KP, D])
        gate_w = sb("gate_w", [P, 2, DC, NE])
        gate_b = sb("gate_b", [T, 2, NE])
        lens_i = sb("lens_i", [T, B], i32)
        lens = sb("lens", [T, B])
        qflag = sb("qflag", [T, B])
        x = sb("x_tokens", [T, B, D])
        xn = sb("xn_tokens", [T, B, D])
        ctx = [sb(f"ctx{u}", [KP, KT, D]) for u in range(2)]
        ctxT = [sb(f"ctxT{u}", [P, DC, KL]) for u in range(2)]
        xa = [sb(f"xa{u}", [T, D]) for u in range(2)]
        rowmax = sb("rowmax", [T, 1])
        esinv = sb("esinv", [T, 1])
        xT = [sb(f"xT{u}", [P, DC, T]) for u in range(2)]
        kT = sb("kT", [P, DC, B * KL])
        vals = sb("vals", [KP, B * KT, D])
        vpad = [sb(f"vpad{u}", [KP, KT, NH, HW]) for u in range(2)]
        scores = sb("scores", [T, KL])
        kmask = sb("kmask", [T, KL])
        probs = [sb(f"probs{i}", [T, KL]) for i in range(4)]
        probsT = [sb(f"probsT{i}", [KP, KT * T]) for i in range(4)]
        oT = sb("oT", [P, DC, T])
        outT = sb("outT", [P, 4, T])
        qT = sb("qT", [P, DC, B, T])
        qmask = [sb(f"qmask{u}", [P, DC, HPC, T]) for u in range(2)]
        nmax = [sb(f"nmax{u}", [T, NH]) for u in range(2)]
        rinv = sb("rinv", [T, NH])
        esum = sb("esum", [T, B])
        lstat = sb("lstat", [T, B, 6])
        lmv = sb("lmv", [T, B, 2])
        lvar = sb("lvar", [T, B])
        rstd = sb("rstd", [T, B])
        w1 = [sb(f"w1_{u}", [P, DC, FF]) for u in range(2)]
        w2 = [sb(f"w2_{u}", [P, FC, D]) for u in range(2)]
        xtok = [sb(f"xtok{u}", [HC, 2, D]) for u in range(2)]
        xsT = [sb(f"xsT{u}", [P, DC, CAP]) for u in range(2)]
        spare = [qmask[u][:].rearrange("p c j t -> p (c j t)") for u in range(2)]
        hT = spare[0][:, 0:FC * CAP].rearrange("p (f t) -> p f t", f=FC)
        yT = spare[0][:, FC * CAP:(FC + DC) * CAP].rearrange("p (d t) -> p d t", d=DC)
        ytok = [spare[1][0:HC, u * 2 * D:(u + 1) * 2 * D].rearrange("p (g d) -> p g d", g=2) for u in range(2)]
        logit = sb("logit", [T, B, NE])
        top8 = sb("top8", [T, B, 8])
        topi = sb("topi", [T, B, 8], u32)
        topf = sb("topf", [T, B, 2])
        hot = sb("hot", [T, 2, B, NE])
        hot16 = sb("hot16", [T, (B + 1) * NE], bf16)
        rank = sb("rank", [T, (B + 1) * NE])
        rt = sb("route_tmp", [T, B, NE])
        rsel = sb("route_sel", [T, 2, B])
        ra = sb("route_a", [T, B])
        rb = sb("route_b", [T, B])
        rc = sb("route_c", [T, B])
        wsel = sb("route_weight", [T, 2, B])
        pos_put = sb("pos_put", [T, 2, B], i32)
        pos_get = sb("pos_get", [T, 2, B], i32)
        ocum = sb("over_cum", [T, 3, NE])
        oid = sb("over_id", [T, 8])
        oid_i = sb("over_id_i", [T, 8], i32)
        got = shared[0:T].rearrange("p (c b d) -> p c b d", c=2, b=B)

        S = {n: sem(n) for n in (
            "consts_made", "consts_step", "weights_in", "biases_in", "bcast_in", "x_in", "zeroed",
            "bias_ps", "bias_sb", "w_ps", "w_sb", "chain",
            "ctx_in0", "ctx_in1", "ctxT_ps", "ctxT_act", "ctxT_dve", "xT_ps", "xT_sb", "s_ps", "s_masked", "s_rowmax",
            "s_max", "s_exp", "kmask_set", "k_ps", "k_sb", "v_ps", "v_sb", "pT_ps", "pT_sb", "o_ps", "o_sb", "y_ps",
            "esum_inv", "xb", "x1", "qm", "vp", "h_s", "h_max", "h_exp", "h_pT", "h_pTa", "h_pTd", "h_av", "h_out",
            "h_outT", "h_rinv", "h_o", "e_oT", "e_oTs", "e_y", "x3", "q_xT", "q_xTs", "q_ps", "q_sb",
            "x2", "layer0_done", "x4a", "x4", "out_done")}
        LN = [{n: sem(f"ln{k}_{n}") for n in ("stats", "aggr", "var", "rstd", "xn")} for k in range(4)]
        R = [{n: sem(f"route{k}_{n}") for n in ("kept", "xT_ps", "xT_sb", "g_ps", "g_sb", "mask", "rank", "diff", "exp",
                                                "pos", "put", "regs")} for k in range(2)]
        G = [[sem(f"got{k}_{u}") for u in range(2)] for k in range(2)]
        F = [{n: sem(f"ffn{k}_{n}") for n in ("w1_in0", "w1_in1", "w2_in0", "w2_in1", "x_in0", "x_in1", "xT_ps", "xT_sb",
                                              "up", "h", "down", "yT", "y_ps", "y_sb", "y_out0", "y_out1")}
             for k in range(2)]

        block = stack.enter_context(nc.Block())

        def at(ap, i):
            if isinstance(i, int):
                return ap[:, i]
            sub = ap[:, bass.ds(i, 1)]
            names = " ".join("abc"[:len(sub.shape) - 2])
            return sub.rearrange(f"p i {names} -> p (i {names.split()[0]}) {' '.join(names.split()[1:])}")

        def pairs(eng):
            with eng.Fori(0, B // 2) as it:
                for u in range(2):
                    yield it * 2 + u, u, it

        names = ["L0_xattn_W", "L1_xattn_Wq", "L1_xattn_Wk", "L1_xattn_Wv", "L1_xattn_Wo"]
        W0, WQ, WK, WV, WO = range(5)
        w1_src = [A[f"L{k}_ffn_w1"].rearrange("e (c p) f -> p e c f", p=P) for k in range(2)]
        w2_src = [A[f"L{k}_ffn_w2"].rearrange("e (c p) d -> p e c d", p=P) for k in range(2)]
        tok_src = [tok_rows[k][0:(ROWS0, ROWS1)[k]].rearrange("(s p g) d -> p s g d", p=HC, g=2) for k in range(2)]
        res_dst = [res_rows[k].rearrange("(s p g) d -> p s g d", p=HC, g=2) for k in range(2)]

        @block.sync
        def _(sp):
            sp.dma_start(x[:], x_rows).then_inc(S["x_in"], 16)
            for n, name in enumerate(names):
                sp.dma_start(raw[:, n], A[name].rearrange("(c p) d -> p c d", p=P)).then_inc(S["weights_in"], 16)
            for k in range(2):
                sp.dma_start(bias_rows[64 * k:64 * k + 64, :],
                             A[f"L{k}_ffn_b1"].rearrange("e (f p) -> (e f) p", p=P)).then_inc(S["biases_in"], 16)
                sp.dma_start(bias_rows2[16 * k:16 * k + 16, :],
                             A[f"L{k}_ffn_b2"].rearrange("e (f p) -> (e f) p", p=P)).then_inc(S["biases_in"], 16)
            for n, name in enumerate(("L1_xattn_bq", "L1_xattn_bk")):
                sp.dma_start(bias_rows2[32 + 2 * n:34 + 2 * n, :],
                             A[name].rearrange("(f p) -> f p", p=P)).then_inc(S["biases_in"], 16)

            def load_ctx(b, u):
                sp.dma_start(ctx[u][:], ctx_rows[:, b]).then_inc(S[f"ctx_in{u}"], 16)

            def load_expert(k, e, u):
                sp.dma_start(w1[u][:], w1_src[k][:, e]).then_inc(F[k][f"w1_in{u}"], 16)
                sp.dma_start(w2[u][:], w2_src[k][:, e]).then_inc(F[k][f"w2_in{u}"], 16)

            load_ctx(0, 0)
            load_ctx(1, 1)
            for u in range(2):
                load_expert(0, u, u)
            sp.wait_ge(S["consts_made"], 1)
            for slots, count in ((tok_rows[0][0:ROWS0], NSLOT0), (tok_rows[1][0:ROWS1], NE), (res_rows[0][NE * CAP:], N_OVER)):
                flat = slots.rearrange("(s p g) d -> s p (g d)", p=HC, g=2)
                for r in range(count):
                    sp.dma_start(flat[r], zeros[0:HC, :]).then_inc(S["zeroed"], 16)
            with sp.Fori(1, B // 2) as it:
                for u in range(2):
                    sp.wait_ge(S["o_ps"], it * 2 + (u - 1))
                    load_ctx(it * 2 + u, u)

            def load_tokens(k, s, u):
                sp.dma_start(xtok[u][:], tok_src[k][:, s]).then_inc(F[k][f"x_in{u}"], 16)

            for k in range(2):
                sp.wait_ge(R[k]["put"], 16 * B * (1 + k))
                for u in range(2):
                    load_tokens(k, u, u)
                with sp.Fori(1, NE // 2) as it:
                    for u in range(2):
                        sp.wait_ge(F[k]["down"], it * 2 + (u - 1))
                        load_expert(k, it * 2 + u, u)
                        load_tokens(k, it * 2 + u, u)
                if k == 0:
                    sp.wait_ge(R[0]["regs"], 1)
                    n_over = sp.value_load(oid_i[0:1, 7:8], min_val=0, max_val=N_OVER)
                    for j in range(N_OVER):
                        u, s = j % 2, NE + j
                        e = sp.value_load(oid_i[0:1, j:j + 1], min_val=0, max_val=NE - 1)
                        with sp.If(n_over > j):
                            sp.wait_ge(F[0]["down"], s - 1)
                            sp.dma_start(w1[u][:], w1_src[0][:, bass.ds(e, 1)].rearrange("p e c f -> p (e c) f")).then_inc(F[0][f"w1_in{u}"], 16)
                            sp.dma_start(w2[u][:], w2_src[0][:, bass.ds(e, 1)].rearrange("p e c f -> p (e c) f")).then_inc(F[0][f"w2_in{u}"], 16)
                            load_tokens(0, s, u)
                    sp.wait_ge(S["layer0_done"], 1)
                    for u in range(2):
                        load_expert(1, u, u)
            with sp.Fori(0, B // 2) as it:
                sp.wait_ge(S["x4"], it * 2 + 2)
                sp.dma_start(out_rows[:, bass.ds(it * 2, 2)], x[:, bass.ds(it * 2, 2), :]).then_inc(S["out_done"], 16)
            sp.wait_ge(S["out_done"], 16 * (B // 2))

        @block.gpsimd
        def _(pool):
            n = [0]

            def step(ins):
                n[0] += 1
                ins.then_inc(S["consts_step"], 1)
                pool.wait_ge(S["consts_step"], n[0])

            pool.memset(zeros[:], 0.0).then_inc(S["consts_made"], 1)
            for k in range(2):
                pool.dma_start(b_attn[:, k, :], A[("L0_xattn_b", "L1_xattn_bo")[k]].partition_broadcast(T)).then_inc(S["bcast_in"], 16)
                pool.dma_start(gate_w[:, k], A[("L0_ffn_switch_w", "L1_ffn_gate_w")[k]].rearrange("(c p) e -> p c e", p=P)).then_inc(S["bcast_in"], 16)
                pool.dma_start(gate_b[:, k, :], A[("L0_ffn_switch_b", "L1_ffn_gate_b")[k]].partition_broadcast(T)).then_inc(S["bcast_in"], 16)
            pool.dma_start(bv[:], A["L1_xattn_bv"].partition_broadcast(KP)).then_inc(S["bcast_in"], 16)
            pool.dma_start(lens_i[:], A["_lenS2"].partition_broadcast(T)).then_inc(S["bcast_in"], 16)
            step(pool.memset(ident[:], 0.0))
            step(pool.affine_select(out=ident[:], in_=ident[:], compare_op=ALU.not_equal, fill=1.0, base=0,
                                    pattern=[[-1, P]], channel_multiplier=1))
            pool.memset(neg_half[:], -0.5)
            for u in range(2):
                pool.memset(vpad[u][:], 0.0)
            pool.memset(ones[:], 1.0)
            step(pool.memset(headmask[:], 1.0))
            step(pool.affine_select(out=headmask[:], in_=headmask[:], compare_op=ALU.is_ge, fill=0.0, base=0,
                                    pattern=[[-HD, HPC]], channel_multiplier=1))
            step(pool.affine_select(out=headmask[:], in_=headmask[:], compare_op=ALU.is_ge, fill=0.0, base=HD - 1,
                                    pattern=[[HD, HPC]], channel_multiplier=-1))
            step(pool.affine_select(out=tri[:], in_=ones[:], compare_op=ALU.is_ge, fill=0.0, base=0,
                                    pattern=[[1, T]], channel_multiplier=-1))
            for u in range(2):
                pool.memset(vpad[u][:, :, :, HD:HD + 1], 1.0)
            pool.iota(kpos_i[:], pattern=[[1, KL]], base=0, channel_multiplier=0)
            pool.iota(qpos_i[:], pattern=[[0, 1]], base=0, channel_multiplier=1)
            pool.iota(eidx_i[:], pattern=[[1, NE]], base=0, channel_multiplier=0)
            step(pool.iota(tokid_i[:], pattern=[[T, B]], base=0, channel_multiplier=1))
            for a, b in ((kpos, kpos_i), (qpos, qpos_i), (eidx, eidx_i)):
                pool.tensor_copy(a[:], b[:])
            pool.tensor_copy(tokid[:], tokid_i[:]).then_inc(S["consts_made"], 1)

            def rsqrt(k):
                pool.wait_ge(LN[k]["var"], 1)
                pool.tensor_tensor(rstd[:], lvar[:], neg_half[:], ALU.pow).then_inc(LN[k]["rstd"], 1)

            def scatter(k):
                pool.wait_ge(S["zeroed"], 16 * (NSLOT0 + NE + N_OVER))
                pool.wait_ge(R[k]["pos"], 1)
                for c in range(k + 1):
                    for b in range(B):
                        pool.indirect_dma_start(
                            out=tok_rows[k], out_offset=bass.IndirectOffsetOnAxis(ap=pos_put[:, c, b:b + 1].bitcast(u32), axis=0),
                            in_=xn[:, b, :], in_offset=None).then_inc(R[k]["put"], 16)

            def gather(k):
                for c in range(k + 1):
                    for b in range(B):
                        pool.indirect_dma_start(
                            out=got[:, c, b, :], out_offset=None, in_=res_rows[k],
                            in_offset=bass.IndirectOffsetOnAxis(ap=pos_get[:, c, b:b + 1].bitcast(u32), axis=0),
                        ).then_inc(G[k][c], 16)

            def store_results(k, s, u):
                pool.wait_ge(F[k]["y_sb"], s + 1)
                pool.dma_start(at(res_dst[k], s), ytok[u]).then_inc(F[k][f"y_out{u}"], 16)

            rsqrt(0)
            rsqrt(1)
            scatter(0)
            for s, u, it in pairs(pool):
                store_results(0, s, u)
            pool.wait_ge(R[0]["regs"], 1)
            n_over = pool.value_load(oid_i[0:1, 7:8], min_val=0, max_val=N_OVER)
            for u in range(2):
                pool.wait_ge(F[0][f"y_out{u}"], 16 * (NE // 2))
            for j in range(N_OVER):
                with pool.If(n_over > j):
                    store_results(0, NE + j, j % 2)
                    pool.wait_ge(F[0][f"y_out{j % 2}"], 16 * ((NE + j) // 2 + 1))
            gather(0)
            rsqrt(2)
            pool.wait_ge(S["v_sb"], 2 * B)

            def head_operands(b, u):
                pool.tensor_copy(vpad[u][:, :, :, 0:HD],
                                 vals[:, bass.ds(b * KT, KT), :].rearrange("p j (h d) -> p j h d", d=HD)).then_inc(S["vp"], 1)
                pool.wait_ge(S["q_sb"], DC * B)
                for c in range(DC):
                    pool.tensor_tensor(qmask[u][:, c], at(qT[:, c], b).unsqueeze(1).to_broadcast([P, HPC, T]),
                                       headmask[:].unsqueeze(2).to_broadcast([P, HPC, T]), ALU.mult).then_inc(S["qm"], 1)

            for u in range(2):
                head_operands(u, u)
            with pool.Fori(1, B // 2) as it:
                for u in range(2):
                    pool.wait_ge(S["h_out"], it * 2 + (u - 1))
                    head_operands(it * 2 + u, u)
            rsqrt(3)
            scatter(1)
            for s, u, it in pairs(pool):
                store_results(1, s, u)
            for u in range(2):
                pool.wait_ge(F[1][f"y_out{u}"], 16 * (NE // 2))
            gather(1)

        @block.tensor
        def _(pe):
            mm, tr = nc.tensor.matmul, nc.tensor.transpose
            pe.wait_ge(S["consts_made"], 2)
            pe.wait_ge(S["weights_in"], 16 * 5)
            for n in range(5):
                if n >= 2:
                    pe.wait_ge(S["w_sb"], n - 1)
                for c in range(DC):
                    for o in range(DC):
                        last = tr(bank[n % 2][:, c * D + o * P:c * D + (o + 1) * P], raw[:, n, o, c * P:(c + 1) * P], ident[:])
                last.then_inc(S["w_ps"], 1)
            pe.wait_ge(S["biases_in"], 16 * 6)
            tr(bank[2][:, 0:P], bias_rows[:], ident[:])
            tr(bank[2][:, P:P + 36], bias_rows2[:], ident[0:36, 0:36]).then_inc(S["bias_ps"], 1)
            pe.wait_ge(S["w_sb"], 5)
            pe.wait_ge(S["bias_sb"], 1)

            for b, u, it in pairs(pe):
                pe.wait_ge(S[f"ctx_in{u}"], 16 * (it + 1))
                for c in range(DC):
                    for j in range(KT):
                        last = tr(bank[c][:, j * KP:(j + 1) * KP], ctx[u][:, j, c * P:(c + 1) * P], ident[0:KP, 0:KP])
                last.then_inc(S["ctxT_ps"], 1)
                pe.wait_ge(LN[0]["xn"], b + 1)
                for c in range(DC):
                    last = tr(bank[2][:, c * T:(c + 1) * T], xa[u][:, c * P:(c + 1) * P], ident[0:T, 0:T])
                last.then_inc(S["xT_ps"], 1)
                pe.wait_ge(S["ctxT_act"], b + 1)
                pe.wait_ge(S["ctxT_dve"], b + 1)
                pe.wait_ge(S["xT_sb"], b + 1)
                for c in range(DC):
                    last = mm(bank[3][0:T, 0:KL], xT[u][:, c, :], ctxT[u][:, c, :], start=(c == 0), stop=(c == 1))
                last.then_inc(S["s_ps"], 1)
                for o in range(DC):
                    for c in range(DC):
                        last = mm(bank[4 + o][:, 0:KL], wT[:, WK, c, o * P:(o + 1) * P], ctxT[u][:, c, :],
                                  start=(c == 0), stop=(c == 1))
                    last.then_inc(S["k_ps"], 1)
                pe.wait_ge(S["s_exp"], b + 1)
                for j in range(KT):
                    last = tr(bank[0][0:KP, j * T:(j + 1) * T], probs[u][:, j * KP:(j + 1) * KP], ident[0:T, 0:T])
                last.then_inc(S["pT_ps"], 1)

                def values(j):
                    for c in range(DC):
                        last = mm(bank[6 + j // 2][0:KP, (j % 2) * D:(j % 2 + 1) * D], ctxT[u][:, c, j * KP:(j + 1) * KP],
                                  wT[:, WV, c, :], start=(c == 0), stop=(c == 1))
                    return last

                values(0)
                values(1).then_inc(S["v_ps"], 1)
                pe.wait_ge(S["pT_sb"], b + 1)
                for c in range(DC):
                    for j in range(KT):
                        last = mm(bank[1][:, c * T:(c + 1) * T], ctx[u][:, j, c * P:(c + 1) * P],
                                  probsT[0][:, j * T:(j + 1) * T], start=(j == 0), stop=(j == KT - 1))
                last.then_inc(S["o_ps"], 1)
                values(2).then_inc(S["v_ps"], 1)
                pe.wait_ge(S["o_sb"], b + 1)
                for c in range(DC):
                    last = mm(bank[2][0:T, 0:D], oT[:, c, :], wT[:, W0, c, :], start=(c == 0), stop=(c == 1))
                last.then_inc(S["y_ps"], 1)
                pe.wait_ge(S["k_sb"], 2 * b + 2)
                pe.wait_ge(S["v_sb"], 2 * b + 2)
                pe.wait_ge(S["x1"], b + 1)

            def gates(k):
                for b, u, it in pairs(pe):
                    pe.wait_ge(LN[1 + 2 * k]["xn"], b + 1)
                    for c in range(DC):
                        last = tr(bank[2][:, c * T:(c + 1) * T], xa[u][:, c * P:(c + 1) * P], ident[0:T, 0:T])
                    last.then_inc(R[k]["xT_ps"], 1)
                    pe.wait_ge(R[k]["xT_sb"], b + 1)
                    for c in range(DC):
                        last = mm(bank[3][0:T, 0:NE], xT[u][:, c, :], gate_w[:, k, c, :], start=(c == 0), stop=(c == 1))
                    last.then_inc(R[k]["g_ps"], 1)
                    pe.wait_ge(R[k]["g_sb"], b + 1)
                pe.wait_ge(R[k]["mask"], 1)
                mm(bank[4][0:T, 0:(B + 1) * NE], tri[:], hot16[:], start=True, stop=False)
                for t in range(1, B + 1):
                    last = mm(bank[4][0:T, t * NE:(B + 1) * NE], ones[:], hot16[:, 0:(B + 1 - t) * NE], start=False, stop=(t == B))
                last.then_inc(R[k]["rank"], 1)

            def slot_tokens(k, s, u, it):
                pe.wait_ge(F[k][f"x_in{u}"], 16 * (it + 1))
                for c in range(DC):
                    for g in range(2):
                        last = tr(bank[0][:, c * CAP + g * HC:c * CAP + (g + 1) * HC], xtok[u][:, g, c * P:(c + 1) * P],
                                  ident[0:HC, 0:HC])
                last.then_inc(F[k]["xT_ps"], 1)

            def slot_expert(k, s, u, it):
                pe.wait_ge(F[k][f"w1_in{u}"], 16 * (it + 1))
                pe.wait_ge(F[k]["xT_sb"], s + 1)
                for q in range(FC // 2):
                    for r in range(2):
                        f = 2 * q + r
                        for c in range(DC):
                            last = mm(bank[1 + q][:, r * CAP:(r + 1) * CAP], w1[u][:, c, f * P:(f + 1) * P], xsT[u][:, c, :],
                                      start=(c == 0), stop=(c == 1))
                    last.then_inc(F[k]["up"], 1)
                pe.wait_ge(F[k][f"w2_in{u}"], 16 * (it + 1))
                for d in range(DC):
                    for f in range(FC):
                        if d == 0 and f % 2 == 0:
                            pe.wait_ge(F[k]["h"], s * 4 + f // 2 + 1)
                        last = mm(bank[5][:, d * CAP:(d + 1) * CAP], w2[u][:, f, d * P:(d + 1) * P], hT[:, f, :],
                                  start=(f == 0), stop=(f == FC - 1))
                last.then_inc(F[k]["down"], 1)

            def slot_results(k, s, s_odd):
                pe.wait_ge(F[k]["yT"], s + 1)
                for g in range(2):
                    for c in range(DC):
                        last = tr(bank[6 + s_odd][0:HC, g * D + c * P:g * D + (c + 1) * P], yT[:, c, g * HC:(g + 1) * HC], ident[:])
                last.then_inc(F[k]["y_ps"], 1)

            def experts(k):
                slot_tokens(k, 0, 0, 0)
                with pe.Fori(0, NE // 2 - 1) as it:
                    for u in range(2):
                        slot_expert(k, it * 2 + u, u, it)
                        slot_tokens(k, it * 2 + u + 1, 1 - u, it + u)
                        slot_results(k, it * 2 + u, u)
                slot_expert(k, NE - 2, 0, NE // 2 - 1)
                slot_tokens(k, NE - 1, 1, NE // 2 - 1)
                slot_results(k, NE - 2, 0)
                slot_expert(k, NE - 1, 1, NE // 2 - 1)
                slot_results(k, NE - 1, 1)

            gates(0)
            experts(0)
            pe.wait_ge(R[0]["regs"], 1)
            n_over = pe.value_load(oid_i[0:1, 7:8], min_val=0, max_val=N_OVER)
            for j in range(N_OVER):
                with pe.If(n_over > j):
                    s = NE + j
                    slot_tokens(0, s, j % 2, s // 2)
                    slot_expert(0, s, j % 2, s // 2)
                    slot_results(0, s, j % 2)
            pe.drain().then_inc(S["layer0_done"], 1)

            for b, u, it in pairs(pe):
                pe.wait_ge(LN[2]["xn"], b + 1)
                for c in range(DC):
                    last = tr(bank[2][:, c * T:(c + 1) * T], xa[u][:, c * P:(c + 1) * P], ident[0:T, 0:T])
                last.then_inc(S["q_xT"], 1)
                pe.wait_ge(S["q_xTs"], b + 1)
                for o in range(DC):
                    for c in range(DC):
                        last = mm(bank[3][:, o * T:(o + 1) * T], wT[:, WQ, c, o * P:(o + 1) * P], xT[u][:, c, :],
                                  start=(c == 0), stop=(c == 1))
                last.then_inc(S["q_ps"], 1)
                pe.wait_ge(S["q_sb"], 2 * b + 2)

            def head_scores(b, u, h):
                pe.wait_ge(S["qm"], b * DC + h // HPC + 1)
                mm(bank[h % 4][0:T, 0:KL], qmask[u][:, h // HPC, h % HPC, :],
                   kT[:, h // HPC, bass.ds(b * KL, KL)], start=True, stop=True).then_inc(S["h_s"], 1)

            def head_transpose(b, h):
                pe.wait_ge(S["h_exp"], b * NH + h + 1)
                for j in range(KT):
                    last = tr(bank[4 + h % 2][0:KP, j * T:(j + 1) * T], probs[h % 4][:, j * KP:(j + 1) * KP], ident[0:T, 0:T])
                last.then_inc(S["h_pT"], 1)

            def head_product(b, u, h):
                if h == 0:
                    pe.wait_ge(S["vp"], b + 1)
                pe.wait_ge(S["h_pTa" if h % 2 == 0 else "h_pTd"], b * (NH // 2) + h // 2 + 1)
                r = HW * (h % 4)
                for j in range(KT):
                    last = mm(bank[6][r:r + HW, (h // 4) * T:(h // 4 + 1) * T], vpad[u][:, j, h, :],
                              probsT[h % 4][:, j * T:(j + 1) * T], start=(j == 0), stop=(j == KT - 1))
                last.then_inc(S["h_av"], 1)

            def out_tokens(b, u):
                pe.wait_ge(S["h_out"], b + 1)
                for q in range(4):
                    last = tr(bank[7][0:T, q * P:(q + 1) * P], outT[:, q, :], ident[:])
                last.then_inc(S["h_outT"], 1)

            def out_transpose(b, u):
                pe.wait_ge(S["h_o"], b + 1)
                for c in range(DC):
                    last = tr(bank[7][:, c * T:(c + 1) * T], xa[u][:, c * P:(c + 1) * P], ident[0:T, 0:T])
                last.then_inc(S["e_oT"], 1)

            def out_project(b, u):
                pe.wait_ge(S["e_oTs"], b + 1)
                for c in range(DC):
                    last = mm(bank[7][0:T, D:2 * D], oT[:, c, :], wT[:, WO, c, :], start=(c == 0), stop=(c == 1))
                last.then_inc(S["e_y"], 1)

            late = {LATE[0]: out_tokens, LATE[1]: out_transpose, LATE[2]: out_project}
            for b, u, it in pairs(pe):
                for i in range(NH + 3):
                    if i < NH:
                        head_scores(b, u, i)
                    if 2 <= i < NH + 2:
                        head_transpose(b, i - 2)
                    if i >= 3:
                        head_product(b, u, i - 3)
                    if u == 1 and i in late:
                        late[i](it * 2, 0)
                pe.wait_ge(S["h_out"], b + 1)
                if u == 1:
                    pe.wait_ge(S["x3"], it * 2 + 1)
                    for i in LATE:
                        late[i](b, u)
                    pe.wait_ge(S["x3"], it * 2 + 2)
            gates(1)
            experts(1)

        @block.scalar
        def _(act):
            def copy(dst, src):
                return nc.scalar.activation(dst, src, ACT.Copy)

            for n in range(5):
                act.wait_ge(S["w_ps"], n + 1)
                copy(wT[:, n].rearrange("p c d -> p (c d)"), bank[n % 2][:]).then_inc(S["w_sb"], 1)
            act.wait_ge(S["bias_ps"], 1)
            copy(biasT[:], bank[2][:, 0:P + 36]).then_inc(S["bias_sb"], 1)
            act.wait_ge(S["bias_sb"], 1)

            for b, u, it in pairs(act):
                act.wait_ge(S["ctxT_ps"], b + 1)
                copy(ctxT[u][:, 0, :], bank[0][:, 0:KL]).then_inc(S["ctxT_act"], 1)
                act.wait_ge(S["s_max"], b + 1)
                nc.scalar.activation(probs[u][:], scores[:], ACT.Exp, bias=rowmax[:], scale=1.0 / 16,
                                     accum_out=at(esum, b) if False else esum[:, bass.ds(b, 1)]).then_inc(S["s_exp"], 1)
                for o in range(DC):
                    act.wait_ge(S["k_ps"], b * 2 + o + 1)
                    nc.scalar.activation(kT[:, o, bass.ds(b * KL, KL)], bank[4 + o][:, 0:KL], ACT.Identity,
                                         bias=biasT[:, P + 34 + o:P + 35 + o]).then_inc(S["k_sb"], 1)
                act.wait_ge(S["pT_ps"], b + 1)
                copy(probsT[0][:], bank[0][0:KP, 0:KT * T]).then_inc(S["pT_sb"], 1)
                act.wait_ge(S["o_ps"], b + 1)
                copy(oT[:].rearrange("p c t -> p (c t)"), bank[1][:, 0:DC * T]).then_inc(S["o_sb"], 1)

            def gates(k):
                for b, u, it in pairs(act):
                    act.wait_ge(LN[1 + 2 * k]["xn"], b + 1)
                    copy(at(xn, b), xa[u][:]).then_inc(R[k]["kept"], 1)
                act.wait_ge(R[k]["diff"], 1)
                if k == 0:
                    nc.scalar.activation(rt[:], rt[:], ACT.Exp).then_inc(R[k]["exp"], 1)
                else:
                    nc.scalar.activation(ra[:], ra[:], ACT.Exp).then_inc(R[k]["exp"], 1)

            def slot(k, s, e):
                func = (ACT.Gelu_apprx_tanh, ACT.Relu)[k]
                for q in range(FC // 2):
                    act.wait_ge(F[k]["up"], s * 4 + q + 1)
                    for r in range(2):
                        f = 2 * q + r
                        last = nc.scalar.activation(hT[:, f, :], bank[1 + q][:, r * CAP:(r + 1) * CAP], func,
                                                    bias=col(64 * k + e * FC + f))
                    last.then_inc(F[k]["h"], 1)
                act.wait_ge(F[k]["down"], s + 1)
                for d in range(DC):
                    last = nc.scalar.activation(yT[:, d, :], bank[5][:, d * CAP:(d + 1) * CAP], ACT.Identity,
                                                bias=col(P + 16 * k + e * DC + d))
                last.then_inc(F[k]["yT"], 1)

            def col(i):
                return biasT[:, i:i + 1] if isinstance(i, int) else biasT[:, bass.ds(i, 1)]

            gates(0)
            for s, u, it in pairs(act):
                slot(0, s, s)
            act.wait_ge(R[0]["regs"], 1)
            n_over = act.value_load(oid_i[0:1, 7:8], min_val=0, max_val=N_OVER)
            for j in range(N_OVER):
                with act.If(n_over > j):
                    slot(0, NE + j, act.value_load(oid_i[0:1, j:j + 1], min_val=0, max_val=NE - 1))

            for b, u, it in pairs(act):
                for i in range(NH + 2):
                    if i < NH:
                        act.wait_ge(S["h_max"], b * NH + i + 1)
                        nc.scalar.activation(probs[i % 4][:], bank[i % 4][0:T, 0:KL], ACT.Exp,
                                             bias=nmax[u][:, i:i + 1]).then_inc(S["h_exp"], 1)
                    if i >= 2 and i % 2 == 0:
                        act.wait_ge(S["h_pT"], b * NH + i - 1)
                        copy(probsT[(i - 2) % 4][:], bank[4][0:KP, 0:KT * T]).then_inc(S["h_pTa"], 1)
                act.wait_ge(S["h_av"], b * NH + NH)
                copy(outT[:].rearrange("p q t -> p (q t)"), bank[6][:, 0:4 * T]).then_inc(S["h_out"], 1)
            gates(1)
            for s, u, it in pairs(act):
                slot(1, s, s)

        @block.vector
        def _(dve):
            v = nc.vector
            done = [0]

            def link(ins):
                done[0] += 1
                ins.then_inc(S["chain"], 1)
                dve.wait_ge(S["chain"], done[0])

            def statistics(k):
                dve.wait_ge(LN[k]["stats"], B)
                for b in range(B):
                    v.bn_aggr(lmv[:, b], lstat[:, b]).then_inc(LN[k]["aggr"], 1)
                dve.wait_ge(LN[k]["aggr"], B)
                v.tensor_scalar(lvar[:], lmv[:, :, 1], EPS, None, ALU.add).then_inc(LN[k]["var"], 1)
                dve.wait_ge(LN[k]["rstd"], 1)

            def stats(k, b):
                v.bn_stats(at(lstat, b), at(x, b)).then_inc(LN[k]["stats"], 1)

            def normalise(k, b, u):
                v.tensor_scalar(xa[u][:], at(x, b), lmv[:, bass.ds(b, 1), 0:1].rearrange("p b o -> p (b o)"),
                                rstd[:, bass.ds(b, 1)], ALU.subtract, ALU.mult).then_inc(LN[k]["xn"], 1)

            dve.wait_ge(S["x_in"], 16)
            with dve.Fori(0, B) as b:
                stats(0, b)
            statistics(0)
            dve.wait_ge(S["bcast_in"], 16 * 8)
            dve.wait_ge(S["consts_made"], 2)
            link(v.memset(hot16[:], 0.0))
            link(v.tensor_copy(lens[:], lens_i[:]))
            link(v.tensor_tensor(qflag[:], qpos[:].to_broadcast([T, B]), lens[:], ALU.is_ge))

            for b, u, it in pairs(dve):
                normalise(0, b, u)
                dve.wait_ge(LN[0]["xn"], b + 1)
                v.tensor_tensor(at(x, b), at(x, b), b_attn[:, 0, :], ALU.add).then_inc(S["xb"], 1)
                v.tensor_scalar(kmask[:], kpos[:], lens[:, bass.ds(b, 1)], BIG, ALU.is_ge, ALU.mult).then_inc(S["kmask_set"], 1)
                dve.wait_ge(S["ctxT_ps"], b + 1)
                v.tensor_copy(ctxT[u][:, 1, :], bank[1][:, 0:KL]).then_inc(S["ctxT_dve"], 1)
                dve.wait_ge(S["xT_ps"], b + 1)
                v.tensor_copy(xT[u][:].rearrange("p c t -> p (c t)"), bank[2][:, 0:DC * T]).then_inc(S["xT_sb"], 1)
                dve.wait_ge(S["s_ps"], b + 1)
                dve.wait_ge(S["kmask_set"], b + 1)
                v.scalar_tensor_tensor(scores[:], kmask[:], qflag[:, bass.ds(b, 1)], bank[3][0:T, 0:KL], ALU.mult,
                                       ALU.add).then_inc(S["s_masked"], 1)
                dve.wait_ge(S["s_masked"], b + 1)
                v.tensor_reduce(rowmax[:], scores[:], axis=AX.X, op=ALU.max, negate=True).then_inc(S["s_rowmax"], 1)
                dve.wait_ge(S["s_rowmax"], b + 1)
                v.tensor_scalar(rowmax[:], rowmax[:], 1.0 / 16, None, ALU.mult).then_inc(S["s_max"], 1)
                dve.wait_ge(S["s_exp"], b + 1)
                v.reciprocal(esinv[:], esum[:, bass.ds(b, 1)]).then_inc(S["esum_inv"], 1)
                dve.wait_ge(S["v_ps"], b * 2 + 1)
                v.tensor_tensor(vals[:, bass.ds(b * KT, 2), :], bank[6][0:KP, :].rearrange("p (j d) -> p j d", d=D),
                                bv[:].unsqueeze(1).to_broadcast([KP, 2, D]), ALU.add).then_inc(S["v_sb"], 1)
                dve.wait_ge(S["v_ps"], b * 2 + 2)
                v.tensor_tensor(at(vals, b * KT + 2), bank[7][0:KP, 0:D], bv[:], ALU.add).then_inc(S["v_sb"], 1)
                dve.wait_ge(S["y_ps"], b + 1)
                dve.wait_ge(S["xb"], b + 1)
                dve.wait_ge(S["esum_inv"], b + 1)
                v.scalar_tensor_tensor(at(x, b), bank[2][0:T, 0:D], esinv[:], at(x, b), ALU.mult, ALU.add).then_inc(S["x1"], 1)

            def gates(k):
                with dve.Fori(0, B) as b:
                    stats(1 + 2 * k, b)
                statistics(1 + 2 * k)
                for b, u, it in pairs(dve):
                    normalise(1 + 2 * k, b, u)
                    dve.wait_ge(R[k]["xT_ps"], b + 1)
                    v.tensor_copy(xT[u][:].rearrange("p c t -> p (c t)"), bank[2][:, 0:DC * T]).then_inc(R[k]["xT_sb"], 1)
                    dve.wait_ge(R[k]["kept"], b + 1)
                    dve.wait_ge(R[k]["g_ps"], b + 1)
                    v.tensor_tensor(at(logit, b), bank[3][0:T, 0:NE], gate_b[:, k, :], ALU.add).then_inc(R[k]["g_sb"], 1)
                dve.wait_ge(R[k]["g_sb"], B)

            def choose(k):
                for b in range(B):
                    last = v.max(top8[:, b], logit[:, b])
                link(last)
                for b in range(B):
                    last = v.max_index(topi[:, b], top8[:, b], logit[:, b])
                link(last)
                link(v.tensor_copy(topf[:], topi[:, :, 0:2]))
                for c in range(k + 1):
                    link(v.tensor_tensor(hot[:, c], eidx[:].unsqueeze(1).to_broadcast([T, B, NE]),
                                         topf[:, :, c:c + 1].to_broadcast([T, B, NE]), ALU.is_equal))
                wide = hot16[:, 0:B * NE].rearrange("p (b e) -> p b e", e=NE)
                if k == 0:
                    v.tensor_copy(wide, hot[:, 0]).then_inc(R[k]["mask"], 1)
                    v.tensor_tensor(rt[:], logit[:], top8[:, :, 0:1].to_broadcast([T, B, NE]), ALU.subtract).then_inc(R[k]["diff"], 1)
                    dve.wait_ge(R[k]["exp"], 1)
                    link(v.tensor_reduce(rb[:], rt[:], axis=AX.X, op=ALU.add))
                    link(v.reciprocal(wsel[:, 0], rb[:]))
                else:
                    v.tensor_tensor(wide, hot[:, 0], hot[:, 1], ALU.add).then_inc(R[k]["mask"], 1)
                    v.tensor_tensor(ra[:], top8[:, :, 1], top8[:, :, 0], ALU.subtract).then_inc(R[k]["diff"], 1)
                    dve.wait_ge(R[k]["exp"], 1)
                    link(v.tensor_scalar(rb[:], ra[:], 1.0, None, ALU.add))
                    link(v.reciprocal(wsel[:, 0], rb[:]))
                    link(v.tensor_tensor(wsel[:, 1], ra[:], wsel[:, 0], ALU.mult))
                dve.wait_ge(R[k]["rank"], 1)
                link(v.tensor_copy(rank[:], bank[4][0:T, 0:(B + 1) * NE]))
                for c in range(k + 1):
                    link(v.tensor_tensor(rt[:], hot[:, c], rank[:, 0:B * NE].rearrange("p (b e) -> p b e", e=NE), ALU.mult))
                    link(v.tensor_reduce(rsel[:, c], rt[:], axis=AX.X, op=ALU.add))

            def place_top1():
                total = rank[:, B * NE:(B + 1) * NE]
                link(v.tensor_scalar(ocum[:, 0], total, float(CAP), None, ALU.is_gt))
                for j in range(2, N_OVER + 1):
                    link(v.scalar_tensor_tensor(ocum[:, j % 2 + 1 if j % 2 == 0 else 0], total, float(CAP * j),
                                                ocum[:, 0 if j % 2 == 0 else 1], ALU.is_gt, ALU.add)
                         if False else
                         v.scalar_tensor_tensor(ocum[:, (j + 1) % 2], total, float(CAP * j), ocum[:, j % 2], ALU.is_gt, ALU.add))
                own = (N_OVER + 1) % 2
                a, b = own, 1 - own
                link(v.tensor_copy(ocum[:, 2], ocum[:, own]))
                for step in (1, 2, 4):
                    v.tensor_copy(ocum[:, b, 0:step], ocum[:, a, 0:step])
                    link(v.tensor_tensor(ocum[:, b, step:], ocum[:, a, step:], ocum[:, a, 0:NE - step], ALU.add))
                    a, b = b, a
                link(v.tensor_tensor(rt[:, 0:N_OVER], ocum[:, a].unsqueeze(1).to_broadcast([T, N_OVER, NE]),
                                     eidx[:, 0:N_OVER].unsqueeze(2).to_broadcast([T, N_OVER, NE]), ALU.is_le))
                link(v.memset(oid[:], 0.0))
                link(v.tensor_reduce(oid[:, 0:N_OVER], rt[:, 0:N_OVER], axis=AX.X, op=ALU.add))
                link(v.tensor_scalar(oid[:, 0:N_OVER], oid[:, 0:N_OVER], float(NE - 1), None, ALU.min))
                link(v.tensor_copy(oid[:, 7:8], ocum[:, a, NE - 1:NE]))
                v.tensor_copy(oid_i[:], oid[:]).then_inc(R[0]["regs"], 1)
                link(v.tensor_tensor(ocum[:, b], ocum[:, a], ocum[:, 2], ALU.subtract))
                link(v.tensor_tensor(rt[:], hot[:, 0], ocum[:, b].unsqueeze(1).to_broadcast([T, B, NE]), ALU.mult))
                link(v.tensor_reduce(rb[:], rt[:], axis=AX.X, op=ALU.add))
                link(v.tensor_scalar(rb[:], rb[:], float(NE - 1), float(CAP), ALU.add, ALU.mult))
                link(v.tensor_scalar(rc[:], topf[:, :, 0], float(CAP), None, ALU.mult))
                link(v.tensor_tensor(rb[:], rb[:], rc[:], ALU.subtract))
                link(v.tensor_scalar(ra[:], rsel[:, 0], float(CAP), None, ALU.is_gt))
                link(v.tensor_tensor(rb[:], rb[:], ra[:], ALU.mult))
                link(v.tensor_tensor(rc[:], rc[:], rb[:], ALU.add))
                link(v.scalar_tensor_tensor(rc[:], rsel[:, 0], -1.0, rc[:], ALU.add, ALU.add))
                link(v.tensor_copy(pos_get[:, 0], rc[:]))
                v.tensor_copy(pos_put[:, 0], rc[:]).then_inc(R[0]["pos"], 1)

            def place_top2():
                for c in range(2):
                    link(v.tensor_scalar(ra[:], rsel[:, c], float(CAP), None, ALU.is_le))
                    link(v.tensor_tensor(wsel[:, c], wsel[:, c], ra[:], ALU.mult))
                    link(v.scalar_tensor_tensor(rb[:], topf[:, :, c], float(CAP), rsel[:, c], ALU.mult, ALU.add))
                    link(v.tensor_scalar(rb[:], rb[:], -1.0, None, ALU.add))
                    link(v.tensor_tensor(rc[:], rb[:], ra[:], ALU.mult))
                    link(v.tensor_copy(pos_get[:, c], rc[:]))
                    link(v.tensor_scalar(rc[:], tokid[:], float(ROWS1 + c * B * T), None, ALU.add))
                    link(v.tensor_tensor(rb[:], rb[:], rc[:], ALU.subtract))
                    link(v.tensor_tensor(rb[:], rb[:], ra[:], ALU.mult))
                    link(v.tensor_tensor(rb[:], rb[:], rc[:], ALU.add))
                    ins = v.tensor_copy(pos_put[:, c], rb[:])
                    if c == 0:
                        link(ins)
                    else:
                        ins.then_inc(R[1]["pos"], 1)

            def slot_tokens(k, s, u):
                dve.wait_ge(F[k]["xT_ps"], s + 1)
                v.tensor_copy(xsT[u][:].rearrange("p c t -> p (c t)"), bank[0][:, 0:DC * CAP]).then_inc(F[k]["xT_sb"], 1)

            def slot_results(k, s, u, it):
                dve.wait_ge(F[k]["y_ps"], s + 1)
                if not (isinstance(it, int) and it == 0):
                    dve.wait_ge(F[k][f"y_out{u}"], it * 16)
                v.tensor_copy(ytok[u].rearrange("p g d -> p (g d)"), bank[6 + u][0:HC, :]).then_inc(F[k]["y_sb"], 1)

            def experts(k):
                slot_tokens(k, 0, 0)
                for u in range(2):
                    slot_tokens(k, u + 1, 1 - u)
                    slot_results(k, u, u, 0)
                with dve.Fori(1, NE // 2 - 1) as it:
                    for u in range(2):
                        slot_tokens(k, it * 2 + u + 1, 1 - u)
                        slot_results(k, it * 2 + u, u, it)
                slot_tokens(k, NE - 1, 1)
                slot_results(k, NE - 2, 0, NE // 2 - 1)
                slot_results(k, NE - 1, 1, NE // 2 - 1)

            dve.wait_ge(S["x1"], B)
            gates(0)
            choose(0)
            place_top1()
            experts(0)
            dve.wait_ge(R[0]["regs"], 1)
            n_over = dve.value_load(oid_i[0:1, 7:8], min_val=0, max_val=N_OVER)
            for j in range(N_OVER):
                with dve.If(n_over > j):
                    slot_tokens(0, NE + j, j % 2)
                    slot_results(0, NE + j, j % 2, (NE + j) // 2)

            dve.wait_ge(G[0][0], 16 * B)
            with dve.Fori(0, B) as b:
                v.scalar_tensor_tensor(at(x, b), got[:, 0, bass.ds(b, 1), :].rearrange("p b d -> p (b d)"),
                                       wsel[:, 0, bass.ds(b, 1)], at(x, b), ALU.mult, ALU.add).then_inc(S["x2"], 1)
            dve.wait_ge(S["x2"], B)
            with dve.Fori(0, B) as b:
                stats(2, b)
            statistics(2)
            for b, u, it in pairs(dve):
                normalise(2, b, u)
                dve.wait_ge(LN[2]["xn"], b + 1)
                v.tensor_tensor(at(x, b), at(x, b), b_attn[:, 1, :], ALU.add).then_inc(S["xb"], 1)
                dve.wait_ge(S["q_xT"], b + 1)
                v.tensor_copy(xT[u][:].rearrange("p c t -> p (c t)"), bank[2][:, 0:DC * T]).then_inc(S["q_xTs"], 1)
                dve.wait_ge(S["q_ps"], b + 1)
                for o in range(DC):
                    v.tensor_scalar(at(qT[:, o], b), bank[3][:, o * T:(o + 1) * T], biasT[:, P + 32 + o:P + 33 + o],
                                    0.25, ALU.add, ALU.mult).then_inc(S["q_sb"], 1)
            dve.wait_ge(S["xb"], 2 * B)

            def out_tokens(b, u):
                dve.wait_ge(S["h_outT"], b + 1)
                o = bank[7][0:T, :].rearrange("p (h w) -> p h w", w=HW)
                v.reciprocal(rinv[:].unsqueeze(2), o[:, :, HD:HD + 1]).then_inc(S["h_rinv"], 1)
                dve.wait_ge(S["h_rinv"], b + 1)
                v.tensor_tensor(xa[u][:].rearrange("p (h d) -> p h d", d=HD), o[:, :, 0:HD],
                                rinv[:].unsqueeze(2).to_broadcast([T, NH, HD]), ALU.mult).then_inc(S["h_o"], 1)

            def out_transpose(b, u):
                dve.wait_ge(S["e_oT"], b + 1)
                v.tensor_copy(oT[:].rearrange("p c t -> p (c t)"), bank[7][:, 0:DC * T]).then_inc(S["e_oTs"], 1)

            def out_project(b, u):
                dve.wait_ge(S["e_y"], b + 1)
                v.tensor_tensor(at(x, b), bank[7][0:T, D:2 * D], at(x, b), ALU.add).then_inc(S["x3"], 1)

            late = {LATE[0]: out_tokens, LATE[1]: out_transpose, LATE[2]: out_project}
            for b, u, it in pairs(dve):
                for i in range(NH + 2):
                    if i < NH:
                        dve.wait_ge(S["h_s"], b * NH + i + 1)
                        v.tensor_reduce(nmax[u][:, i:i + 1], bank[i % 4][0:T, 0:KL], axis=AX.X, op=ALU.max,
                                        negate=True).then_inc(S["h_max"], 1)
                    if i >= 2 and i % 2 == 1:
                        dve.wait_ge(S["h_pT"], b * NH + i - 1)
                        v.tensor_copy(probsT[(i - 2) % 4][:], bank[5][0:KP, 0:KT * T]).then_inc(S["h_pTd"], 1)
                    if u == 1 and i in late:
                        late[i](it * 2, 0)
                if u == 1:
                    for i in LATE:
                        late[i](b, u)
            dve.wait_ge(S["x3"], B)
            gates(1)
            choose(1)
            place_top2()
            experts(1)
            for c in range(2):
                dve.wait_ge(G[1][c], 16 * B)
            with dve.Fori(0, B) as b:
                v.scalar_tensor_tensor(at(x, b), got[:, 0, bass.ds(b, 1), :].rearrange("p b d -> p (b d)"),
                                       wsel[:, 0, bass.ds(b, 1)], at(x, b), ALU.mult, ALU.add).then_inc(S["x4a"], 1)
            with dve.Fori(0, B) as b:
                dve.wait_ge(S["x4a"], b + 1)
                v.scalar_tensor_tensor(at(x, b), got[:, 1, bass.ds(b, 1), :].rearrange("p b d -> p (b d)"),
                                       wsel[:, 1, bass.ds(b, 1)], at(x, b), ALU.mult, ALU.add).then_inc(S["x4"], 1)


_INS = ["x", "ctx_1024", "_lenS2", "L0_xattn_W", "L0_xattn_b", "L0_ffn_switch_w", "L0_ffn_switch_b", "L0_ffn_w1",
        "L0_ffn_b1", "L0_ffn_w2", "L0_ffn_b2", "L1_xattn_Wq", "L1_xattn_bq", "L1_xattn_Wk", "L1_xattn_bk",
        "L1_xattn_Wv", "L1_xattn_bv", "L1_xattn_Wo", "L1_xattn_bo", "L1_ffn_gate_w", "L1_ffn_gate_b", "L1_ffn_w1",
        "L1_ffn_b1", "L1_ffn_w2", "L1_ffn_b2"]


def kernel(**inputs):
    import numpy as np
    import concourse.bacc as bacc
    from concourse import mybir as mb
    from concourse.bass_utils import run_bass_kernel_spmd

    nc = bacc.Bacc("TRN2", target_bir_lowering=False, num_devices=1)
    arrays, A = {}, {}
    for name in _INS:
        a = np.ascontiguousarray(inputs[name])
        arrays[f"in_{name}"] = a
        A[name] = nc.dram_tensor(f"in_{name}", a.shape, mb.dt.from_np(a.dtype), kind="ExternalInput").ap()
    out = nc.dram_tensor("out_tokens", A["x"].shape, mb.dt.float32, kind="ExternalOutput").ap()
    build_program(nc, A, out)
    r = run_bass_kernel_spmd(nc, [arrays], core_ids=[0])
    return r.results[0]["out_tokens"]
```

```python
import concourse.bass as bass
from concourse import mybir
from contextlib import ExitStack


def build_program(nc, A, out):
    f32 = mybir.dt.float32
    bf16 = mybir.dt.bfloat16
    i32 = mybir.dt.int32
    u32 = mybir.dt.uint32
    ALU = mybir.AluOpType
    ACT = mybir.ActivationFunctionType
    AX = mybir.AxisListType

    B, T, D = A["x"].shape
    KL = A["ctx_1024"].shape[1]
    NE = A["L0_ffn_w1"].shape[0]
    FF = A["L0_ffn_w1"].shape[2]
    P = 128
    DC = D // P
    FC = FF // P
    KT = 3
    KP = KL // KT
    NH, HD = 16, D // 16
    HPC = P // HD
    HW = 32
    CAP = int(1.25 * B * T / NE)
    HC = CAP // 2
    N_OVER = 6
    STRIDE = 8 * CAP
    RW = D + 4
    BIG = -16.0e13
    EPS = 1e-5
    HOPS = (9, 15)

    x_rows = A["x"].rearrange("b t d -> t b d")
    out_rows = out.rearrange("b t d -> t b d")
    ctx_rows = A["ctx_1024"].rearrange("b (j p) d -> p b j d", p=KP)

    tok_rows = [nc.dram_tensor("slot_tokens_0", (NE * STRIDE, RW), f32).ap(),
                nc.dram_tensor("slot_tokens_1", (NE * CAP + 2 * B * T, RW), f32).ap()]
    acc = [nc.dram_tensor("stream_0", (B * T + CAP, D), f32).ap(), nc.dram_tensor("stream_1", (B * T + CAP, D), f32).ap()]

    stack = ExitStack()
    with stack:
        def sb(name, shape, dt=f32):
            return stack.enter_context(nc.sbuf_tensor(name, list(shape), dt))

        def sem(name):
            return stack.enter_context(nc.semaphore(name))

        bank = [stack.enter_context(nc.psum_tensor(f"bank{i}", [P, 512], f32)) for i in range(8)]

        ident = sb("ident", [P, P])
        tri = sb("tri", [T, T], bf16)
        ones = sb("ones", [T, T], bf16)
        kpos = sb("kpos", [T, KL])
        kpos_i = sb("kpos_i", [T, KL], i32)
        qpos = sb("qpos", [T, 1])
        qpos_i = sb("qpos_i", [T, 1], i32)
        eidx = sb("eidx", [T, NE])
        eidx_i = sb("eidx_i", [T, NE], i32)
        headmask = sb("headmask", [P, HPC])
        tokid = sb("tokid", [T, B])
        tokid_i = sb("tokid_i", [T, B], i32)
        neg_half = sb("neg_half", [T, 1])
        pad_i = sb("pad_i", [HC, 2], i32)
        empty = sb("empty_rows", [HC, 2, RW])
        raw = sb("raw_weights", [P, 5, DC, D])
        wT = sb("weights_T", [P, 5, DC, D])
        bias_rows = sb("bias_rows", [P, P])
        bias_rows2 = sb("bias_rows2", [4 * NE + 4, P])
        biasT = sb("biasT", [P, P + 4 * NE + 4])
        b_attn = sb("b_attn", [T, 2, D])
        bv = sb("bv", [KP, D])
        gate_w = sb("gate_w", [P, 2, DC, NE])
        gate_b = sb("gate_b", [T, 2, NE])
        lens_i = sb("lens_i", [T, B], i32)
        lens = sb("lens", [T, B])
        qflag = sb("qflag", [T, B])
        x = sb("x_tokens", [T, B, D])
        xrow = [[sb(f"xrow{c}{u}", [T, RW]) for u in range(2)] for c in range(2)]
        ctx = [sb(f"ctx{u}", [KP, KT, D]) for u in range(2)]
        ctxT = [sb(f"ctxT{u}", [P, DC, KL]) for u in range(2)]
        xa = [sb(f"xa{u}", [T, D]) for u in range(2)]
        rowmax = [sb(f"rowmax{u}", [T, 1]) for u in range(2)]
        xgT = sb("xgT", [P, DC, T])
        esinv = sb("esinv", [T, 1])
        xT = [sb(f"xT{u}", [P, DC, T]) for u in range(2)]
        kT = sb("kT", [P, DC, B * KL])
        vals = sb("vals", [KP, B * KT, D])
        vpad = [sb(f"vpad{u}", [KP, KT, NH, HW]) for u in range(2)]
        scores = sb("scores", [T, KL])
        kmask = sb("kmask", [T, KL])
        probs = [sb(f"probs{i}", [T, KL]) for i in range(4)]
        probsT = [sb(f"probsT{i}", [KP, KT * T]) for i in range(4)]
        oT = sb("oT", [P, DC, T])
        outT = sb("outT", [P, 4, T])
        qT = [sb(f"qT{u}", [P, DC, T]) for u in range(2)]
        oa = sb("out_heads", [T, D])
        qmask = [sb(f"qmask{u}", [P, DC, HPC, T]) for u in range(2)]
        nmax = [sb(f"nmax{u}", [T, NH]) for u in range(2)]
        rinv = sb("rinv", [T, NH])
        esum = [sb(f"esum{u}", [T, 1]) for u in range(2)]
        lstat = [sb(f"ln_stats{k}", [T, 6]) for k in range(4)]
        lmv = [sb(f"ln_mean_var{k}", [T, 2]) for k in range(4)]
        lvar = [sb(f"ln_var_eps{k}", [T, 1]) for k in range(4)]
        rstd = [sb(f"ln_rstd{k}", [T, 1]) for k in range(4)]
        w1 = [sb(f"w1_{u}", [P, DC, FF]) for u in range(2)]
        w2 = [sb(f"w2_{u}", [P, FC, D]) for u in range(2)]
        xtok = [sb(f"xtok{u}", [HC, 2, RW]) for u in range(2)]
        sid = [sb(f"slot_ids{u}", [HC, 2], u32) for u in range(2)]
        xsT = [sb(f"xsT{u}", [P, DC, CAP]) for u in range(2)]
        spare = [qmask[u][:].rearrange("p c j t -> p (c j t)") for u in range(2)]
        hT = spare[0][:, 0:FC * CAP].rearrange("p (f t) -> p f t", f=FC)
        yT = spare[0][:, FC * CAP:(FC + DC) * CAP].rearrange("p (d t) -> p d t", d=DC)
        ytok = [spare[1][0:HC, u * 2 * D:(u + 1) * 2 * D].rearrange("p (g d) -> p g d", g=2) for u in range(2)]
        logit = sb("logit", [T, NE])
        top8 = sb("top8", [T, 8])
        topn = sb("topn", [T, 1])
        topi = sb("topi", [T, 8], u32)
        topf = sb("topf", [T, 2])
        hot = sb("hot", [T, 2, NE])
        hot16 = sb("hot16", [T, NE], bf16)
        seen = [sb(f"seen{k}", [T, NE]) for k in range(2)]
        wexp = sb("wexp", [T, NE])
        wsum = sb("wsum", [T, 1])
        trash = sb("trash", [T, B, 2])
        seen16 = [sb(f"seen16_{k}", [T, NE], bf16) for k in range(2)]
        rank = sb("rank", [T, NE])
        rt = sb("route_tmp", [T, NE])
        rs = sb("route_sum", [T, 2])
        ra = sb("route_a", [T, 2])
        rb = sb("route_b", [T, 2])
        keep = sb("route_keep", [T, 2])
        pos = [[sb(f"pos{c}{u}", [T, 1], i32) for u in range(2)] for c in range(2)]
        total = sb("total", [T, NE])
        ocum = sb("over_cum", [T, 3, NE])
        oat = sb("over_at", [T, N_OVER, NE])
        ofl = sb("over_table", [T, 4, NE])
        table = sb("over_table_i", [T, 4, NE], i32)

        S = {n: sem(n) for n in (
            "ident_made", "passed", "ranks_read", "consts_made", "consts_step", "weights_in", "biases_in", "bcast_in", "x_in", "emptied", "refilled",
            "bias_ps", "bias_sb", "w_ps", "w_sb", "chain", "empty_made", "vpad_made",
            "ctx_in0", "ctx_in1", "ctxT_ps", "ctxT_act", "ctxT_dve", "xT_ps", "xT_sb", "s_ps", "s_masked", "s_rowmax",
            "s_max", "s_exp", "kmask_set", "k_ps", "k_sb", "v_ps", "v_sb", "pT_ps", "pT_sb", "o_ps", "o_sb", "y_ps",
            "esum_inv", "xb", "x1", "qm", "vp", "h_s", "h_max", "h_exp", "h_pT", "h_pTa", "h_pTd", "h_av", "h_out",
            "h_outT", "h_rinv", "h_o", "e_oT", "e_oTs", "e_y", "x3", "q_xT", "q_xTs", "q_ps", "q_sb", "xo",
            "layer0_done", "out_done", "x2_in0", "x2_in1", "table_set")}
        LN = [{n: sem(f"ln{k}_{n}") for n in ("stats", "var", "eps", "rstd", "xn")} for k in range(4)]
        R = [{n: sem(f"route{k}_{n}") for n in ("xT_ps", "xT_sb", "g_ps", "g_sb", "step", "best", "hot", "seen", "rank", "wexp",
                                                "row2", "row", "put0", "put1", "saved")} for k in range(2)]
        F = [{n: sem(f"ffn{k}_{n}") for n in ("w1_in0", "w1_in1", "w2_in0", "w2_in1", "x_in0", "x_in1", "xT_ps", "xT_sb",
                                              "up", "h", "down", "yT", "y_ps", "y_sb", "id", "added0", "added1")}
             for k in range(2)]

        block = stack.enter_context(nc.Block())

        def at(ap, i):
            if isinstance(i, int):
                return ap[:, i]
            sub = ap[:, bass.ds(i, 1)]
            names = " ".join("abc"[:len(sub.shape) - 2])
            return sub.rearrange(f"p i {names} -> p (i {names.split()[0]}) {' '.join(names.split()[1:])}")

        def batches(eng):
            yield 0, 0, 0, False, True
            with eng.Fori(0, B // 2 - 1) as it:
                yield it * 2 + 1, 1, it, True, True
                yield it * 2 + 2, 0, it + 1, True, True
            yield B - 1, 1, B // 2 - 1, True, False

        def pairs(eng):
            with eng.Fori(0, B // 2) as it:
                for u in range(2):
                    yield it * 2 + u, u, it

        names = ["L0_xattn_W", "L1_xattn_Wq", "L1_xattn_Wk", "L1_xattn_Wv", "L1_xattn_Wo"]
        W0, WQ, WK, WV, WO = range(5)
        w1_src = [A[f"L{k}_ffn_w1"].rearrange("e (c p) f -> p e c f", p=P) for k in range(2)]
        w2_src = [A[f"L{k}_ffn_w2"].rearrange("e (c p) d -> p e c d", p=P) for k in range(2)]
        slots = [t[0:n].rearrange("(e r) d -> e r d", e=NE)[:, 0:CAP].rearrange("e (p g) d -> p e (g d)", g=2)
                 for t, n in zip(tok_rows, (NE * STRIDE, NE * CAP))]

        GATE, RANK = 480, 488

        def plain(eng):
            eng.sem_inc(S["passed"], 1)

        def before(u, it):
            return 1 - u, (it if u == 1 else it - 1)

        @block.sync
        def _(sp):
            def load_ctx(b, u):
                sp.dma_start(ctx[u][:], at(ctx_rows, b)).then_inc(S[f"ctx_in{u}"], 16)

            def load_expert(k, e, u):
                sp.dma_start(w1[u][:], at(w1_src[k], e)).then_inc(F[k][f"w1_in{u}"], 16)
                sp.dma_start(w2[u][:], at(w2_src[k], e)).then_inc(F[k][f"w2_in{u}"], 16)

            def store_stream(k, b):
                sp.dma_start(acc[k][bass.ds(b * T, T), :], at(x, b)).then_inc(R[k]["saved"], 16)

            load_ctx(0, 0)
            sp.dma_start(x[:], x_rows).then_inc(S["x_in"], 16)
            for n, name in enumerate(names):
                sp.dma_start(raw[:, n], A[name].rearrange("(c p) d -> p c d", p=P)).then_inc(S["weights_in"], 16)
            load_ctx(1, 1)
            for k in range(2):
                sp.dma_start(bias_rows[64 * k:64 * k + 64, :],
                             A[f"L{k}_ffn_b1"].rearrange("e (f p) -> (e f) p", p=P)).then_inc(S["biases_in"], 16)
                sp.dma_start(bias_rows2[16 * k:16 * k + 16, :],
                             A[f"L{k}_ffn_b2"].rearrange("e (f p) -> (e f) p", p=P)).then_inc(S["biases_in"], 16)
            for n, name in enumerate(("L1_xattn_bq", "L1_xattn_bk")):
                sp.dma_start(bias_rows2[32 + 2 * n:34 + 2 * n, :],
                             A[name].rearrange("(f p) -> f p", p=P)).then_inc(S["biases_in"], 16)
            sp.wait_ge(S["empty_made"], 1)
            blank = empty[:].rearrange("p g d -> p (g d)")
            for k in range(2):
                for e in range(NE):
                    sp.dma_start(slots[k][:, e], blank).then_inc(S["emptied"], 16)
                sp.dma_start(acc[k][B * T:].rearrange("(p g) d -> p g d", g=2), empty[:, :, 0:D]).then_inc(S["emptied"], 16)
            for u in range(2):
                load_expert(0, u, u)
            with sp.Fori(0, B // 2 - 1) as it:
                for u in range(2):
                    sp.wait_ge(S["o_ps"], it * 2 + u + 1)
                    plain(sp)
                    load_ctx(it * 2 + u + 2, u)
                    sp.wait_ge(S["x1"], it * 2 + u + 1)
                    plain(sp)
                    store_stream(0, it * 2 + u)
            for b in (B - 2, B - 1):
                sp.wait_ge(S["x1"], b + 1)
                plain(sp)
                store_stream(0, b)

            def load_tokens(k, s, u):
                sp.dma_start(xtok[u][:].rearrange("p g d -> p (g d)"), at(slots[k], s)).then_inc(F[k][f"x_in{u}"], 16)

            def load_slots(k):
                for u in range(2):
                    sp.wait_ge(R[k][f"put{u}"], 16 * (B // 2) * (1 + k))
                for u in range(2):
                    load_tokens(k, u, u)

            def load_slots_rest(k):
                with sp.Fori(1, NE // 2) as it:
                    for u in range(2):
                        sp.wait_ge(F[k]["down"], it * 2 + (u - 1))
                        plain(sp)
                        load_expert(k, it * 2 + u, u)
                        sp.wait_ge(F[k]["y_sb"], it * 2 + (u - 1))
                        plain(sp)
                        sp.wait_ge(F[k][f"added{u}"], it * 32)
                        plain(sp)
                        load_tokens(k, it * 2 + u, u)

            load_slots(0)
            sp.wait_ge(S["table_set"], 1)
            n_over = sp.value_load(table[0:1, 3, 0:1], min_val=0, max_val=N_OVER)
            with sp.If(n_over > 0):
                for e in range(NE):
                    row = sp.value_load(table[0:1, 2, e:e + 1], min_val=0, max_val=NE * STRIDE - CAP)
                    sp.dma_start(tok_rows[0][bass.ds(row, CAP), :].rearrange("(p g) d -> p (g d)", g=2), blank).then_inc(S["refilled"], 16)
            load_slots_rest(0)
            for j in range(N_OVER):
                u, s = j % 2, NE + j
                with sp.If(n_over > j):
                    e = sp.value_load(table[0:1, 0, j:j + 1], min_val=0, max_val=NE - 1)
                    row = sp.value_load(table[0:1, 1, j:j + 1], min_val=0, max_val=NE * STRIDE - CAP)
                    if j == 0:
                        sp.wait_ge(S["refilled"], 16 * NE)
                    sp.wait_ge(F[0]["down"], s - 1)
                    load_expert(0, e, u)
                    sp.wait_ge(F[0]["y_sb"], s - 1)
                    sp.wait_ge(F[0][f"added{u}"], 32 * (s // 2))
                    sp.dma_start(xtok[u][:].rearrange("p g d -> p (g d)"),
                                 tok_rows[0][bass.ds(row, CAP), :].rearrange("(p g) d -> p (g d)", g=2)).then_inc(F[0][f"x_in{u}"], 16)
            for u in range(2):
                sp.wait_ge(F[0][f"added{u}"], 32 * (NE // 2))
            for j in range(N_OVER):
                with sp.If(n_over > j):
                    sp.wait_ge(F[0][f"added{j % 2}"], 32 * ((NE + j) // 2 + 1))
            for n, (a, b) in enumerate(((0, 1), (1, B))):
                sp.dma_start(x[:, a:b], acc[0][a * T:b * T, :].rearrange("(b t) d -> t b d", t=T)).then_inc(S[f"x2_in{n}"], 16)
            sp.wait_ge(S["layer0_done"], 1)
            for u in range(2):
                load_expert(1, u, u)
            with sp.Fori(0, B) as b:
                sp.wait_ge(S["x3"], b + 1)
                plain(sp)
                store_stream(1, b)
            load_slots(1)
            load_slots_rest(1)
            for u in range(2):
                sp.wait_ge(F[1][f"added{u}"], 32 * (NE // 2))
            sp.dma_start(out.rearrange("b t d -> (b t) d"), acc[1][0:B * T, :]).then_inc(S["out_done"], 16)
            sp.wait_ge(S["out_done"], 16)

        @block.gpsimd
        def _(pool):
            n = [0]

            def step(ins):
                n[0] += 1
                ins.then_inc(S["consts_step"], 1)
                pool.wait_ge(S["consts_step"], n[0])

            step(pool.memset(ident[:], 0.0))
            pool.affine_select(out=ident[:], in_=ident[:], compare_op=ALU.not_equal, fill=1.0, base=0,
                               pattern=[[-1, P]], channel_multiplier=1).then_inc(S["ident_made"], 1)
            for k in range(2):
                pool.dma_start(b_attn[:, k, :], A[("L0_xattn_b", "L1_xattn_bo")[k]].partition_broadcast(T)).then_inc(S["bcast_in"], 16)
                pool.dma_start(gate_w[:, k], A[("L0_ffn_switch_w", "L1_ffn_gate_w")[k]].rearrange("(c p) e -> p c e", p=P)).then_inc(S["bcast_in"], 16)
                pool.dma_start(gate_b[:, k, :], A[("L0_ffn_switch_b", "L1_ffn_gate_b")[k]].partition_broadcast(T)).then_inc(S["bcast_in"], 16)
            pool.dma_start(bv[:], A["L1_xattn_bv"].partition_broadcast(KP)).then_inc(S["bcast_in"], 16)
            pool.dma_start(lens_i[:], A["_lenS2"].partition_broadcast(T)).then_inc(S["bcast_in"], 16)
            pool.iota(kpos_i[:], pattern=[[1, KL]], base=0, channel_multiplier=0)
            pool.iota(qpos_i[:], pattern=[[0, 1]], base=0, channel_multiplier=1)
            pool.iota(eidx_i[:], pattern=[[1, NE]], base=0, channel_multiplier=0)
            pool.iota(pad_i[:], pattern=[[1, 2]], base=B * T, channel_multiplier=2)
            pool.iota(tokid_i[:], pattern=[[T, B]], base=0, channel_multiplier=1)
            pool.memset(ones[:], 1.0)
            pool.memset(neg_half[:], -0.5)
            step(pool.memset(headmask[:], 1.0))
            step(pool.affine_select(out=headmask[:], in_=headmask[:], compare_op=ALU.is_ge, fill=0.0, base=0,
                                    pattern=[[-HD, HPC]], channel_multiplier=1))
            step(pool.affine_select(out=headmask[:], in_=headmask[:], compare_op=ALU.is_ge, fill=0.0, base=HD - 1,
                                    pattern=[[HD, HPC]], channel_multiplier=-1))
            pool.affine_select(out=tri[:], in_=ones[:], compare_op=ALU.is_ge, fill=0.0, base=0,
                               pattern=[[1, T]], channel_multiplier=-1).then_inc(S["consts_made"], 1)

            def rsqrt(k, b):
                pool.wait_ge(LN[k]["var"], b + 1)
                plain(pool)
                pool.tensor_scalar(lvar[k][:], lmv[k][:, 1:2], EPS, None, ALU.add).then_inc(LN[k]["eps"], 1)
                pool.wait_ge(LN[k]["eps"], b + 1)
                pool.tensor_tensor(rstd[k][:], lvar[k][:], neg_half[:], ALU.pow).then_inc(LN[k]["rstd"], 1)

            def scatter(k, b, u):
                pool.wait_ge(R[k]["row"], b + 1)
                plain(pool)
                for c in range(k + 1):
                    pool.indirect_dma_start(
                        out=tok_rows[k], out_offset=bass.IndirectOffsetOnAxis(ap=pos[c][u][:].bitcast(u32), axis=0),
                        in_=xrow[c][u][:], in_offset=None).then_inc(R[k][f"put{u}"], 16)

            def add_results(k, s, u):
                pool.wait_ge(F[k]["y_sb"], s + 1)
                plain(pool)
                for g in range(2):
                    pool.indirect_dma_start(
                        out=acc[k], out_offset=bass.IndirectOffsetOnAxis(ap=sid[u][:, g:g + 1], axis=0),
                        in_=ytok[u][:, g, :], in_offset=None, compute_op=ALU.add).then_inc(F[k][f"added{u}"], 16)

            def added(k, u, it):
                pool.wait_ge(F[k][f"added{u}"], 32 * (it + 1))

            for b, u, it, late, early in batches(pool):
                rsqrt(0, b)
                if not late:
                    pool.wait_ge(S["emptied"], 16 * 2 * (NE + 1))
                if late:
                    rsqrt(1, b - 1)
                    scatter(0, b - 1, 1 - u)
            rsqrt(1, B - 1)
            scatter(0, B - 1, 1)
            pool.wait_ge(R[0]["saved"], 16 * B)
            for s, u, it in pairs(pool):
                add_results(0, s, u)
                added(0, u, it)
            pool.wait_ge(S["table_set"], 1)
            n_over = pool.value_load(table[0:1, 3, 0:1], min_val=0, max_val=N_OVER)
            for j in range(N_OVER):
                with pool.If(n_over > j):
                    add_results(0, NE + j, j % 2)
                    added(0, j % 2, (NE + j) // 2)
            pool.wait_ge(S["v_sb"], 2 * B)
            pool.wait_ge(S["vpad_made"], 1)

            def head_operands(b, u):
                pool.tensor_copy(vpad[u][:, :, :, 0:HD],
                                 vals[:, bass.ds(b * KT, KT), :].rearrange("p j (h d) -> p j h d", d=HD)).then_inc(S["vp"], 1)
                pool.wait_ge(S["q_sb"], DC * b + DC)
                for c in range(DC):
                    pool.tensor_tensor(qmask[u][:, c], qT[u][:, c].unsqueeze(1).to_broadcast([P, HPC, T]),
                                       headmask[:].unsqueeze(2).to_broadcast([P, HPC, T]), ALU.mult).then_inc(S["qm"], 1)

            rsqrt(2, 0)
            head_operands(0, 0)
            for b, u, it, late, early in batches(pool):
                if early:
                    rsqrt(2, b + 1)
                if late:
                    rsqrt(3, b - 1)
                if early:
                    pool.wait_ge(S["q_sb"], DC * b + 2 * DC)
                    head_operands(b + 1, 1 - u)
                if late:
                    scatter(1, b - 1, 1 - u)
            rsqrt(3, B - 1)
            scatter(1, B - 1, 1)
            pool.wait_ge(R[1]["saved"], 16 * B)
            for s, u, it in pairs(pool):
                add_results(1, s, u)
                added(1, u, it)

        @block.tensor
        def _(pe):
            mm, tr = nc.tensor.matmul, nc.tensor.transpose

            def turn(bank_out, src):
                for c in range(DC):
                    last = tr(bank_out[:, c * T:(c + 1) * T], src[:, c * P:(c + 1) * P], ident[0:T, 0:T])
                return last

            pe.wait_ge(S["ident_made"], 1)

            def gate_turn(k, b, u, dst):
                pe.wait_ge(LN[1 + 2 * k]["xn"], b + 1)
                turn(dst, xrow[0][u]).then_inc(R[k]["xT_ps"], 1)

            def gate_logits(k, b):
                pe.wait_ge(R[k]["xT_sb"], b + 1)
                for c in range(DC):
                    last = mm(bank[3][0:T, GATE:GATE + NE], xgT[:, c, :], gate_w[:, k, c, :], start=(c == 0), stop=(c == 1))
                last.then_inc(R[k]["g_ps"], 1)

            def gate_ranks(k, b):
                pe.wait_ge(R[k]["hot"], b + 1)
                mm(bank[3][0:T, RANK:RANK + NE], tri[:], hot16[:], start=True, stop=False)
                mm(bank[3][0:T, RANK:RANK + NE], ones[:], seen16[k][:], start=False, stop=True).then_inc(R[k]["rank"], 1)

            def weights():
                pe.wait_ge(S["weights_in"], 16 * 5)
                for n in range(5):
                    if n >= 2:
                        pe.wait_ge(S["w_sb"], n - 1)
                    for c in range(DC):
                        for o in range(DC):
                            last = tr(bank[6 + n % 2][:, c * D + o * P:c * D + (o + 1) * P], raw[:, n, o, c * P:(c + 1) * P], ident[:])
                    last.then_inc(S["w_ps"], 1)
                pe.wait_ge(S["biases_in"], 16 * 6)
                tr(bank[5][:, 0:P], bias_rows[:], ident[:])
                tr(bank[5][:, P:P + 36], bias_rows2[:], ident[0:36, 0:36]).then_inc(S["bias_ps"], 1)
                pe.wait_ge(S["w_sb"], 5)
                pe.wait_ge(S["bias_sb"], 1)

            for b, u, it, late, early in batches(pe):
                pe.wait_ge(S[f"ctx_in{u}"], 16 * (it + 1))
                for c in range(DC):
                    for j in range(KT):
                        last = tr(bank[c][:, j * KP:(j + 1) * KP], ctx[u][:, j, c * P:(c + 1) * P], ident[0:KP, 0:KP])
                last.then_inc(S["ctxT_ps"], 1)
                pe.wait_ge(LN[0]["xn"], b + 1)
                turn(bank[2], xa[u]).then_inc(S["xT_ps"], 1)
                pe.wait_ge(S["ctxT_act"], b + 1)
                pe.wait_ge(S["ctxT_dve"], b + 1)
                pe.wait_ge(S["xT_sb"], b + 1)
                for c in range(DC):
                    last = mm(bank[3][0:T, 0:KL], xT[u][:, c, :], ctxT[u][:, c, :], start=(c == 0), stop=(c == 1))
                last.then_inc(S["s_ps"], 1)
                if late:
                    pe.wait_ge(S["k_sb"], 2 * b)
                else:
                    weights()
                for o in range(DC):
                    for c in range(DC):
                        last = mm(bank[4 + o][:, 0:KL], wT[:, WK, c, o * P:(o + 1) * P], ctxT[u][:, c, :],
                                  start=(c == 0), stop=(c == 1))
                    last.then_inc(S["k_ps"], 1)
                    if late and o == 0:
                        gate_turn(0, b - 1, 1 - u, bank[2][:, D:2 * D])
                if late:
                    pe.wait_ge(S["s_masked"], b + 1)
                    gate_logits(0, b - 1)
                pe.wait_ge(S["s_exp"], b + 1)
                for j in range(KT):
                    last = tr(bank[0][0:KP, j * T:(j + 1) * T], probs[u][:, j * KP:(j + 1) * KP], ident[0:T, 0:T])
                last.then_inc(S["pT_ps"], 1)
                if late:
                    pe.wait_ge(S["v_sb"], 2 * b)
                    pe.wait_ge(S["x1"], b)

                def values(j):
                    for c in range(DC):
                        last = mm(bank[6 + j // 2][0:KP, (j % 2) * D:(j % 2 + 1) * D], ctxT[u][:, c, j * KP:(j + 1) * KP],
                                  wT[:, WV, c, :], start=(c == 0), stop=(c == 1))
                    return last

                values(0)
                values(1).then_inc(S["v_ps"], 1)
                if late:
                    gate_ranks(0, b - 1)
                pe.wait_ge(S["pT_sb"], b + 1)
                for c in range(DC):
                    for j in range(KT):
                        last = mm(bank[1][:, c * T:(c + 1) * T], ctx[u][:, j, c * P:(c + 1) * P],
                                  probsT[0][:, j * T:(j + 1) * T], start=(j == 0), stop=(j == KT - 1))
                last.then_inc(S["o_ps"], 1)
                values(2).then_inc(S["v_ps"], 1)
                pe.wait_ge(S["o_sb"], b + 1)
                pe.wait_ge(S["v_sb"], 2 * b + 2)
                for c in range(DC):
                    last = mm(bank[7][0:T, D:2 * D], oT[:, c, :], wT[:, W0, c, :], start=(c == 0), stop=(c == 1))
                last.then_inc(S["y_ps"], 1)
                if late:
                    pe.wait_ge(R[0]["seen"], b)
            gate_turn(0, B - 1, 1, bank[2][:, D:2 * D])
            gate_logits(0, B - 1)
            gate_ranks(0, B - 1)
            pe.wait_ge(R[0]["seen"], B)
            mm(bank[3][0:T, RANK:RANK + NE], ones[:], seen16[0][:], start=True, stop=True).then_inc(R[0]["rank"], 1)

            def slot_tokens(k, s, u, it):
                pe.wait_ge(F[k][f"x_in{u}"], 16 * (it + 1))
                for c in range(DC):
                    for g in range(2):
                        last = tr(bank[0][:, c * CAP + g * HC:c * CAP + (g + 1) * HC], xtok[u][:, g, c * P:(c + 1) * P],
                                  ident[0:HC, 0:HC])
                last.then_inc(F[k]["xT_ps"], 1)

            def slot_expert(k, s, u, it):
                pe.wait_ge(F[k][f"w1_in{u}"], 16 * (it + 1))
                pe.wait_ge(F[k]["xT_sb"], s + 1)
                for q in range(FC // 2):
                    for r in range(2):
                        f = 2 * q + r
                        for c in range(DC):
                            last = mm(bank[1 + q][:, r * CAP:(r + 1) * CAP], w1[u][:, c, f * P:(f + 1) * P], xsT[u][:, c, :],
                                      start=(c == 0), stop=(c == 1))
                    last.then_inc(F[k]["up"], 1)
                pe.wait_ge(F[k][f"w2_in{u}"], 16 * (it + 1))
                for d in range(DC):
                    for f in range(FC):
                        if d == 0 and f % 2 == 0:
                            pe.wait_ge(F[k]["h"], s * 4 + f // 2 + 1)
                        last = mm(bank[5][:, d * CAP:(d + 1) * CAP], w2[u][:, f, d * P:(d + 1) * P], hT[:, f, :],
                                  start=(f == 0), stop=(f == FC - 1))
                last.then_inc(F[k]["down"], 1)

            def slot_results(k, s, u):
                pe.wait_ge(F[k]["yT"], s + 1)
                for g in range(2):
                    for c in range(DC):
                        last = tr(bank[6 + u][0:HC, g * D + c * P:g * D + (c + 1) * P], yT[:, c, g * HC:(g + 1) * HC], ident[:])
                last.then_inc(F[k]["y_ps"], 1)

            def experts(k):
                slot_tokens(k, 0, 0, 0)
                with pe.Fori(0, NE // 2 - 1) as it:
                    for u in range(2):
                        slot_expert(k, it * 2 + u, u, it)
                        slot_tokens(k, it * 2 + u + 1, 1 - u, it + u)
                        slot_results(k, it * 2 + u, u)
                slot_expert(k, NE - 2, 0, NE // 2 - 1)
                slot_tokens(k, NE - 1, 1, NE // 2 - 1)
                slot_results(k, NE - 2, 0)
                slot_expert(k, NE - 1, 1, NE // 2 - 1)
                slot_results(k, NE - 1, 1)

            experts(0)
            pe.wait_ge(S["table_set"], 1)
            n_over = pe.value_load(table[0:1, 3, 0:1], min_val=0, max_val=N_OVER)
            for j in range(N_OVER):
                with pe.If(n_over > j):
                    s = NE + j
                    slot_tokens(0, s, j % 2, s // 2)
                    slot_expert(0, s, j % 2, s // 2)
                    slot_results(0, s, j % 2)
            pe.drain().then_inc(S["layer0_done"], 1)

            def query_turn(b, u):
                pe.wait_ge(LN[2]["xn"], b + 1)
                if not isinstance(b, int):
                    pe.wait_ge(S["ranks_read"], b - 1)
                turn(bank[3], xa[u]).then_inc(S["q_xT"], 1)

            def query_project(b, u):
                pe.wait_ge(S["q_xTs"], b + 1)
                for o in range(DC):
                    for c in range(DC):
                        last = mm(bank[3][:, D + o * T:D + (o + 1) * T], wT[:, WQ, c, o * P:(o + 1) * P], xT[u][:, c, :],
                                  start=(c == 0), stop=(c == 1))
                last.then_inc(S["q_ps"], 1)

            def head_scores(b, u, h):
                if h % HPC == 0:
                    pe.wait_ge(S["qm"], b * DC + h // HPC + 1)
                mm(bank[h % 3][0:T, 0:KL], qmask[u][:, h // HPC, h % HPC, :],
                   kT[:, h // HPC, bass.ds(b * KL, KL)], start=True, stop=True).then_inc(S["h_s"], 1)

            def head_transpose(b, h):
                pe.wait_ge(S["h_exp"], b * NH + h + 1)
                for j in range(KT):
                    last = tr(bank[4 + h % 2][0:KP, j * T:(j + 1) * T], probs[h % 4][:, j * KP:(j + 1) * KP], ident[0:T, 0:T])
                last.then_inc(S["h_pT"], 1)

            def head_product(b, u, h, late):
                if h == 0:
                    pe.wait_ge(S["vp"], b + 1)
                    if late:
                        pe.wait_ge(S["h_out"], b)
                pe.wait_ge(S["h_pTa" if h % 2 == 0 else "h_pTd"], b * (NH // 2) + h // 2 + 1)
                r = HW * (h % 4)
                for j in range(KT):
                    last = mm(bank[6][r:r + HW, (h // 4) * T:(h // 4 + 1) * T], vpad[u][:, j, h, :],
                              probsT[h % 4][:, j * T:(j + 1) * T], start=(j == 0), stop=(j == KT - 1))
                last.then_inc(S["h_av"], 1)

            def out_tokens(b, u):
                pe.wait_ge(S["h_out"], b + 1)
                for q in range(4):
                    last = tr(bank[7][0:T, q * P:(q + 1) * P], outT[:, q, :], ident[:])
                last.then_inc(S["h_outT"], 1)

            def out_turn(b, u):
                pe.wait_ge(S["h_o"], b + 1)
                turn(bank[7], oa).then_inc(S["e_oT"], 1)

            def out_project(b, u):
                pe.wait_ge(S["e_oTs"], b + 1)
                for c in range(DC):
                    last = mm(bank[7][0:T, D:2 * D], oT[:, c, :], wT[:, WO, c, :], start=(c == 0), stop=(c == 1))
                last.then_inc(S["e_y"], 1)

            before_steps = {3: out_tokens, 5: out_turn, 7: out_project,
                            12: lambda b, u: gate_turn(1, b, u, bank[7][:, 0:D]),
                            14: lambda b, u: gate_logits(1, b), 17: lambda b, u: gate_ranks(1, b)}
            after_steps = {6: query_turn, 9: query_project}
            query_turn(0, 0)
            query_project(0, 0)
            for b, u, it, late, early in batches(pe):
                for i in range(NH + 3):
                    if i < NH:
                        head_scores(b, u, i)
                    if 2 <= i < NH + 2:
                        head_transpose(b, i - 2)
                    if i >= 3:
                        head_product(b, u, i - 3, late)
                    if late and early and i == 14:
                        pe.wait_ge(S["q_sb"], DC * b + 2 * DC)
                    if late and i in before_steps:
                        before_steps[i](b - 1, 1 - u)
                    if early and i in after_steps:
                        after_steps[i](b + 1, 1 - u)
            for i in sorted(before_steps):
                before_steps[i](B - 1, 1)
            experts(1)

        @block.scalar
        def _(act):
            def copy(dst, src):
                return nc.scalar.activation(dst, src, ACT.Copy)

            def col(i):
                return biasT[:, i:i + 1] if isinstance(i, int) else biasT[:, bass.ds(i, 1)]

            def chances(k, b, u):
                act.wait_ge(R[k]["best"], b + 1)
                src, n = ((logit, NE), (top8, 2))[k]
                nc.scalar.activation(wexp[:, 0:n], src[:, 0:n], ACT.Exp, bias=topn[:], accum_out=wsum[:]).then_inc(R[k]["wexp"], 1)

            for b, u, it, late, early in batches(act):
                act.wait_ge(S["ctxT_ps"], b + 1)
                copy(ctxT[u][:, 0, :], bank[0][:, 0:KL]).then_inc(S["ctxT_act"], 1)
                if not late:
                    for n in range(5):
                        act.wait_ge(S["w_ps"], n + 1)
                        copy(wT[:, n].rearrange("p c d -> p (c d)"), bank[6 + n % 2][:]).then_inc(S["w_sb"], 1)
                    act.wait_ge(S["bias_ps"], 1)
                    copy(biasT[:], bank[5][:, 0:P + 36]).then_inc(S["bias_sb"], 1)
                    act.wait_ge(S["bias_sb"], 1)
                act.wait_ge(S["s_max"], b + 1)
                nc.scalar.activation(probs[u][:], scores[:], ACT.Exp, bias=rowmax[u][:], scale=1.0 / 16,
                                     accum_out=esum[u][:]).then_inc(S["s_exp"], 1)
                for o in range(DC):
                    act.wait_ge(S["k_ps"], b * 2 + o + 1)
                    nc.scalar.activation(kT[:, o, bass.ds(b * KL, KL)], bank[4 + o][:, 0:KL], ACT.Identity,
                                         bias=biasT[:, P + 34 + o:P + 35 + o]).then_inc(S["k_sb"], 1)
                act.wait_ge(S["pT_ps"], b + 1)
                copy(probsT[0][:], bank[0][0:KP, 0:KT * T]).then_inc(S["pT_sb"], 1)
                if late:
                    chances(0, b - 1, 1 - u)
                act.wait_ge(S["o_ps"], b + 1)
                copy(oT[:].rearrange("p c t -> p (c t)"), bank[1][:, 0:DC * T]).then_inc(S["o_sb"], 1)
            chances(0, B - 1, 1)

            def slot(k, s, e):
                func = (ACT.Gelu_apprx_tanh, ACT.Relu)[k]
                for q in range(FC // 2):
                    act.wait_ge(F[k]["up"], s * 4 + q + 1)
                    for r in range(2):
                        f = 2 * q + r
                        last = nc.scalar.activation(hT[:, f, :], bank[1 + q][:, r * CAP:(r + 1) * CAP], func,
                                                    bias=col(64 * k + e * FC + f))
                    last.then_inc(F[k]["h"], 1)
                act.wait_ge(F[k]["down"], s + 1)
                for d in range(DC):
                    last = nc.scalar.activation(yT[:, d, :], bank[5][:, d * CAP:(d + 1) * CAP], ACT.Identity,
                                                bias=col(P + 16 * k + e * DC + d))
                last.then_inc(F[k]["yT"], 1)

            for s, u, it in pairs(act):
                slot(0, s, s)
            act.wait_ge(S["table_set"], 1)
            n_over = act.value_load(table[0:1, 3, 0:1], min_val=0, max_val=N_OVER)
            for j in range(N_OVER):
                with act.If(n_over > j):
                    slot(0, NE + j, act.value_load(table[0:1, 0, j:j + 1], min_val=0, max_val=NE - 1))

            def second_row(b, u):
                act.wait_ge(LN[3]["xn"], b + 1)
                copy(xrow[1][u][:, 0:D], xrow[0][u][:, 0:D]).then_inc(R[1]["row2"], 1)

            before_steps = {11: second_row, 15: lambda b, u: chances(1, b, u)}
            for b, u, it, late, early in batches(act):
                for i in range(NH + 2):
                    if i < NH:
                        act.wait_ge(S["h_max"], b * NH + i + 1)
                        nc.scalar.activation(probs[i % 4][:], bank[i % 3][0:T, 0:KL], ACT.Exp,
                                             bias=nmax[u][:, i:i + 1]).then_inc(S["h_exp"], 1)
                    if i >= 2 and i % 2 == 0:
                        act.wait_ge(S["h_pT"], b * NH + i - 1)
                        copy(probsT[(i - 2) % 4][:], bank[4][0:KP, 0:KT * T]).then_inc(S["h_pTa"], 1)
                    if late and i in before_steps:
                        before_steps[i](b - 1, 1 - u)
                act.wait_ge(S["h_av"], b * NH + NH)
                copy(outT[:].rearrange("p q t -> p (q t)"), bank[6][:, 0:4 * T]).then_inc(S["h_out"], 1)
            for i in sorted(before_steps):
                before_steps[i](B - 1, 1)
            for s, u, it in pairs(act):
                slot(1, s, s)

        @block.vector
        def _(dve):
            v = nc.vector
            done = [0]

            def link(ins):
                done[0] += 1
                ins.then_inc(S["chain"], 1)
                dve.wait_ge(S["chain"], done[0])

            def flat(ap):
                return ap.rearrange("p c t -> p (c t)")

            def moments(k, b):
                plain(dve)
                v.bn_stats(lstat[k][:], at(x, b)).then_inc(LN[k]["stats"], 1)
                dve.wait_ge(LN[k]["stats"], b + 1)
                plain(dve)
                v.bn_aggr(lmv[k][:], lstat[k][:]).then_inc(LN[k]["var"], 1)

            def normalise(k, b, dst):
                dve.wait_ge(LN[k]["rstd"], b + 1)
                v.tensor_scalar(dst, at(x, b), lmv[k][:, 0:1], rstd[k][:], ALU.subtract, ALU.mult).then_inc(LN[k]["xn"], 1)

            def gate_norm(k, b, u, it):
                if not (isinstance(it, int) and it == 0):
                    dve.wait_ge(R[k][f"put{u}"], it * 16 * (k + 1))
                normalise(1 + 2 * k, b, xrow[0][u][:, 0:D])

            def gate_turn(k, b, u, src):
                dve.wait_ge(R[k]["xT_ps"], b + 1)
                v.tensor_copy(flat(xgT[:]), src).then_inc(R[k]["xT_sb"], 1)

            def gate_choose(k, b, u):
                n = [0]

                def hop(ins):
                    n[0] += 1
                    ins.then_inc(R[k]["step"], 1)
                    dve.wait_ge(R[k]["step"], b * HOPS[k] + n[0])
                    plain(dve)

                dve.wait_ge(R[k]["g_ps"], b + 1)
                hop(v.tensor_tensor(logit[:], bank[3][0:T, GATE:GATE + NE], gate_b[:, k, :], ALU.add))
                hop(v.max(top8[:], logit[:]))
                v.tensor_scalar(topn[:], top8[:, 0:1], -1.0, None, ALU.mult).then_inc(R[k]["best"], 1)
                hop(v.max_index(topi[:], top8[:], logit[:]))
                hop(v.tensor_copy(topf[:], topi[:, 0:2]))
                for c in range(k + 1):
                    hop(v.tensor_scalar(hot[:, c], eidx[:], topf[:, c:c + 1], None, ALU.is_equal))
                if k == 0:
                    v.tensor_copy(hot16[:], hot[:, 0]).then_inc(R[k]["hot"], 1)
                else:
                    v.tensor_tensor(hot16[:], hot[:, 0], hot[:, 1], ALU.add).then_inc(R[k]["hot"], 1)
                return n[0]

            def gate_place(k, b, u, n0):
                n = [n0]

                def hop(ins):
                    n[0] += 1
                    ins.then_inc(R[k]["step"], 1)
                    dve.wait_ge(R[k]["step"], b * HOPS[k] + n[0])

                v.tensor_copy(xrow[0][u][:, D:D + 1], tokid[:, bass.ds(b, 1)])
                if k == 1:
                    v.tensor_copy(xrow[1][u][:, D:D + 1], tokid[:, bass.ds(b, 1)])
                dve.wait_ge(R[k]["wexp"], b + 1)
                hop(v.reciprocal(rb[:, 0:1], wsum[:]))
                if k == 0:
                    v.tensor_copy(xrow[0][u][:, D + 1:D + 2], rb[:, 0:1])
                else:
                    for c in range(2):
                        v.tensor_tensor(xrow[c][u][:, D + 1:D + 2], wexp[:, c:c + 1], rb[:, 0:1], ALU.mult)
                dve.wait_ge(R[k]["rank"], b + 1)
                for c in range(k + 1):
                    hop(v.scalar_tensor_tensor(rt[:], hot[:, c], 1.0, bank[3][0:T, RANK:RANK + NE], ALU.mult, ALU.mult,
                                               accum_out=rs[:, c:c + 1]))
                dve.wait_ge(R[k]["hot"], b + 1)
                hop(v.tensor_tensor(seen[k][:], seen[k][:], hot16[:], ALU.add))
                v.tensor_copy(seen16[k][:], seen[k][:]).then_inc(R[k]["seen"], 1)
                if k == 1:
                    dve.sem_inc(S["ranks_read"], 1)
                if k == 0:
                    hop(v.scalar_tensor_tensor(ra[:, 0:1], topf[:, 0:1], float(STRIDE), rs[:, 0:1], ALU.mult, ALU.add))
                    v.tensor_scalar(pos[0][u][:], ra[:, 0:1], -1.0, None, ALU.add).then_inc(R[k]["row"], 1)
                else:
                    aside = bass.ds(b, 1)
                    hop(v.tensor_scalar(keep[:], rs[:], float(CAP), None, ALU.is_le))
                    hop(v.scalar_tensor_tensor(ra[:], topf[:], float(CAP), rs[:], ALU.mult, ALU.add))
                    hop(v.tensor_tensor(ra[:], ra[:], at(trash, b), ALU.subtract))
                    hop(v.tensor_tensor(ra[:], ra[:], keep[:], ALU.mult))
                    hop(v.tensor_tensor(ra[:], ra[:], at(trash, b), ALU.add))
                    dve.wait_ge(R[k]["row2"], b + 1)
                    v.tensor_scalar(pos[0][u][:], ra[:, 0:1], -1.0, None, ALU.add)
                    v.tensor_scalar(pos[1][u][:], ra[:, 1:2], -1.0, None, ALU.add).then_inc(R[k]["row"], 1)
                assert n[0] == HOPS[k], n

            link(v.memset(empty[:], 0.0))
            dve.sem_inc(S["ranks_read"], 1)
            dve.wait_ge(S["consts_made"], 1)
            v.tensor_copy(empty[:, :, D], pad_i[:]).then_inc(S["empty_made"], 1)
            for k in range(2):
                v.memset(seen[k][:], 0.0)
                v.memset(seen16[k][:], 0.0)
                for u in range(2):
                    v.memset(xrow[k][u][:, D:RW], 0.0)
            for a, i in ((kpos, kpos_i), (qpos, qpos_i), (eidx, eidx_i), (tokid, tokid_i)):
                link(v.tensor_copy(a[:], i[:]))
            for c in range(2):
                link(v.tensor_scalar(trash[:, :, c], tokid[:], float(NE * CAP + c * B * T + 1), None, ALU.add))
            dve.wait_ge(S["bcast_in"], 16 * 8)
            link(v.tensor_copy(lens[:], lens_i[:]))
            link(v.tensor_tensor(qflag[:], qpos[:].to_broadcast([T, B]), lens[:], ALU.is_ge))
            dve.wait_ge(S["x_in"], 16)
            moments(0, 0)
            for u in range(2):
                link(v.memset(vpad[u][:], 0.0))
                last = v.memset(vpad[u][:, :, :, HD:HD + 1], 1.0)
            last.then_inc(S["vpad_made"], 1)

            for b, u, it, late, early in batches(dve):
                normalise(0, b, xa[u][:])
                dve.wait_ge(LN[0]["xn"], b + 1)
                v.tensor_tensor(at(x, b), at(x, b), b_attn[:, 0, :], ALU.add).then_inc(S["xb"], 1)
                v.tensor_scalar(kmask[:], kpos[:], lens[:, bass.ds(b, 1)], BIG, ALU.is_ge, ALU.mult).then_inc(S["kmask_set"], 1)
                dve.wait_ge(S["ctxT_ps"], b + 1)
                v.tensor_copy(ctxT[u][:, 1, :], bank[1][:, 0:KL]).then_inc(S["ctxT_dve"], 1)
                dve.wait_ge(S["xT_ps"], b + 1)
                v.tensor_copy(flat(xT[u][:]), bank[2][:, 0:DC * T]).then_inc(S["xT_sb"], 1)
                if late:
                    pu, pit = before(u, it)
                    gate_norm(0, b - 1, pu, pit)
                dve.wait_ge(S["s_ps"], b + 1)
                dve.wait_ge(S["kmask_set"], b + 1)
                v.scalar_tensor_tensor(scores[:], kmask[:], qflag[:, bass.ds(b, 1)], bank[3][0:T, 0:KL], ALU.mult,
                                       ALU.add).then_inc(S["s_masked"], 1)
                dve.wait_ge(S["s_masked"], b + 1)
                v.tensor_reduce(rowmax[u][:], scores[:], axis=AX.X, op=ALU.max, negate=True).then_inc(S["s_rowmax"], 1)
                dve.wait_ge(S["s_rowmax"], b + 1)
                v.tensor_scalar(rowmax[u][:], rowmax[u][:], 1.0 / 16, None, ALU.mult).then_inc(S["s_max"], 1)
                if late:
                    gate_turn(0, b - 1, 1 - u, bank[2][:, D:D + DC * T])
                    n0 = gate_choose(0, b - 1, 1 - u)
                dve.wait_ge(S["s_exp"], b + 1)
                v.reciprocal(esinv[:], esum[u][:]).then_inc(S["esum_inv"], 1)
                dve.wait_ge(S["v_ps"], b * 2 + 1)
                v.tensor_tensor(vals[:, bass.ds(b * KT, 2), :], bank[6][0:KP, :].rearrange("p (j d) -> p j d", d=D),
                                bv[:].unsqueeze(1).to_broadcast([KP, 2, D]), ALU.add).then_inc(S["v_sb"], 1)
                if late:
                    gate_place(0, b - 1, 1 - u, n0)
                dve.wait_ge(S["v_ps"], b * 2 + 2)
                v.tensor_tensor(at(vals, b * KT + 2), bank[7][0:KP, 0:D], bv[:], ALU.add).then_inc(S["v_sb"], 1)
                if early:
                    moments(0, b + 1)
                dve.wait_ge(S["y_ps"], b + 1)
                dve.wait_ge(S["xb"], b + 1)
                dve.wait_ge(S["esum_inv"], b + 1)
                v.scalar_tensor_tensor(at(x, b), bank[7][0:T, D:2 * D], esinv[:], at(x, b), ALU.mult, ALU.add).then_inc(S["x1"], 1)
                dve.wait_ge(S["x1"], b + 1)
                moments(1, b)
            gate_norm(0, B - 1, 1, B // 2 - 1)
            gate_turn(0, B - 1, 1, bank[2][:, D:D + DC * T])
            gate_place(0, B - 1, 1, gate_choose(0, B - 1, 1))

            dve.wait_ge(R[0]["rank"], B + 1)
            link(v.tensor_copy(total[:], bank[3][0:T, RANK:RANK + NE]))
            link(v.memset(ofl[:], 0.0))
            link(v.tensor_scalar(ocum[:, 0], total[:], float(CAP), None, ALU.is_gt))
            for j in range(2, N_OVER + 1):
                link(v.scalar_tensor_tensor(ocum[:, (j + 1) % 2], total[:], float(CAP * j), ocum[:, j % 2], ALU.is_gt, ALU.add))
            a, c = (N_OVER + 1) % 2, N_OVER % 2
            link(v.tensor_copy(ocum[:, 2], ocum[:, a]))
            for hop_by in (1, 2, 4):
                v.tensor_copy(ocum[:, c, 0:hop_by], ocum[:, a, 0:hop_by])
                link(v.tensor_tensor(ocum[:, c, hop_by:], ocum[:, a, hop_by:], ocum[:, a, 0:NE - hop_by], ALU.add))
                a, c = c, a
            link(v.tensor_tensor(oat[:], ocum[:, a].unsqueeze(1).to_broadcast([T, N_OVER, NE]),
                                 eidx[:, 0:N_OVER].unsqueeze(2).to_broadcast([T, N_OVER, NE]), ALU.is_le))
            link(v.tensor_reduce(ofl[:, 0, 0:N_OVER], oat[:], axis=AX.X, op=ALU.add))
            link(v.tensor_scalar(ofl[:, 0], ofl[:, 0], float(NE - 1), None, ALU.min))
            link(v.tensor_tensor(oat[:], oat[:], ocum[:, 2].unsqueeze(1).to_broadcast([T, N_OVER, NE]), ALU.mult))
            link(v.tensor_reduce(ofl[:, 1, 0:N_OVER], oat[:], axis=AX.X, op=ALU.add))
            link(v.tensor_tensor(ofl[:, 1], eidx[:], ofl[:, 1], ALU.subtract))
            link(v.tensor_scalar(ofl[:, 1], ofl[:, 1], 1.0, float(CAP), ALU.add, ALU.mult))
            link(v.scalar_tensor_tensor(ofl[:, 1], ofl[:, 0], float(STRIDE), ofl[:, 1], ALU.mult, ALU.add))
            link(v.tensor_scalar(ofl[:, 1], ofl[:, 1], float(NE * STRIDE - CAP), None, ALU.min))
            link(v.tensor_scalar(ofl[:, 2], total[:], float(CAP), None, ALU.max))
            link(v.scalar_tensor_tensor(ofl[:, 2], eidx[:], float(STRIDE), ofl[:, 2], ALU.mult, ALU.add))
            link(v.tensor_copy(ofl[:, 3, 0:1], ocum[:, a, NE - 1:NE]))
            v.tensor_copy(table[:], ofl[:]).then_inc(S["table_set"], 1)

            def slot_tokens(k, s, u):
                dve.wait_ge(F[k]["xT_ps"], s + 1)
                v.tensor_copy(flat(xsT[u][:]), bank[0][:, 0:DC * CAP]).then_inc(F[k]["xT_sb"], 1)

            def slot_results(k, s, u, it):
                if not (isinstance(it, int) and it == 0):
                    dve.wait_ge(F[k][f"added{u}"], it * 32)
                v.tensor_copy(sid[u][:], xtok[u][:, :, D]).then_inc(F[k]["id"], 1)
                dve.wait_ge(F[k]["y_ps"], s + 1)
                for g in range(2):
                    last = v.tensor_scalar(ytok[u][:, g, :], bank[6 + u][0:HC, g * D:(g + 1) * D],
                                           xtok[u][:, g, D + 1:D + 2], None, ALU.mult)
                last.then_inc(F[k]["y_sb"], 1)

            def experts(k):
                slot_tokens(k, 0, 0)
                for u in range(2):
                    slot_tokens(k, u + 1, 1 - u)
                    slot_results(k, u, u, 0)
                with dve.Fori(1, NE // 2 - 1) as it:
                    for u in range(2):
                        slot_tokens(k, it * 2 + u + 1, 1 - u)
                        slot_results(k, it * 2 + u, u, it)
                slot_tokens(k, NE - 1, 1)
                slot_results(k, NE - 2, 0, NE // 2 - 1)
                slot_results(k, NE - 1, 1, NE // 2 - 1)

            experts(0)
            n_over = dve.value_load(table[0:1, 3, 0:1], min_val=0, max_val=N_OVER)
            for j in range(N_OVER):
                with dve.If(n_over > j):
                    slot_tokens(0, NE + j, j % 2)
                    slot_results(0, NE + j, j % 2, (NE + j) // 2)

            def query_norm(b, u):
                normalise(2, b, xa[u][:])

            def query_turn(b, u):
                dve.wait_ge(S["q_xT"], b + 1)
                v.tensor_copy(flat(xT[u][:]), bank[3][:, 0:DC * T]).then_inc(S["q_xTs"], 1)

            def query_scale(b, u):
                dve.wait_ge(S["q_ps"], b + 1)
                for o in range(DC):
                    v.tensor_scalar(qT[u][:, o], bank[3][:, D + o * T:D + (o + 1) * T], biasT[:, P + 32 + o:P + 33 + o],
                                    0.25, ALU.add, ALU.mult).then_inc(S["q_sb"], 1)
                v.tensor_tensor(at(x, b), at(x, b), b_attn[:, 1, :], ALU.add).then_inc(S["xo"], 1)

            def out_tokens(b, u, it):
                dve.wait_ge(S["h_outT"], b + 1)
                o = bank[7][0:T, :].rearrange("p (h w) -> p h w", w=HW)
                v.reciprocal(rinv[:].unsqueeze(2), o[:, :, HD:HD + 1]).then_inc(S["h_rinv"], 1)
                dve.wait_ge(S["h_rinv"], b + 1)
                v.tensor_tensor(oa[:].rearrange("p (h d) -> p h d", d=HD), o[:, :, 0:HD],
                                rinv[:].unsqueeze(2).to_broadcast([T, NH, HD]), ALU.mult).then_inc(S["h_o"], 1)

            def out_turn(b, u, it):
                dve.wait_ge(S["e_oT"], b + 1)
                v.tensor_copy(flat(oT[:]), bank[7][:, 0:DC * T]).then_inc(S["e_oTs"], 1)

            def out_add(b, u, it):
                dve.wait_ge(S["e_y"], b + 1)
                dve.wait_ge(S["xo"], b + 1)
                v.tensor_tensor(at(x, b), bank[7][0:T, D:2 * D], at(x, b), ALU.add).then_inc(S["x3"], 1)
                dve.wait_ge(S["x3"], b + 1)
                moments(3, b)

            hops = [0]

            def choose(b, u, it):
                hops[0] = gate_choose(1, b, u)

            before_steps = {3: out_tokens, 5: out_turn, 7: out_add,
                            10: lambda b, u, it: gate_norm(1, b, u, it),
                            12: lambda b, u, it: gate_turn(1, b, u, bank[7][:, 0:DC * T]),
                            14: choose, 17: lambda b, u, it: gate_place(1, b, u, hops[0])}
            after_steps = {1: lambda b, u: moments(2, b), 4: query_norm, 6: query_turn, 9: query_scale}

            dve.wait_ge(S["x2_in0"], 16)
            for i in sorted(after_steps):
                after_steps[i](0, 0)
            dve.wait_ge(S["x2_in1"], 16)
            for b, u, it, late, early in batches(dve):
                for i in range(NH + 2):
                    if i < NH:
                        dve.wait_ge(S["h_s"], b * NH + i + 1)
                        v.tensor_reduce(nmax[u][:, i:i + 1], bank[i % 3][0:T, 0:KL], axis=AX.X, op=ALU.max,
                                        negate=True).then_inc(S["h_max"], 1)
                    if i >= 2 and i % 2 == 1:
                        dve.wait_ge(S["h_pT"], b * NH + i - 1)
                        v.tensor_copy(probsT[(i - 2) % 4][:], bank[5][0:KP, 0:KT * T]).then_inc(S["h_pTd"], 1)
                    if late and i in before_steps:
                        before_steps[i](b - 1, *before(u, it))
                    if early and i in after_steps:
                        after_steps[i](b + 1, 1 - u)
            for i in sorted(before_steps):
                before_steps[i](B - 1, 1, B // 2 - 1)
            experts(1)


_INS = ["x", "ctx_1024", "_lenS2", "L0_xattn_W", "L0_xattn_b", "L0_ffn_switch_w", "L0_ffn_switch_b", "L0_ffn_w1",
        "L0_ffn_b1", "L0_ffn_w2", "L0_ffn_b2", "L1_xattn_Wq", "L1_xattn_bq", "L1_xattn_Wk", "L1_xattn_bk",
        "L1_xattn_Wv", "L1_xattn_bv", "L1_xattn_Wo", "L1_xattn_bo", "L1_ffn_gate_w", "L1_ffn_gate_b", "L1_ffn_w1",
        "L1_ffn_b1", "L1_ffn_w2", "L1_ffn_b2"]


def kernel(**inputs):
    import numpy as np
    import concourse.bacc as bacc
    from concourse import mybir as mb
    from concourse.bass_utils import run_bass_kernel_spmd

    nc = bacc.Bacc("TRN2", target_bir_lowering=False, num_devices=1)
    arrays, A = {}, {}
    for name in _INS:
        a = np.ascontiguousarray(inputs[name])
        arrays[f"in_{name}"] = a
        A[name] = nc.dram_tensor(f"in_{name}", a.shape, mb.dt.from_np(a.dtype), kind="ExternalInput").ap()
    out = nc.dram_tensor("out_tokens", A["x"].shape, mb.dt.float32, kind="ExternalOutput").ap()
    build_program(nc, A, out)
    r = run_bass_kernel_spmd(nc, [arrays], core_ids=[0])
    return r.results[0]["out_tokens"]
```

```python
import concourse.bass as bass
from concourse import mybir
from contextlib import ExitStack


def build_program(nc, A, out):
    f32 = mybir.dt.float32
    bf16 = mybir.dt.bfloat16
    i32 = mybir.dt.int32
    u32 = mybir.dt.uint32
    ALU = mybir.AluOpType
    ACT = mybir.ActivationFunctionType
    AX = mybir.AxisListType

    B, T, D = A["x"].shape
    KL = A["ctx_1024"].shape[1]
    NE = A["L0_ffn_w1"].shape[0]
    FF = A["L0_ffn_w1"].shape[2]
    P = 128
    DC = D // P
    FC = FF // P
    KT = 3
    KP = KL // KT
    NH, HD = 16, D // 16
    HPC = P // HD
    HW = 32
    CAP = int(1.25 * B * T / NE)
    HC = CAP // 2
    N_OVER = 6
    STRIDE = 8 * CAP
    RW = D + 4
    BIG = -16.0e13
    EPS = 1e-5
    SAVES = 3 * 16
    HOPS = (8, 11)

    x_rows = A["x"].rearrange("b t d -> t b d")
    ctx_rows = A["ctx_1024"].rearrange("b (j p) d -> p b j d", p=KP)

    tok_rows = [nc.dram_tensor("slot_tokens_0", (NE * STRIDE, RW), f32).ap(),
                nc.dram_tensor("slot_tokens_1", (NE * CAP + 2 * B * T, RW), f32).ap()]
    k_parts = nc.dram_tensor("key_parts", (B, P, 8, DC, KL), bf16).ap()
    q_parts = nc.dram_tensor("query_parts", (B, P, 8, DC, T), bf16).ap()
    acc = [nc.dram_tensor("stream_0", (B * T + CAP, D), f32).ap(), nc.dram_tensor("stream_1", (B * T + CAP, D), f32).ap()]

    stack = ExitStack()
    with stack:
        def sb(name, shape, dt=f32):
            return stack.enter_context(nc.sbuf_tensor(name, list(shape), dt))

        def sem(name):
            return stack.enter_context(nc.semaphore(name))

        bank = [stack.enter_context(nc.psum_tensor(f"bank{i}", [P, 512], f32)) for i in range(8)]

        ident = sb("ident", [P, P])
        tri = sb("tri", [T, T], bf16)
        ones = sb("ones", [T, T], bf16)
        kpos = sb("kpos", [T, KL])
        qpos = sb("qpos", [T, 1])
        qpos_i = sb("qpos_i", [T, 1], i32)
        eidx = sb("eidx", [T, NE])
        eidx_i = sb("eidx_i", [T, NE], i32)
        ident16 = sb("ident16", [T, T], bf16)
        pick_f = sb("pick_f", [P, HPC])
        pick = sb("pick_max", [P, HPC, KP], bf16)
        tokid = sb("tokid", [T, B])
        tokid_i = sb("tokid_i", [T, B], i32)
        neg_half = sb("neg_half", [T, 1])
        pad_i = sb("pad_i", [HC, 2], i32)
        empty = sb("empty_rows", [HC, 2, RW])
        raw = sb("raw_weights", [P, 5, DC, D])
        wT = sb("weights_T", [P, 5, DC, D])
        bias_rows = sb("bias_rows", [P, P])
        bias_rows2 = sb("bias_rows2", [4 * NE + 4, P])
        biasT = sb("biasT", [P, P + 4 * NE + 4])
        b_attn = sb("b_attn", [T, 2, D])
        bv = sb("bv", [KP, D])
        gate_w = sb("gate_w", [P, 2, DC, NE])
        gate_b = sb("gate_b", [T, 2, NE])
        lens_i = sb("lens_i", [T, B], i32)
        lens = sb("lens", [T, B])
        qflag = sb("qflag", [T, B])
        x = sb("x_tokens", [T, B, D])
        xrow = [[sb(f"xrow{c}{u}", [T, RW]) for u in range(2)] for c in range(2)]
        ctx = [sb(f"ctx{u}", [KP, KT, D]) for u in range(2)]
        ctxT = [sb(f"ctxT{u}", [P, DC, KL]) for u in range(2)]
        xa = [sb(f"xa{u}", [T, D]) for u in range(2)]
        rowmax = [sb(f"rowmax{u}", [T, 1]) for u in range(2)]
        xgT = sb("xgT", [P, DC, T])
        esinv = sb("esinv", [T, 1])
        xT = [sb(f"xT{u}", [P, DC, T]) for u in range(2)]
        kf = [sb(f"keys_f32_{u}", [P, DC, KL]) for u in range(2)]
        kpairs = [sb(f"key_parts{u}", [P, 3 * DC * max(KL, B // 2 * T) // 2]) for u in range(2)]
        kparts = [kpairs[u][:, 0:3 * DC * KL // 2].bitcast(bf16).rearrange("p (r c t) -> p r c t", r=3, c=DC) for u in range(2)]
        qf = [kf[u][:, :, 0:T] for u in range(2)]
        qparts = [kpairs[u][:, 0:3 * DC * B // 2 * T // 2].bitcast(bf16).rearrange("p (i r n) -> p i r n", i=B // 2, r=3)
                  for u in range(2)]
        kpos_i = kf[0][0:T, 0, :].bitcast(i32)
        kst = [[sb(f"key_stack{u}{g}", [P, HPC, KL], bf16) for g in range(DC)] for u in range(2)]
        qst = [[sb(f"query_stack{u}{g}", [P, HPC, T], bf16) for g in range(DC)] for u in range(2)]
        vals = sb("vals", [KP, B * KT, D])
        vpad = [sb(f"vpad{u}", [KP, KT, NH, HW]) for u in range(2)]
        scores = sb("scores", [T, KL])
        kmask = sb("kmask", [T, KL])
        probs = [sb(f"probs{i}", [T, KL]) for i in range(2)]
        probsT = [sb(f"probsT{i}", [KP, KT * T]) for i in range(4)]
        oT = sb("oT", [P, DC, T])
        outT = sb("outT", [P, 4, T])
        oa = sb("out_heads", [T, D])
        hmax = [sb(f"head_max{g}", [T, HPC]) for g in range(DC)]
        mparts = [sb(f"max_parts{g}", [T, P], bf16) for g in range(DC)]
        mT = [sb(f"max_T{g}", [P, T], bf16) for g in range(DC)]
        rinv = sb("rinv", [T, NH])
        esum = [sb(f"esum{u}", [T, 1]) for u in range(2)]
        lstat = [sb(f"ln_stats{k}", [T, 6]) for k in range(4)]
        lmv = [sb(f"ln_mean_var{k}", [T, 2]) for k in range(4)]
        lvar = [sb(f"ln_var_eps{k}", [T, 1]) for k in range(4)]
        rstd = [sb(f"ln_rstd{k}", [T, 1]) for k in range(4)]
        w1 = [sb(f"w1_{u}", [P, DC, FF]) for u in range(2)]
        w2 = [sb(f"w2_{u}", [P, FC, D]) for u in range(2)]
        xtok = [sb(f"xtok{u}", [HC, 2, RW]) for u in range(2)]
        sid = [sb(f"slot_ids{u}", [HC, 2], u32) for u in range(2)]
        xsT = [sb(f"xsT{u}", [P, DC, CAP]) for u in range(2)]
        hT = kpairs[0][:, 0:FC * CAP].rearrange("p (f t) -> p f t", f=FC)
        yT = sb("yT", [P, DC, CAP])
        ytok = [kf[u][0:HC].rearrange("p c t -> p (c t)")[:, 0:2 * D].rearrange("p (g d) -> p g d", g=2) for u in range(2)]
        logit = sb("logit", [T, NE])
        top8 = sb("top8", [T, 8])
        topn = sb("topn", [T, 1])
        topi = sb("topi", [T, 8], u32)
        topf = sb("topf", [T, 2])
        hot = sb("hot", [T, 2, NE])
        hot16 = sb("hot16", [T, NE], bf16)
        seen = [sb(f"seen{k}", [T, NE]) for k in range(2)]
        wexp = sb("wexp", [T, NE])
        wsum = sb("wsum", [T, 1])
        trash = sb("trash", [T, B, 2])
        seen16 = [sb(f"seen16_{k}", [T, NE], bf16) for k in range(2)]
        rank = sb("rank", [T, NE])
        rt = [sb(f"route_tmp{c}", [T, NE]) for c in range(2)]
        rs = sb("route_sum", [T, 2])
        ra = sb("route_a", [T, 2])
        rb = sb("route_b", [T, 2])
        keep = sb("route_keep", [T, 2])
        pos = [[sb(f"pos{c}{u}", [T, 1], i32) for u in range(2)] for c in range(2)]
        total = sb("total", [T, NE])
        ocum = sb("over_cum", [T, 3, NE])
        oat = sb("over_at", [T, N_OVER, NE])
        ofl = sb("over_table", [T, 4, NE])
        table = sb("over_table_i", [T, 4, NE], i32)

        S = {n: sem(n) for n in (
            "ident_made", "passed", "consts_made", "consts_step", "weights_in", "biases_in", "bcast_in", "first_in", "x_in0", "x_in1", "emptied0", "emptied1", "refilled", "refills_done",
            "bias_ps", "bias_sb", "w_ps", "w_sb", "chain", "empty_made", "vpad_made",
            "ctx_in0", "ctx_in1", "ctxT_ps", "ctxT_act", "ctxT_dve", "xT_ps", "xT_sb", "s_ps", "s_masked", "s_rowmax",
            "s_max", "s_exp", "kmask_set", "k_ps", "k_sb", "v_ps", "v_sb", "pT_ps", "pT_sb", "o_ps", "o_sb", "y_ps",
            "esum_inv", "xb", "x1", "vp", "h_s", "h_max", "h_sT", "h_exp", "h_av", "h_out", "m_step", "m_parts", "m_ps", "m_sb",
            "part_h", "part_r", "part_m", "part_l", "parts_saved0", "parts_saved1", 
            "stack_in00", "stack_in01", "stack_in10", "stack_in11", "pick_made",
            "h_outT", "h_rinv", "h_o", "e_oT", "e_oTs", "e_y", "x3", "q_xT", "q_xTs", "q_ps", "q_sb", "xo",
            "layer0_done", "out_done", "x2_in0", "x2_in1", "table_set")}
        LN = [{n: sem(f"ln{k}_{n}") for n in ("stats", "var", "eps", "rstd", "xn")} for k in range(2)] * 2
        R = [{n: sem(f"route{k}_{n}") for n in ("xT_ps", "xT_sb", "g_ps", "step", "best", "hot", "seen", "rank", "wexp",
                                                "row2", "row", "put0", "put1", "saved")} for k in range(2)]
        F = [{n: sem(f"ffn{k}_{n}") for n in ("w1_in0", "w1_in1", "w2_in0", "w2_in1", "x_in0", "x_in1", "xT_ps", "xT_sb",
                                              "up", "h", "down", "yT", "y_ps", "y_sb", "id", "added0", "added1")}
             for k in range(2)]

        block = stack.enter_context(nc.Block())

        def at(ap, i):
            if isinstance(i, int):
                return ap[:, i]
            sub = ap[:, bass.ds(i, 1)]
            names = " ".join("abc"[:len(sub.shape) - 2])
            return sub.rearrange(f"p i {names} -> p (i {names.split()[0]}) {' '.join(names.split()[1:])}")

        def batches(eng):
            yield 0, 0, 0, False, True
            with eng.Fori(0, B // 2 - 1) as it:
                yield it * 2 + 1, 1, it, True, True
                yield it * 2 + 2, 0, it + 1, True, True
            yield B - 1, 1, B // 2 - 1, True, False

        def pairs(eng):
            with eng.Fori(0, B // 2) as it:
                for u in range(2):
                    yield it * 2 + u, u, it

        names = ["L0_xattn_W", "L1_xattn_Wq", "L1_xattn_Wk", "L1_xattn_Wv", "L1_xattn_Wo"]
        W0, WQ, WK, WV, WO = range(5)
        w1_src = [A[f"L{k}_ffn_w1"].rearrange("e (c p) f -> p e c f", p=P) for k in range(2)]
        w2_src = [A[f"L{k}_ffn_w2"].rearrange("e (c p) d -> p e c d", p=P) for k in range(2)]
        slots = [t[0:n].rearrange("(e r) d -> e r d", e=NE)[:, 0:CAP].rearrange("e (p g) d -> p e (g d)", g=2)
                 for t, n in zip(tok_rows, (NE * STRIDE, NE * CAP))]

        AHEAD = 11
        MAX1, MAX0 = 7, NH + 1
        MAXB = (7, 3)
        GATE, RANK = 480, 488

        def nth(k, b):
            return k // 2 * B + b + 1

        def plain(eng):
            eng.sem_inc(S["passed"], 1)

        def before(u, it):
            return 1 - u, (it if u == 1 else it - 1)

        @block.sync
        def _(sp):
            def load_ctx(b, u):
                sp.dma_start(ctx[u][:], at(ctx_rows, b)).then_inc(S[f"ctx_in{u}"], 16)

            def load_first(k, e, u):
                sp.dma_start(w1[u][:], at(w1_src[k], e)).then_inc(F[k][f"w1_in{u}"], 16)

            def load_second(k, e, u):
                sp.dma_start(w2[u][:], at(w2_src[k], e)).then_inc(F[k][f"w2_in{u}"], 16)

            def load_expert(k, e, u):
                load_first(k, e, u)
                load_second(k, e, u)

            def store_stream(k, b):
                sp.dma_start(acc[k][bass.ds(b * T, T), :], at(x, b)).then_inc(R[k]["saved"], 16)

            def store_keys(b, u):
                sp.wait_ge(S["part_l"], b + 1)
                plain(sp)
                for r in (0, 3, 6):
                    n = min(3, 8 - r)
                    sp.dma_start(k_parts[bass.ds(b, 1), :, r:r + n].rearrange("b p r c t -> p (b r c t)"),
                                 kparts[u][:, 0:n].rearrange("p r c t -> p (r c t)")).then_inc(S[f"parts_saved{u}"], 16)

            def store_queries(b, u, it):
                sp.wait_ge(S["part_l"], B + b + 1)
                plain(sp)
                for r in (0, 3, 6):
                    n = min(3, 8 - r)
                    sp.dma_start(q_parts[bass.ds(b, 1), :, r:r + n].rearrange("b p r c t -> p (b r) (c t)"),
                                 at(qparts[u], it)[:, r // 3].unsqueeze(1).to_broadcast([P, n, DC * T])
                                 ).then_inc(S[f"parts_saved{u}"], 16)

            def load_stack(dst, src, b, u, g):
                sp.dma_start(dst[u][g][:], src[bass.ds(b, 1), :, :, g].rearrange("b (h d) r t -> (d r) (b h) t", d=HD)
                             ).then_inc(S[f"stack_in{u}{g}"], 16)

            load_ctx(0, 0)
            sp.dma_start(x[:, 0], x_rows[:, 0]).then_inc(S["x_in0"], 16)
            for n, name in enumerate(names):
                sp.dma_start(raw[:, n], A[name].rearrange("(c p) d -> p c d", p=P)).then_inc(S["weights_in"], 16)
            for k in range(2):
                sp.dma_start(bias_rows[64 * k:64 * k + 64, :],
                             A[f"L{k}_ffn_b1"].rearrange("e (f p) -> (e f) p", p=P)).then_inc(S["biases_in"], 16)
                sp.dma_start(bias_rows2[16 * k:16 * k + 16, :],
                             A[f"L{k}_ffn_b2"].rearrange("e (f p) -> (e f) p", p=P)).then_inc(S["biases_in"], 16)
            for n, name in enumerate(("L1_xattn_bq", "L1_xattn_bk")):
                sp.dma_start(bias_rows2[32 + 2 * n:34 + 2 * n, :],
                             A[name].rearrange("(f p) -> f p", p=P)).then_inc(S["biases_in"], 16)
            sp.dma_start(bv[:], A["L1_xattn_bv"].partition_broadcast(KP)).then_inc(S["bcast_in"], 16)
            sp.dma_start(b_attn[:, 1, :], A["L1_xattn_bo"].partition_broadcast(T)).then_inc(S["bcast_in"], 16)
            for k in range(2):
                sp.dma_start(gate_w[:, k], A[("L0_ffn_switch_w", "L1_ffn_gate_w")[k]].rearrange("(c p) e -> p c e", p=P)).then_inc(S["bcast_in"], 16)
                sp.dma_start(gate_b[:, k, :], A[("L0_ffn_switch_b", "L1_ffn_gate_b")[k]].partition_broadcast(T)).then_inc(S["bcast_in"], 16)
            load_ctx(1, 1)
            sp.dma_start(x[:, 1:], x_rows[:, 1:]).then_inc(S["x_in1"], 16)
            sp.wait_ge(S["empty_made"], 1)
            blank = empty[:].rearrange("p g d -> p (g d)")

            def empty_slots(k):
                for e in range(2, NE):
                    sp.dma_start(slots[k][:, e], blank).then_inc(S[f"emptied{k}"], 16)
                sp.dma_start(acc[k][B * T:].rearrange("(p g) d -> p g d", g=2), empty[:, :, 0:D]).then_inc(S[f"emptied{k}"], 16)

            empty_slots(0)
            for u in range(2):
                load_expert(0, u, u)
            with sp.Fori(0, B // 2 - 1) as it:
                for u in range(2):
                    sp.wait_ge(S["o_ps"], it * 2 + u + 1)
                    plain(sp)
                    load_ctx(it * 2 + u + 2, u)
                    sp.wait_ge(S["x1"], it * 2 + u + 1)
                    plain(sp)
                    store_stream(0, it * 2 + u)
                    store_keys(it * 2 + u, u)
            empty_slots(1)
            for b in (B - 2, B - 1):
                sp.wait_ge(S["x1"], b + 1)
                plain(sp)
                store_stream(0, b)
                if b < B - 1:
                    store_keys(b, b % 2)

            def load_tokens(k, s, u):
                sp.dma_start(xtok[u][:].rearrange("p g d -> p (g d)"), at(slots[k], s)).then_inc(F[k][f"x_in{u}"], 16)

            def load_slots(k):
                for u in range(2):
                    sp.wait_ge(R[k][f"put{u}"], 16 * (1 + (B // 2) * (1 + k)))
                for u in range(2):
                    load_tokens(k, u, u)

            def load_slots_rest(k):
                with sp.Fori(1, NE // 2) as it:
                    for u in range(2):
                        sp.wait_ge(F[k]["up"], it * 8 + 4 * (u - 1))
                        plain(sp)
                        load_first(k, it * 2 + u, u)
                        sp.wait_ge(F[k]["down"], it * 2 + (u - 1))
                        plain(sp)
                        load_second(k, it * 2 + u, u)
                        sp.wait_ge(F[k]["y_sb"], it * 2 + (u - 1))
                        plain(sp)
                        load_tokens(k, it * 2 + u, u)

            load_slots(0)
            store_keys(B - 1, 1)
            load_slots_rest(0)
            sp.wait_ge(S["table_set"], 1)
            n_over = sp.value_load(table[0:1, 3, 0:1], min_val=0, max_val=N_OVER)
            for j in range(N_OVER):
                u, s = j % 2, NE + j
                with sp.If(n_over > j):
                    e = sp.value_load(table[0:1, 0, j:j + 1], min_val=0, max_val=NE - 1)
                    row = sp.value_load(table[0:1, 1, j:j + 1], min_val=0, max_val=NE * STRIDE - CAP)
                    if j == 0:
                        sp.wait_ge(S["refills_done"], 1)
                    sp.wait_ge(F[0]["up"], 4 * (s - 1))
                    load_first(0, e, u)
                    sp.wait_ge(F[0]["down"], s - 1)
                    load_second(0, e, u)
                    sp.wait_ge(F[0]["y_sb"], s - 1)
                    sp.dma_start(xtok[u][:].rearrange("p g d -> p (g d)"),
                                 tok_rows[0][bass.ds(row, CAP), :].rearrange("(p g) d -> p (g d)", g=2)).then_inc(F[0][f"x_in{u}"], 16)
            for u in range(2):
                sp.wait_ge(S[f"parts_saved{u}"], SAVES * (B // 2) + 1)
            for u in range(2):
                for g in range(DC):
                    load_stack(kst, k_parts, u, u, g)
            for u in range(2):
                sp.wait_ge(F[0][f"added{u}"], 32 * (NE // 2))
            for j in range(N_OVER):
                with sp.If(n_over > j):
                    sp.wait_ge(F[0][f"added{j % 2}"], 32 * ((NE + j) // 2 + 1))
            for n, (a, b) in enumerate(((0, 1), (1, B))):
                sp.dma_start(x[:, a:b], acc[0][a * T:b * T, :].rearrange("(b t) d -> t b d", t=T)).then_inc(S[f"x2_in{n}"], 16)
            for b in range(2):
                store_queries(b, b, 0)
            for u in range(2):
                sp.wait_ge(S[f"parts_saved{u}"], SAVES * (B // 2 + 1) + 1)
                for g in range(DC):
                    load_stack(qst, q_parts, u, u, g)
            with sp.Fori(1, B // 2) as it:
                for u in range(2):
                    store_queries(it * 2 + u, u, it)
            for u in range(2):
                sp.wait_ge(S[f"parts_saved{u}"], SAVES * B + 1)
            sp.wait_ge(S["layer0_done"], 1)
            for u in range(2):
                load_expert(1, u, u)
            with sp.Fori(0, B // 2 - 1) as it:
                for u in range(2):
                    b = it * 2 + u
                    for g in range(DC):
                        sp.wait_ge(S["h_sT"], b * NH + (g + 1) * HPC)
                        plain(sp)
                        load_stack(kst, k_parts, b + 2, u, g)
                        load_stack(qst, q_parts, b + 2, u, g)
                    sp.wait_ge(S["x3"], b + 1)
                    plain(sp)
                    store_stream(1, b)
            for b in (B - 2, B - 1):
                sp.wait_ge(S["x3"], b + 1)
                plain(sp)
                store_stream(1, b)
            load_slots(1)
            load_slots_rest(1)
            for u in range(2):
                sp.wait_ge(F[1][f"added{u}"], 32 * (NE // 2))
            sp.dma_start(out.rearrange("b t d -> (b t) d"), acc[1][0:B * T, :]).then_inc(S["out_done"], 16)
            sp.wait_ge(S["out_done"], 16)

        @block.gpsimd
        def _(pool):
            n = [0]

            def step(ins):
                n[0] += 1
                ins.then_inc(S["consts_step"], 1)
                pool.wait_ge(S["consts_step"], n[0])

            step(pool.memset(ident[:], 0.0))
            pool.affine_select(out=ident[:], in_=ident[:], compare_op=ALU.not_equal, fill=1.0, base=0,
                               pattern=[[-1, P]], channel_multiplier=1).then_inc(S["ident_made"], 1)
            pool.memset(neg_half[:], -0.5)
            pool.iota(kpos_i, pattern=[[1, KL]], base=0, channel_multiplier=0)
            pool.iota(qpos_i[:], pattern=[[0, 1]], base=0, channel_multiplier=1)
            pool.iota(eidx_i[:], pattern=[[1, NE]], base=0, channel_multiplier=0)
            pool.iota(pad_i[:], pattern=[[1, 2]], base=B * T, channel_multiplier=2)
            pool.iota(tokid_i[:], pattern=[[T, B]], base=0, channel_multiplier=1).then_inc(S["consts_made"], 1)

            def rsqrt(k, b):
                pool.wait_ge(LN[k]["var"], nth(k, b))
                plain(pool)
                pool.tensor_scalar(lvar[k][:], lmv[k][:, 1:2], EPS, None, ALU.add).then_inc(LN[k]["eps"], 1)
                pool.wait_ge(LN[k]["eps"], nth(k, b))
                pool.tensor_tensor(rstd[k][:], lvar[k][:], neg_half[:], ALU.pow).then_inc(LN[k]["rstd"], 1)

            def scatter(k, b, u):
                pool.wait_ge(R[k]["row"], b + 1)
                plain(pool)
                for c in range(k + 1):
                    pool.indirect_dma_start(
                        out=tok_rows[k], out_offset=bass.IndirectOffsetOnAxis(ap=pos[c][u][:].bitcast(u32), axis=0),
                        in_=xrow[c][u][:], in_offset=None).then_inc(R[k][f"put{u}"], 16)

            def add_results(k, s, u):
                pool.wait_ge(F[k]["y_sb"], s + 1)
                plain(pool)
                for g in range(2):
                    pool.indirect_dma_start(
                        out=acc[k], out_offset=bass.IndirectOffsetOnAxis(ap=sid[u][:, g:g + 1], axis=0),
                        in_=ytok[u][:, g, :], in_offset=None, compute_op=ALU.add).then_inc(F[k][f"added{u}"], 16)

            def added(k, u, it):
                pool.wait_ge(F[k][f"added{u}"], 32 * (it + 1))

            rsqrt(0, 0)
            pool.memset(ones[:], 1.0)
            step(pool.memset(pick_f[:], 0.0))
            for part in range(3):
                step(pool.affine_select(out=pick_f[:], in_=pick_f[:], compare_op=ALU.not_equal, fill=-1.0,
                                        base=-HPC * part, pattern=[[-1, HPC]], channel_multiplier=1))
            pool.affine_select(out=tri[:], in_=ones[:], compare_op=ALU.is_ge, fill=0.0, base=0,
                               pattern=[[1, T]], channel_multiplier=-1).then_inc(S["consts_made"], 1)
            pool.wait_ge(S["empty_made"], 1)
            for k in range(2):
                for u in range(2):
                    pool.dma_start(slots[k][:, u], empty[:].rearrange("p g d -> p (g d)")).then_inc(R[k][f"put{u}"], 16)
            for u in range(2):
                step(pool.memset(vpad[u][:], 0.0))
                last = pool.memset(vpad[u][:, :, :, HD:HD + 1], 1.0)
            last.then_inc(S["vpad_made"], 1)
            for k in range(2):
                for u in range(2):
                    pool.wait_ge(R[k][f"put{u}"], 16)
            pool.wait_ge(S["emptied0"], 16 * (NE - 1))
            for b, u, it, late, early in batches(pool):
                if late:
                    rsqrt(1, b - 1)
                if early:
                    rsqrt(0, b + 1)
                if late:
                    scatter(0, b - 1, 1 - u)
            rsqrt(1, B - 1)
            scatter(0, B - 1, 1)
            pool.wait_ge(R[0]["saved"], 16 * B)
            pool.wait_ge(S["table_set"], 1)
            n_over = pool.value_load(table[0:1, 3, 0:1], min_val=0, max_val=N_OVER)
            with pool.If(n_over > 0):
                for j in range(N_OVER):
                    with pool.If(n_over > j):
                        row = pool.value_load(table[0:1, 2, j:j + 1], min_val=0, max_val=NE * STRIDE - CAP)
                        pool.dma_start(tok_rows[0][bass.ds(row, CAP), :].rearrange("(p g) d -> p (g d)", g=2),
                                       empty[:].rearrange("p g d -> p (g d)")).then_inc(S["refilled"], 16)
                        pool.wait_ge(S["refilled"], 16 * (j + 1))
                pool.sem_inc(S["refills_done"], 1)
            for s, u, it in pairs(pool):
                add_results(0, s, u)
                added(0, u, it)
            for j in range(N_OVER):
                with pool.If(n_over > j):
                    add_results(0, NE + j, j % 2)
                    added(0, j % 2, (NE + j) // 2)

            def max_parts(b, g):
                def hop(ins, n):
                    ins.then_inc(S["m_step"], 1)
                    pool.wait_ge(S["m_step"], (b * DC + g) * 4 + n)
                    plain(pool)

                part = [mparts[g][:, r * HPC:(r + 1) * HPC] for r in range(3)]
                pool.wait_ge(S["h_max"], b * NH + (g + 1) * HPC)
                plain(pool)
                hop(pool.tensor_copy(part[0], hmax[g][:]), 1)
                hop(pool.tensor_tensor(hmax[g][:], hmax[g][:], part[0], ALU.subtract), 2)
                hop(pool.tensor_copy(part[1], hmax[g][:]), 3)
                hop(pool.tensor_tensor(hmax[g][:], hmax[g][:], part[1], ALU.subtract), 4)
                pool.tensor_copy(part[2], hmax[g][:]).then_inc(S["m_parts"], 1)

            for b, u, it in pairs(pool):
                rsqrt(2, b)
            pool.wait_ge(LN[2]["xn"], nth(2, B - 1))
            for b in range(2):
                pool.tensor_tensor(x[:, b * (B // 2):(b + 1) * (B // 2)], x[:, b * (B // 2):(b + 1) * (B // 2)],
                                   b_attn[:, 1, :].unsqueeze(1).to_broadcast([T, B // 2, D]), ALU.add).then_inc(S["xo"], B // 2)
            pool.wait_ge(S["emptied1"], 16 * (NE - 1))
            max_parts(0, 0)
            for b, u, it, late, early in batches(pool):
                max_parts(b, 1)
                if late:
                    rsqrt(3, b - 1)
                if early:
                    max_parts(b + 1, 0)
                if late:
                    scatter(1, b - 1, 1 - u)
            rsqrt(3, B - 1)
            scatter(1, B - 1, 1)
            pool.wait_ge(R[1]["saved"], 16 * B)
            for s, u, it in pairs(pool):
                add_results(1, s, u)
                added(1, u, it)

        @block.tensor
        def _(pe):
            mm, tr = nc.tensor.matmul, nc.tensor.transpose

            def turn(bank_out, src):
                for c in range(DC):
                    last = tr(bank_out[:, c * T:(c + 1) * T], src[:, c * P:(c + 1) * P], ident[0:T, 0:T])
                return last

            def keep_clock(n):
                for _ in range(n):
                    mm(bank[7][0:T, 0:4 * T].rearrange("p (k t) -> p k t", t=T), ones[:],
                       tri[:].unsqueeze(1).to_broadcast([T, 4, T]), start=True, stop=True)

            pe.wait_ge(S["ident_made"], 1)

            def gate_turn(k, b, u, dst):
                pe.wait_ge(LN[1 + 2 * k]["xn"], nth(1 + 2 * k, b))
                turn(dst, xrow[0][u]).then_inc(R[k]["xT_ps"], 1)

            def gate_logits(k, b):
                pe.wait_ge(R[k]["xT_sb"], b + 1)
                for c in range(DC):
                    last = mm(bank[3][0:T, GATE:GATE + NE], xgT[:, c, :], gate_w[:, k, c, :], start=(c == 0), stop=(c == 1))
                last.then_inc(R[k]["g_ps"], 1)

            def gate_ranks(k, b):
                pe.wait_ge(R[k]["hot"], b + 1)
                mm(bank[3][0:T, RANK:RANK + NE], tri[:], hot16[:], start=True, stop=False)
                mm(bank[3][0:T, RANK:RANK + NE], ones[:], seen16[k][:], start=False, stop=True).then_inc(R[k]["rank"], 1)

            def weights():
                pe.wait_ge(S["consts_made"], 2)
                pe.wait_ge(S["weights_in"], 16 * 5)
                for n in range(5):
                    if n >= 2:
                        pe.wait_ge(S["w_sb"], n - 1)
                    for c in range(DC):
                        for o in range(DC):
                            last = tr(bank[6 + n % 2][:, c * D + o * P:c * D + (o + 1) * P], raw[:, n, o, c * P:(c + 1) * P], ident[:])
                    last.then_inc(S["w_ps"], 1)
                pe.wait_ge(S["biases_in"], 16 * 6)
                pe.wait_ge(S["bcast_in"], 16 * 6)
                tr(bank[5][:, 0:P], bias_rows[:], ident[:])
                tr(bank[5][:, P:P + 36], bias_rows2[:], ident[0:36, 0:36]).then_inc(S["bias_ps"], 1)
                pe.wait_ge(S["w_sb"], 5)
                pe.wait_ge(S["bias_sb"], 1)

            def context_turn(b, u, it, c):
                pe.wait_ge(S[f"ctx_in{u}"], 16 * (it + 1))
                for j in range(KT):
                    last = tr(bank[c][:, j * KP:(j + 1) * KP], ctx[u][:, j, c * P:(c + 1) * P], ident[0:KP, 0:KP])
                last.then_inc(S["ctxT_ps"], 1)

            def tokens_turn(b, u):
                pe.wait_ge(LN[0]["xn"], b + 1)
                turn(bank[2], xa[u]).then_inc(S["xT_ps"], 1)

            for c in range(DC):
                context_turn(0, 0, 0, c)
            tokens_turn(0, 0)
            for b, u, it, late, early in batches(pe):
                nit = it + 1 if u else it
                pe.wait_ge(S["ctxT_act"], b + 1)
                pe.wait_ge(S["ctxT_dve"], b + 1)
                pe.wait_ge(S["xT_sb"], b + 1)
                for c in range(DC):
                    last = mm(bank[3][0:T, 0:KL], xT[u][:, c, :], ctxT[u][:, c, :], start=(c == 0), stop=(c == 1))
                last.then_inc(S["s_ps"], 1)
                if late:
                    pe.wait_ge(S["k_sb"], 2 * b)
                else:
                    weights()
                for o in range(DC):
                    for c in range(DC):
                        last = mm(bank[4 + o][:, 0:KL], wT[:, WK, c, o * P:(o + 1) * P], ctxT[u][:, c, :],
                                  start=(c == 0), stop=(c == 1))
                    last.then_inc(S["k_ps"], 1)
                    if late and o == 0:
                        gate_turn(0, b - 1, 1 - u, bank[2][:, D:2 * D])
                if late:
                    pe.wait_ge(S["s_masked"], b + 1)
                    gate_logits(0, b - 1)

                def values(j):
                    for c in range(DC):
                        last = mm(bank[6 + j // 2][0:KP, (j % 2) * D:(j % 2 + 1) * D], ctxT[u][:, c, j * KP:(j + 1) * KP],
                                  wT[:, WV, c, :], start=(c == 0), stop=(c == 1))
                    return last

                if late:
                    pe.wait_ge(S["v_sb"], 2 * b)
                values(0)
                pe.wait_ge(S["s_exp"], b + 1)
                for j in range(KT):
                    last = tr(bank[0][0:KP, j * T:(j + 1) * T], probs[u][:, j * KP:(j + 1) * KP], ident[0:T, 0:T])
                last.then_inc(S["pT_ps"], 1)
                values(1).then_inc(S["v_ps"], 1)
                if late:
                    pe.wait_ge(S["x1"], b)
                values(2).then_inc(S["v_ps"], 1)
                if late:
                    gate_ranks(0, b - 1)
                pe.wait_ge(S["pT_sb"], b + 1)
                for c in range(DC):
                    for j in range(KT):
                        last = mm(bank[1][:, c * T:(c + 1) * T], ctx[u][:, j, c * P:(c + 1) * P],
                                  probsT[0][:, j * T:(j + 1) * T], start=(j == 0), stop=(j == KT - 1))
                last.then_inc(S["o_ps"], 1)
                if early:
                    context_turn(b + 1, 1 - u, nit, 0)
                pe.wait_ge(S["o_sb"], b + 1)
                if early:
                    context_turn(b + 1, 1 - u, nit, 1)
                    tokens_turn(b + 1, 1 - u)
                pe.wait_ge(S["v_sb"], 2 * b + 2)
                for c in range(DC):
                    last = mm(bank[7][0:T, D:2 * D], oT[:, c, :], wT[:, W0, c, :], start=(c == 0), stop=(c == 1))
                last.then_inc(S["y_ps"], 1)
                if late:
                    pe.wait_ge(R[0]["seen"], b)
            pe.wait_ge(S["x1"], B)
            keep_clock(8)
            gate_turn(0, B - 1, 1, bank[2][:, D:2 * D])
            gate_logits(0, B - 1)
            keep_clock(6)
            gate_ranks(0, B - 1)
            pe.wait_ge(R[0]["seen"], B)
            mm(bank[3][0:T, RANK:RANK + NE], ones[:], seen16[0][:], start=True, stop=True).then_inc(R[0]["rank"], 1)
            keep_clock(20)

            def slot_tokens(k, s, u, it):
                pe.wait_ge(F[k][f"x_in{u}"], 16 * (it + 1))
                for c in range(DC):
                    for g in range(2):
                        last = tr(bank[0][:, c * CAP + g * HC:c * CAP + (g + 1) * HC], xtok[u][:, g, c * P:(c + 1) * P],
                                  ident[0:HC, 0:HC])
                last.then_inc(F[k]["xT_ps"], 1)

            def slot_expert(k, s, u, it):
                pe.wait_ge(F[k][f"w1_in{u}"], 16 * (it + 1))
                pe.wait_ge(F[k]["xT_sb"], s + 1)
                for q in range(FC // 2):
                    for r in range(2):
                        f = 2 * q + r
                        for c in range(DC):
                            last = mm(bank[1 + q][:, r * CAP:(r + 1) * CAP], w1[u][:, c, f * P:(f + 1) * P], xsT[u][:, c, :],
                                      start=(c == 0), stop=(c == 1))
                    last.then_inc(F[k]["up"], 1)
                pe.wait_ge(F[k][f"w2_in{u}"], 16 * (it + 1))
                for d in range(DC):
                    for f in range(FC):
                        if d == 0 and f % 2 == 0:
                            pe.wait_ge(F[k]["h"], s * 4 + f // 2 + 1)
                        last = mm(bank[5][:, d * CAP:(d + 1) * CAP], w2[u][:, f, d * P:(d + 1) * P], hT[:, f, :],
                                  start=(f == 0), stop=(f == FC - 1))
                last.then_inc(F[k]["down"], 1)

            def slot_results(k, s, u):
                pe.wait_ge(F[k]["yT"], s + 1)
                for g in range(2):
                    for c in range(DC):
                        last = tr(bank[6 + u][0:HC, g * D + c * P:g * D + (c + 1) * P], yT[:, c, g * HC:(g + 1) * HC], ident[:])
                last.then_inc(F[k]["y_ps"], 1)

            def experts(k):
                slot_tokens(k, 0, 0, 0)
                with pe.Fori(0, NE // 2 - 1) as it:
                    for u in range(2):
                        slot_expert(k, it * 2 + u, u, it)
                        slot_tokens(k, it * 2 + u + 1, 1 - u, it + u)
                        slot_results(k, it * 2 + u, u)
                slot_expert(k, NE - 2, 0, NE // 2 - 1)
                slot_tokens(k, NE - 1, 1, NE // 2 - 1)
                slot_results(k, NE - 2, 0)
                slot_expert(k, NE - 1, 1, NE // 2 - 1)
                slot_results(k, NE - 1, 1)

            experts(0)
            pe.wait_ge(S["table_set"], 1)
            n_over = pe.value_load(table[0:1, 3, 0:1], min_val=0, max_val=N_OVER)
            for j in range(N_OVER):
                with pe.If(n_over > j):
                    s = NE + j
                    slot_tokens(0, s, j % 2, s // 2)
                    slot_expert(0, s, j % 2, s // 2)
                    slot_results(0, s, j % 2)
            pe.drain().then_inc(S["layer0_done"], 1)
            pe.wait_ge(F[0]["y_sb"], NE)
            for j in range(1, N_OVER, 2):
                with pe.If(n_over > j):
                    pe.wait_ge(F[0]["y_sb"], NE + j + 1)
            keep_clock(40)

            def query_project(b, u):
                pe.wait_ge(S["q_xTs"], b + 1)
                for o in range(DC):
                    for c in range(DC):
                        last = mm(bank[2 + u][:, o * T:(o + 1) * T], wT[:, WQ, c, o * P:(o + 1) * P], xT[u][:, c, :],
                                  start=(c == 0), stop=(c == 1))
                last.then_inc(S["q_ps"], 1)

            for b, u, it, late, early in batches(pe):
                if late:
                    query_project(b - 1, 1 - u)
                pe.wait_ge(LN[2]["xn"], nth(2, b))
                turn(bank[u], xa[u]).then_inc(S["q_xT"], 1)
                keep_clock(3)
            query_project(B - 1, 1)

            def head_scores(b, u, it, h):
                g, j = h // HPC, h % HPC
                if j == 0:
                    pe.wait_ge(S[f"stack_in{u}{g}"], 16 * 2 * (it + 1))
                if not (isinstance(b, int) and b == 0 and h < 3):
                    pe.wait_ge(S["h_max"], b * NH + (h - 2 if h > 2 else (0, -2, -1)[h]))
                mm(bank[h % 3][0:T, 0:KL], qst[u][g][:, j, :], kst[u][g][:, j, :], start=True, stop=True).then_inc(S["h_s"], 1)

            def maxes_turn(b, g):
                pe.wait_ge(S["m_parts"], DC * b + g + 1)
                mm(bank[MAXB[g]][:, 0:T], mparts[g][:], ident16[:], start=True, stop=True).then_inc(S["m_ps"], 1)

            def head_scoresT(b, u, h):
                g, j = h // HPC, h % HPC
                if j == 0:
                    pe.wait_ge(S["m_sb"], DC * b + g + 1)
                if not (isinstance(b, int) and b == 0 and h < 2):
                    pe.wait_ge(S["h_exp"], b * NH + h - 1)
                dst = bank[4 + h % 2][0:KP, 0:KT * T]
                mm(dst.rearrange("p (k t) -> p k t", t=T), pick[:, j, :], mT[g][:].unsqueeze(1).to_broadcast([P, KT, T]),
                   start=True, stop=False)
                for k in range(KT):
                    last = mm(dst[:, k * T:(k + 1) * T], kst[u][g][:, j, k * KP:(k + 1) * KP], qst[u][g][:, j, :],
                              start=False, stop=(k == KT - 1))
                last.then_inc(S["h_sT"], 1)

            def head_product(b, u, h, late):
                if h == 0:
                    pe.wait_ge(S["vp"], KT * (b + 1))
                    if late:
                        pe.wait_ge(S["h_out"], b)
                pe.wait_ge(S["h_exp"], b * NH + h + 1)
                r = HW * (h % 4)
                for j in range(KT):
                    last = mm(bank[6][r:r + HW, (h // 4) * T:(h // 4 + 1) * T], vpad[u][:, j, h, :],
                              probsT[h % 4][:, j * T:(j + 1) * T], start=(j == 0), stop=(j == KT - 1))
                last.then_inc(S["h_av"], 1)

            def out_tokens(b, u):
                pe.wait_ge(S["h_out"], b + 1)
                for q in range(4):
                    last = tr(bank[7][0:T, q * P:(q + 1) * P], outT[:, q, :], ident[:])
                last.then_inc(S["h_outT"], 1)

            def out_turn(b, u):
                pe.wait_ge(S["h_o"], b + 1)
                turn(bank[7], oa).then_inc(S["e_oT"], 1)

            def out_project(b, u):
                pe.wait_ge(S["e_oTs"], b + 1)
                for c in range(DC):
                    last = mm(bank[7][0:T, D:2 * D], oT[:, c, :], wT[:, WO, c, :], start=(c == 0), stop=(c == 1))
                last.then_inc(S["e_y"], 1)

            before_steps = {2: out_tokens, 4: out_turn, 5: out_project,
                            9: lambda b, u: gate_turn(1, b, u, bank[7][:, 0:D]),
                            10: lambda b, u: gate_logits(1, b), 15: lambda b, u: gate_ranks(1, b)}
            pe.wait_ge(S["pick_made"], 1)
            pe.wait_ge(S["q_sb"], B)
            for h in range(AHEAD):
                head_scores(0, 0, 0, h)
            maxes_turn(0, 0)
            for b, u, it, late, early in batches(pe):
                nit = it + 1 if u else it
                for i in range(NH + 2):
                    if i + AHEAD < NH:
                        head_scores(b, u, it, i + AHEAD)
                    if early and i >= NH + 2 - AHEAD:
                        head_scores(b + 1, 1 - u, nit, i - (NH + 2 - AHEAD))
                    if i == MAX1:
                        maxes_turn(b, 1)
                    if early and i == MAX0:
                        maxes_turn(b + 1, 0)
                    if i < NH:
                        head_scoresT(b, u, i)
                    if i >= 2:
                        head_product(b, u, i - 2, late)
                    if late and i in before_steps:
                        before_steps[i](b - 1, 1 - u)
            for i in sorted(before_steps):
                before_steps[i](B - 1, 1)
                if i == 5:
                    pe.wait_ge(S["x3"], B)
                    keep_clock(8)
                if i == 10:
                    keep_clock(6)
            keep_clock(34)
            experts(1)

        @block.scalar
        def _(act):
            def copy(dst, src):
                return nc.scalar.activation(dst, src, ACT.Copy)

            def col(i):
                return biasT[:, i:i + 1] if isinstance(i, int) else biasT[:, bass.ds(i, 1)]

            def chances(k, b, u):
                act.wait_ge(R[k]["best"], b + 1)
                src, n = ((logit, NE), (top8, 2))[k]
                nc.scalar.activation(wexp[:, 0:n], src[:, 0:n], ACT.Exp, bias=topn[:], accum_out=wsum[:]).then_inc(R[k]["wexp"], 1)

            act.dma_start(lens_i[:], A["_lenS2"].partition_broadcast(T)).then_inc(S["first_in"], 16)
            act.dma_start(b_attn[:, 0, :], A["L0_xattn_b"].partition_broadcast(T)).then_inc(S["first_in"], 16)

            def context_copy(b, u):
                act.wait_ge(S["ctxT_ps"], b * DC + 1)
                copy(ctxT[u][:, 0, :], bank[0][:, 0:KL]).then_inc(S["ctxT_act"], 1)

            context_copy(0, 0)
            for b, u, it, late, early in batches(act):
                if not late:
                    for n in range(5):
                        act.wait_ge(S["w_ps"], n + 1)
                        copy(wT[:, n].rearrange("p c d -> p (c d)"), bank[6 + n % 2][:]).then_inc(S["w_sb"], 1)
                    act.wait_ge(S["bias_ps"], 1)
                    copy(biasT[:], bank[5][:, 0:P + 36]).then_inc(S["bias_sb"], 1)
                    act.wait_ge(S["bias_sb"], 1)
                act.wait_ge(S["s_max"], b + 1)
                nc.scalar.activation(probs[u][:], scores[:], ACT.Exp, bias=rowmax[u][:], scale=1.0 / 16,
                                     accum_out=esum[u][:]).then_inc(S["s_exp"], 1)
                for o in range(DC):
                    act.wait_ge(S["k_ps"], b * 2 + o + 1)
                    nc.scalar.activation(kf[u][:, o, :], bank[4 + o][:, 0:KL], ACT.Identity,
                                         bias=biasT[:, P + 34 + o:P + 35 + o]).then_inc(S["k_sb"], 1)
                act.wait_ge(S["k_sb"], b * 2 + 2)
                if late:
                    act.wait_ge(S[f"parts_saved{u}"], it * SAVES + 1)
                copy(kparts[u][:, 0], kf[u][:]).then_inc(S["part_h"], 1)
                act.wait_ge(S["pT_ps"], b + 1)
                copy(probsT[0][:], bank[0][0:KP, 0:KT * T]).then_inc(S["pT_sb"], 1)
                if late:
                    chances(0, b - 1, 1 - u)
                act.wait_ge(S["o_ps"], b + 1)
                copy(oT[:].rearrange("p c t -> p (c t)"), bank[1][:, 0:DC * T]).then_inc(S["o_sb"], 1)
                if early:
                    context_copy(b + 1, 1 - u)
            chances(0, B - 1, 1)

            def slot(k, s, e):
                func = (ACT.Gelu_apprx_tanh, ACT.Relu)[k]
                for q in range(FC // 2):
                    act.wait_ge(F[k]["up"], s * 4 + q + 1)
                    for r in range(2):
                        f = 2 * q + r
                        last = nc.scalar.activation(hT[:, f, :], bank[1 + q][:, r * CAP:(r + 1) * CAP], func,
                                                    bias=col(64 * k + e * FC + f))
                    last.then_inc(F[k]["h"], 1)
                act.wait_ge(F[k]["down"], s + 1)
                for d in range(DC):
                    last = nc.scalar.activation(yT[:, d, :], bank[5][:, d * CAP:(d + 1) * CAP], ACT.Identity,
                                                bias=col(P + 16 * k + e * DC + d))
                last.then_inc(F[k]["yT"], 1)

            act.wait_ge(S["parts_saved0"], SAVES * (B // 2) + 1)
            for s, u, it in pairs(act):
                slot(0, s, s)
            act.wait_ge(S["table_set"], 1)
            n_over = act.value_load(table[0:1, 3, 0:1], min_val=0, max_val=N_OVER)
            for j in range(N_OVER):
                with act.If(n_over > j):
                    slot(0, NE + j, act.value_load(table[0:1, 0, j:j + 1], min_val=0, max_val=NE - 1))

            def query_bias(b, u, it):
                act.wait_ge(S["q_ps"], b + 1)
                act.wait_ge(S["part_l"], B + b - 1)
                for o in range(DC):
                    last = nc.scalar.activation(qf[u][:, o, :], bank[2 + u][:, o * T:(o + 1) * T], ACT.Identity,
                                                bias=biasT[:, P + 32 + o:P + 33 + o])
                last.then_inc(S["q_sb"], 1)
                act.wait_ge(S["q_sb"], b + 1)
                copy(at(qparts[u], it)[:, 0].rearrange("p (c t) -> p c t", t=T), qf[u]).then_inc(S["part_h"], 1)

            act.wait_ge(S["parts_saved1"], SAVES * (B // 2) + 1)
            for b, u, it, late, early in batches(act):
                if late:
                    query_bias(b - 1, *before(u, it))
                act.wait_ge(S["q_xT"], b + 1)
                copy(xT[u][:].rearrange("p c t -> p (c t)"), bank[u][:, 0:DC * T]).then_inc(S["q_xTs"], 1)
            query_bias(B - 1, 1, B // 2 - 1)

            def second_row(b, u):
                act.wait_ge(LN[3]["xn"], nth(3, b))
                copy(xrow[1][u][:, 0:D], xrow[0][u][:, 0:D]).then_inc(R[1]["row2"], 1)

            def maxes_turn(b, g):
                act.wait_ge(S["m_ps"], DC * b + g + 1)
                copy(mT[g][:], bank[MAXB[g]][:, 0:T]).then_inc(S["m_sb"], 1)

            def head_values(b, u, j):
                nc.scalar.activation(vpad[u][:, j, :, 0:HD], at(vals, b * KT + j).rearrange("p (h d) -> p h d", d=HD),
                                     ACT.Copy).then_inc(S["vp"], 1)

            def out_turn(b, u):
                act.wait_ge(S["e_oT"], b + 1)
                copy(oT[:].rearrange("p c t -> p (c t)"), bank[7][:, 0:DC * T]).then_inc(S["e_oTs"], 1)

            def gate_turn(b, u):
                act.wait_ge(R[1]["xT_ps"], b + 1)
                copy(xgT[:].rearrange("p c t -> p (c t)"), bank[7][:, 0:DC * T]).then_inc(R[1]["xT_sb"], 1)

            act.wait_ge(S["v_sb"], 2 * B)
            act.wait_ge(S["vpad_made"], 1)
            for j in range(KT):
                head_values(0, 0, j)
            before_steps = {4: (out_turn,), 9: (gate_turn, second_row), 12: (lambda b, u: chances(1, b, u),)}
            maxes_turn(0, 0)
            for b, u, it, late, early in batches(act):
                for i in range(NH + 2):
                    if i == MAX1:
                        maxes_turn(b, 1)
                    if early and i == MAX0:
                        maxes_turn(b + 1, 0)
                    if i < NH:
                        act.wait_ge(S["h_sT"], b * NH + i + 1)
                        nc.scalar.activation(probsT[i % 4][:], bank[4 + i % 2][0:KP, 0:KT * T], ACT.Exp,
                                             scale=1.0 / HD ** 0.5).then_inc(S["h_exp"], 1)
                    for step in before_steps.get(i, ()) if late else ():
                        step(b - 1, 1 - u)
                    if early and i in (5, 7, 10):
                        head_values(b + 1, 1 - u, (5, 7, 10).index(i))
                act.wait_ge(S["h_av"], b * NH + NH)
                copy(outT[:].rearrange("p q t -> p (q t)"), bank[6][:, 0:4 * T]).then_inc(S["h_out"], 1)
            for i in sorted(before_steps):
                for step in before_steps[i]:
                    step(B - 1, 1)
            for s, u, it in pairs(act):
                slot(1, s, s)

        @block.vector
        def _(dve):
            v = nc.vector
            done = [0]

            def link(ins):
                done[0] += 1
                ins.then_inc(S["chain"], 1)
                dve.wait_ge(S["chain"], done[0])

            def flat(ap):
                return ap.rearrange("p c t -> p (c t)")

            def moments(k, b):
                plain(dve)
                v.bn_stats(lstat[k][:], at(x, b)).then_inc(LN[k]["stats"], 1)
                dve.wait_ge(LN[k]["stats"], nth(k, b))
                plain(dve)
                v.bn_aggr(lmv[k][:], lstat[k][:]).then_inc(LN[k]["var"], 1)

            def normalise(k, b, dst):
                dve.wait_ge(LN[k]["rstd"], nth(k, b))
                v.tensor_scalar(dst, at(x, b), lmv[k][:, 0:1], rstd[k][:], ALU.subtract, ALU.mult).then_inc(LN[k]["xn"], 1)

            def gate_norm(k, b, u, it):
                dve.wait_ge(R[k][f"put{u}"], it * 16 * (k + 1) + 16)
                normalise(1 + 2 * k, b, xrow[0][u][:, 0:D])

            def gate_turn(k, b, u, src):
                dve.wait_ge(R[k]["xT_ps"], b + 1)
                v.tensor_copy(flat(xgT[:]), src).then_inc(R[k]["xT_sb"], 1)

            def hop(k, ins):
                ins.then_inc(R[k]["step"], 1)

            def hopped(k, b, n):
                dve.wait_ge(R[k]["step"], b * HOPS[k] + n)
                plain(dve)

            def choose_logits(k, b):
                dve.wait_ge(R[k]["g_ps"], b + 1)
                hop(k, v.tensor_tensor(logit[:], bank[3][0:T, GATE:GATE + NE], gate_b[:, k, :], ALU.add))

            def choose_best(k, b):
                hopped(k, b, 1)
                hop(k, v.max(top8[:], logit[:]))

            def choose_index(k, b):
                hopped(k, b, 2)
                v.tensor_scalar(topn[:], top8[:, 0:1], -1.0, None, ALU.mult).then_inc(R[k]["best"], 1)
                hop(k, v.max_index(topi[:], top8[:], logit[:]))

            def choose_number(k, b):
                hopped(k, b, 3)
                hop(k, v.tensor_copy(topf[:], topi[:, 0:2]))

            def choose_hot(k, b):
                hopped(k, b, 4)
                for c in range(k + 1):
                    last = v.tensor_scalar(hot[:, c], eidx[:], topf[:, c:c + 1], None, ALU.is_equal)
                hop(k, last)

            def choose_sum(k, b):
                hopped(k, b, 5)
                if k == 0:
                    v.tensor_copy(hot16[:], hot[:, 0]).then_inc(R[k]["hot"], 1)
                else:
                    v.tensor_tensor(hot16[:], hot[:, 0], hot[:, 1], ALU.add).then_inc(R[k]["hot"], 1)

            def place_number(k, b, u):
                for c in range(k + 1):
                    v.tensor_copy(xrow[c][u][:, D:D + 1], tokid[:, bass.ds(b, 1)])
                dve.wait_ge(R[k]["wexp"], b + 1)
                hop(k, v.reciprocal(rb[:, 0:1], wsum[:]))

            def place_weight(k, b, u):
                hopped(k, b, 6)
                if k == 0:
                    v.tensor_copy(xrow[0][u][:, D + 1:D + 2], rb[:, 0:1])
                else:
                    for c in range(2):
                        v.tensor_tensor(xrow[c][u][:, D + 1:D + 2], wexp[:, c:c + 1], rb[:, 0:1], ALU.mult)

            def place_ranks(k, b):
                dve.wait_ge(R[k]["rank"], b + 1)
                v.scalar_tensor_tensor(rt[0][:], hot[:, 0], 1.0, bank[3][0:T, RANK:RANK + NE], ALU.mult, ALU.mult,
                                       accum_out=rs[:, 0:1])
                if k == 1:
                    v.scalar_tensor_tensor(rt[1][:], hot[:, 1], 1.0, bank[3][0:T, RANK:RANK + NE], ALU.mult, ALU.mult,
                                           accum_out=rs[:, 1:2])
                dve.wait_ge(R[k]["hot"], b + 1)
                hop(k, v.tensor_tensor(seen[k][:], seen[k][:], hot16[:], ALU.add))

            def place_row(k, b):
                hopped(k, b, 7)
                v.tensor_copy(seen16[k][:], seen[k][:]).then_inc(R[k]["seen"], 1)
                if k == 0:
                    hop(k, v.scalar_tensor_tensor(ra[:, 0:1], topf[:, 0:1], float(STRIDE), rs[:, 0:1], ALU.mult, ALU.add))
                else:
                    v.tensor_scalar(keep[:], rs[:], float(CAP), None, ALU.is_le)
                    hop(k, v.scalar_tensor_tensor(ra[:], topf[:], float(CAP), rs[:], ALU.mult, ALU.add))

            def place_shift(b):
                hopped(1, b, 8)
                hop(1, v.tensor_tensor(ra[:], ra[:], at(trash, b), ALU.subtract))

            def place_keep(b):
                hopped(1, b, 9)
                hop(1, v.tensor_tensor(ra[:], ra[:], keep[:], ALU.mult))

            def place_back(b):
                hopped(1, b, 10)
                hop(1, v.tensor_tensor(ra[:], ra[:], at(trash, b), ALU.add))

            def place_done(k, b, u):
                hopped(k, b, HOPS[k])
                if k == 1:
                    dve.wait_ge(R[k]["row2"], b + 1)
                for c in range(k + 1):
                    last = v.tensor_scalar(pos[c][u][:], ra[:, c:c + 1], -1.0, None, ALU.add)
                last.then_inc(R[k]["row"], 1)

            dve.wait_ge(S["x_in0"], 16)
            moments(0, 0)
            for u in range(2):
                dve.sem_inc(S[f"parts_saved{u}"], 1)
            link(v.memset(empty[:], 0.0))
            dve.wait_ge(S["consts_made"], 1)
            v.tensor_copy(empty[:, :, D], pad_i[:]).then_inc(S["empty_made"], 1)
            link(v.tensor_copy(kpos[:], kpos_i))
            for a, i in ((qpos, qpos_i), (eidx, eidx_i), (tokid, tokid_i)):
                link(v.tensor_copy(a[:], i[:]))
            normalise(0, 0, xa[0][:])
            dve.wait_ge(S["first_in"], 16 * 2)
            link(v.tensor_copy(lens[:], lens_i[:]))
            link(v.tensor_tensor(qflag[:], qpos[:].to_broadcast([T, B]), lens[:], ALU.is_ge))

            def split_rest(n, whole, parts):
                dve.wait_ge(S["part_h"], n + 1)
                v.tensor_tensor(whole, whole, parts[:, 0], ALU.subtract).then_inc(S["part_r"], 1)

            def split_second(n, whole, parts):
                dve.wait_ge(S["part_r"], n + 1)
                v.tensor_copy(parts[:, 1], whole).then_inc(S["part_m"], 1)

            def split_third(n, whole, parts):
                dve.wait_ge(S["part_m"], n + 1)
                v.tensor_tensor(parts[:, 2], whole, parts[:, 1], ALU.subtract).then_inc(S["part_l"], 1)

            def split(n, whole, parts):
                for part in (split_rest, split_second, split_third):
                    part(n, whole, parts)

            def split_queries(b, u, it):
                split(B + b, qf[u], at(qparts[u], it).rearrange("p r (c t) -> p r c t", t=T))

            def tokens_norm(b, u):
                normalise(0, b, xa[u][:])

            def tokens_bias(b):
                dve.wait_ge(LN[0]["xn"], b + 1)
                v.tensor_tensor(at(x, b), at(x, b), b_attn[:, 0, :], ALU.add).then_inc(S["xb"], 1)

            def mask_keys(b):
                v.tensor_scalar(kmask[:], kpos[:], lens[:, bass.ds(b, 1)], BIG, ALU.is_ge, ALU.mult).then_inc(S["kmask_set"], 1)

            def context_copy(b, u):
                dve.wait_ge(S["ctxT_ps"], b * DC + 2)
                v.tensor_copy(ctxT[u][:, 1, :], bank[1][:, 0:KL]).then_inc(S["ctxT_dve"], 1)

            def tokens_copy(b, u):
                dve.wait_ge(S["xT_ps"], b + 1)
                v.tensor_copy(flat(xT[u][:]), bank[2][:, 0:DC * T]).then_inc(S["xT_sb"], 1)

            mask_keys(0)
            tokens_bias(0)
            context_copy(0, 0)
            tokens_copy(0, 0)
            for k in range(2):
                v.memset(seen[k][:], 0.0)
                v.memset(seen16[k][:], 0.0)
                for u in range(2):
                    v.memset(xrow[k][u][:, D:RW], 0.0)
            for c in range(2):
                v.tensor_scalar(trash[:, :, c], tokid[:], float(NE * CAP + c * B * T + 1), None, ALU.add)
            for g in range(DC):
                v.memset(mparts[g][:], 0.0)
            link(v.tensor_copy(ident16[:], ident[0:T, 0:T]))
            dve.wait_ge(S["x_in1"], 16)
            dve.wait_ge(S["bcast_in"], 16 * 6)
            for b, u, it, late, early in batches(dve):
                dve.wait_ge(S["s_ps"], b + 1)
                dve.wait_ge(S["kmask_set"], b + 1)
                v.scalar_tensor_tensor(scores[:], kmask[:], qflag[:, bass.ds(b, 1)], bank[3][0:T, 0:KL], ALU.mult,
                                       ALU.add).then_inc(S["s_masked"], 1)
                dve.wait_ge(S["s_masked"], b + 1)
                v.tensor_reduce(rowmax[u][:], scores[:], axis=AX.X, op=ALU.max, negate=True).then_inc(S["s_rowmax"], 1)
                dve.wait_ge(S["s_rowmax"], b + 1)
                v.tensor_scalar(rowmax[u][:], rowmax[u][:], 1.0 / 16, None, ALU.mult).then_inc(S["s_max"], 1)
                if late:
                    gate_norm(0, b - 1, *before(u, it))
                if early:
                    mask_keys(b + 1)
                if late:
                    gate_turn(0, b - 1, 1 - u, bank[2][:, D:D + DC * T])
                    split_rest(b - 1, kf[1 - u][:], kparts[1 - u])
                    choose_logits(0, b - 1)
                    split_second(b - 1, kf[1 - u][:], kparts[1 - u])
                    choose_best(0, b - 1)
                    split_third(b - 1, kf[1 - u][:], kparts[1 - u])
                    choose_index(0, b - 1)
                dve.wait_ge(S["s_exp"], b + 1)
                v.reciprocal(esinv[:], esum[u][:]).then_inc(S["esum_inv"], 1)
                if early:
                    moments(0, b + 1)
                if late:
                    choose_number(0, b - 1)
                    choose_hot(0, b - 1)
                dve.wait_ge(S["v_ps"], b * 2 + 1)
                v.tensor_tensor(vals[:, bass.ds(b * KT, 2), :], bank[6][0:KP, :].rearrange("p (j d) -> p j d", d=D),
                                bv[:].unsqueeze(1).to_broadcast([KP, 2, D]), ALU.add).then_inc(S["v_sb"], 1)
                if late:
                    choose_sum(0, b - 1)
                    place_number(0, b - 1, 1 - u)
                dve.wait_ge(S["v_ps"], b * 2 + 2)
                v.tensor_tensor(at(vals, b * KT + 2), bank[7][0:KP, 0:D], bv[:], ALU.add).then_inc(S["v_sb"], 1)
                if early:
                    tokens_norm(b + 1, 1 - u)
                if late:
                    place_weight(0, b - 1, 1 - u)
                    place_ranks(0, b - 1)
                if early:
                    tokens_bias(b + 1)
                if late:
                    place_row(0, b - 1)
                if early:
                    context_copy(b + 1, 1 - u)
                    tokens_copy(b + 1, 1 - u)
                if late:
                    place_done(0, b - 1, 1 - u)
                dve.wait_ge(S["y_ps"], b + 1)
                dve.wait_ge(S["xb"], b + 1)
                dve.wait_ge(S["esum_inv"], b + 1)
                v.scalar_tensor_tensor(at(x, b), bank[7][0:T, D:2 * D], esinv[:], at(x, b), ALU.mult, ALU.add).then_inc(S["x1"], 1)
                dve.wait_ge(S["x1"], b + 1)
                moments(1, b)
            gate_norm(0, B - 1, 1, B // 2 - 1)
            gate_turn(0, B - 1, 1, bank[2][:, D:D + DC * T])
            for step in (choose_logits, choose_best, choose_index, choose_number, choose_hot, choose_sum):
                step(0, B - 1)
            place_number(0, B - 1, 1)
            place_weight(0, B - 1, 1)
            place_ranks(0, B - 1)
            place_row(0, B - 1)
            place_done(0, B - 1, 1)
            split(B - 1, kf[1][:], kparts[1])

            def slot_tokens(k, s, u):
                dve.wait_ge(F[k]["xT_ps"], s + 1)
                v.tensor_copy(flat(xsT[u][:]), bank[0][:, 0:DC * CAP]).then_inc(F[k]["xT_sb"], 1)

            def slot_results(k, s, u, it):
                if not (isinstance(it, int) and it == 0):
                    dve.wait_ge(F[k][f"added{u}"], it * 32)
                v.tensor_copy(sid[u][:], xtok[u][:, :, D]).then_inc(F[k]["id"], 1)
                dve.wait_ge(F[k]["y_ps"], s + 1)
                for g in range(2):
                    last = v.tensor_scalar(ytok[u][:, g, :], bank[6 + u][0:HC, g * D:(g + 1) * D],
                                           xtok[u][:, g, D + 1:D + 2], None, ALU.mult)
                last.then_inc(F[k]["y_sb"], 1)

            def experts(k):
                for u in range(2):
                    slot_tokens(k, u + 1, 1 - u)
                    slot_results(k, u, u, 0)
                with dve.Fori(1, NE // 2 - 1) as it:
                    for u in range(2):
                        slot_tokens(k, it * 2 + u + 1, 1 - u)
                        slot_results(k, it * 2 + u, u, it)
                slot_tokens(k, NE - 1, 1)
                slot_results(k, NE - 2, 0, NE // 2 - 1)
                slot_results(k, NE - 1, 1, NE // 2 - 1)

            dve.wait_ge(R[0]["rank"], B + 1)
            link(v.tensor_copy(total[:], bank[3][0:T, RANK:RANK + NE]))
            slot_tokens(0, 0, 0)
            link(v.memset(ofl[:], 0.0))
            link(v.tensor_scalar(ocum[:, 0], total[:], float(CAP), None, ALU.is_gt))
            for j in range(2, N_OVER + 1):
                link(v.scalar_tensor_tensor(ocum[:, (j + 1) % 2], total[:], float(CAP * j), ocum[:, j % 2], ALU.is_gt, ALU.add))
            a, c = (N_OVER + 1) % 2, N_OVER % 2
            link(v.tensor_copy(ocum[:, 2], ocum[:, a]))
            for hop_by in (1, 2, 4):
                v.tensor_copy(ocum[:, c, 0:hop_by], ocum[:, a, 0:hop_by])
                link(v.tensor_tensor(ocum[:, c, hop_by:], ocum[:, a, hop_by:], ocum[:, a, 0:NE - hop_by], ALU.add))
                a, c = c, a
            link(v.tensor_tensor(oat[:], ocum[:, a].unsqueeze(1).to_broadcast([T, N_OVER, NE]),
                                 eidx[:, 0:N_OVER].unsqueeze(2).to_broadcast([T, N_OVER, NE]), ALU.is_le))
            link(v.tensor_reduce(ofl[:, 0, 0:N_OVER], oat[:], axis=AX.X, op=ALU.add))
            link(v.tensor_scalar(ofl[:, 0], ofl[:, 0], float(NE - 1), None, ALU.min))
            link(v.tensor_tensor(oat[:], oat[:], ocum[:, 2].unsqueeze(1).to_broadcast([T, N_OVER, NE]), ALU.mult))
            link(v.tensor_reduce(ofl[:, 1, 0:N_OVER], oat[:], axis=AX.X, op=ALU.add))
            link(v.tensor_tensor(ofl[:, 1], eidx[:], ofl[:, 1], ALU.subtract))
            link(v.tensor_scalar(ofl[:, 1], ofl[:, 1], 1.0, float(CAP), ALU.add, ALU.mult))
            link(v.scalar_tensor_tensor(ofl[:, 1], ofl[:, 0], float(STRIDE), ofl[:, 1], ALU.mult, ALU.add))
            link(v.tensor_scalar(ofl[:, 1], ofl[:, 1], float(NE * STRIDE - CAP), None, ALU.min))
            link(v.tensor_scalar(ofl[:, 2], total[:], float(CAP), None, ALU.max))
            link(v.scalar_tensor_tensor(total[:], eidx[:], float(STRIDE), ofl[:, 2], ALU.mult, ALU.add))
            link(v.tensor_tensor(oat[:], ofl[:, 0, 0:N_OVER].unsqueeze(2).to_broadcast([T, N_OVER, NE]),
                                 eidx[:].unsqueeze(1).to_broadcast([T, N_OVER, NE]), ALU.is_equal))
            link(v.tensor_tensor(oat[:], oat[:], total[:].unsqueeze(1).to_broadcast([T, N_OVER, NE]), ALU.mult))
            link(v.tensor_reduce(ofl[:, 2, 0:N_OVER], oat[:], axis=AX.X, op=ALU.add))
            link(v.tensor_copy(ofl[:, 3, 0:1], ocum[:, a, NE - 1:NE]))
            v.tensor_copy(table[:], ofl[:]).then_inc(S["table_set"], 1)

            dve.wait_ge(S["consts_made"], 2)
            v.tensor_copy(pick[:], pick_f[:].unsqueeze(2).to_broadcast([P, HPC, KP])).then_inc(S["pick_made"], 1)
            dve.wait_ge(S["part_l"], B)
            experts(0)
            n_over = dve.value_load(table[0:1, 3, 0:1], min_val=0, max_val=N_OVER)
            for j in range(N_OVER):
                with dve.If(n_over > j):
                    slot_tokens(0, NE + j, j % 2)
                    slot_results(0, NE + j, j % 2, (NE + j) // 2)

            dve.wait_ge(S["x2_in0"], 16)
            moments(2, 0)
            for b, u, it, late, early in batches(dve):
                normalise(2, b, xa[u][:])
                if early:
                    if not late:
                        dve.wait_ge(S["x2_in1"], 16)
                    dve.wait_ge(LN[2]["xn"], nth(2, b))
                    moments(2, b + 1)
                if late:
                    split_queries(b - 1, *before(u, it))
            split_queries(B - 1, 1, B // 2 - 1)

            def head_max(b, h):
                g, j = h // HPC, h % HPC
                if j == 0 and not (isinstance(b, int) and b == 0):
                    dve.wait_ge(S["m_parts"], b * DC + g - 1)
                dve.wait_ge(S["h_s"], b * NH + h + 1)
                v.tensor_reduce(hmax[g][:, j:j + 1], bank[h % 3][0:T, 0:KL], axis=AX.X, op=ALU.max).then_inc(S["h_max"], 1)
            def out_tokens(b, u, it):
                dve.wait_ge(S["h_outT"], b + 1)
                o = bank[7][0:T, :].rearrange("p (h w) -> p h w", w=HW)
                v.reciprocal(rinv[:].unsqueeze(2), o[:, :, HD:HD + 1]).then_inc(S["h_rinv"], 1)
                dve.wait_ge(S["h_rinv"], b + 1)
                v.tensor_tensor(oa[:].rearrange("p (h d) -> p h d", d=HD), o[:, :, 0:HD],
                                rinv[:].unsqueeze(2).to_broadcast([T, NH, HD]), ALU.mult).then_inc(S["h_o"], 1)

            def out_add(b, u, it):
                dve.wait_ge(S["e_y"], b + 1)
                dve.wait_ge(S["xo"], b + 1)
                v.tensor_tensor(at(x, b), bank[7][0:T, D:2 * D], at(x, b), ALU.add).then_inc(S["x3"], 1)
                dve.wait_ge(S["x3"], b + 1)
                moments(3, b)

            before_steps = {2: (out_tokens,), 5: (out_add,), 8: (lambda b, u, it: gate_norm(1, b, u, it),),
                            10: (lambda b, u, it: choose_logits(1, b), lambda b, u, it: choose_best(1, b)),
                            11: (lambda b, u, it: choose_index(1, b),),
                            12: (lambda b, u, it: choose_number(1, b), lambda b, u, it: choose_hot(1, b)),
                            13: (lambda b, u, it: choose_sum(1, b),),
                            14: (lambda b, u, it: place_number(1, b, u), lambda b, u, it: place_weight(1, b, u)),
                            15: (lambda b, u, it: place_ranks(1, b), lambda b, u, it: place_row(1, b)),
                            16: (lambda b, u, it: place_shift(b), lambda b, u, it: place_keep(b)),
                            17: (lambda b, u, it: place_back(b), lambda b, u, it: place_done(1, b, u))}

            for h in range(AHEAD):
                head_max(0, h)
            for b, u, it, late, early in batches(dve):
                for i in range(NH + 2):
                    if i + AHEAD < NH:
                        head_max(b, i + AHEAD)
                    if early and i >= NH + 2 - AHEAD:
                        head_max(b + 1, i - (NH + 2 - AHEAD))
                    for step in before_steps.get(i, ()) if late else ():
                        step(b - 1, *before(u, it))
            for i in sorted(before_steps):
                for step in before_steps[i]:
                    step(B - 1, 1, B // 2 - 1)
            slot_tokens(1, 0, 0)
            experts(1)


_INS = ["x", "ctx_1024", "_lenS2", "L0_xattn_W", "L0_xattn_b", "L0_ffn_switch_w", "L0_ffn_switch_b", "L0_ffn_w1",
        "L0_ffn_b1", "L0_ffn_w2", "L0_ffn_b2", "L1_xattn_Wq", "L1_xattn_bq", "L1_xattn_Wk", "L1_xattn_bk",
        "L1_xattn_Wv", "L1_xattn_bv", "L1_xattn_Wo", "L1_xattn_bo", "L1_ffn_gate_w", "L1_ffn_gate_b", "L1_ffn_w1",
        "L1_ffn_b1", "L1_ffn_w2", "L1_ffn_b2"]


def kernel(**inputs):
    import numpy as np
    import concourse.bacc as bacc
    from concourse import mybir as mb
    from concourse.bass_utils import run_bass_kernel_spmd

    nc = bacc.Bacc("TRN2", target_bir_lowering=False, num_devices=1)
    arrays, A = {}, {}
    for name in _INS:
        a = np.ascontiguousarray(inputs[name])
        arrays[f"in_{name}"] = a
        A[name] = nc.dram_tensor(f"in_{name}", a.shape, mb.dt.from_np(a.dtype), kind="ExternalInput").ap()
    out = nc.dram_tensor("out_tokens", A["x"].shape, mb.dt.float32, kind="ExternalOutput").ap()
    build_program(nc, A, out)
    r = run_bass_kernel_spmd(nc, [arrays], core_ids=[0])
    return r.results[0]["out_tokens"]
```
